# Optimizing a Trainium2 kernel written in Bass

```python
import numpy as np
import jax
import jax.numpy as jnp

def _softmax(x, axis=-1):
    return jax.nn.softmax(x, axis=axis)

def _gelu(x):
    return jax.nn.gelu(x, approximate=True)

def _silu(x):
    return jax.nn.silu(x)

def _sigmoid(x):
    return jax.nn.sigmoid(x)

def _layernorm(x, axis=-1, eps=1e-05):
    m = jnp.mean(x, axis=axis, keepdims=True)
    v = jnp.var(x, axis=axis, keepdims=True)
    return (x - m) / jnp.sqrt(v + eps)

def _scatter_add(tgt, idx, src, axis=0):
    return tgt.at[idx].add(src)

def _segment_sum(src, seg, n):
    return jax.ops.segment_sum(src, seg, n)
kernel_name = 'mk_prb_d1_jaxref_r8_148c53'

def setup_inputs(seed: int=0):
    np.random.seed(seed)
    _w = jnp.asarray

    def _L0_attn_setup():
        import jax, jax.numpy as jnp
        import numpy as np
        import math
        EMBED_DIM = 256
        NUM_HEADS = 16
        HEAD_DIM = EMBED_DIM // NUM_HEADS
        BATCH = 4
        SEQ = 256
        key = jax.random.key(seed)
        ks = jax.random.split(key, 5)
        scale_qkv = 1.0 / math.sqrt(EMBED_DIM)
        x = jax.random.normal(ks[0], (BATCH, SEQ, EMBED_DIM), dtype=jnp.float32)
        w_qkv = jax.random.normal(ks[1], (3 * EMBED_DIM, EMBED_DIM), dtype=jnp.float32) * scale_qkv
        b_qkv = jnp.zeros((3 * EMBED_DIM,), dtype=jnp.float32)
        w_o = jax.random.normal(ks[2], (EMBED_DIM, EMBED_DIM), dtype=jnp.float32) * scale_qkv
        b_o = jnp.zeros((EMBED_DIM,), dtype=jnp.float32)
        return {'x': x, 'w_qkv': w_qkv, 'b_qkv': b_qkv, 'w_o': w_o, 'b_o': b_o}
    _L0_attn_in = _L0_attn_setup()

    def _L0_ffn_setup():
        import jax, jax.numpy as jnp
        import numpy as np
        HIDDEN = 256
        FFN = 176
        N_EXPERTS = 64
        TOP_K = 6
        N_SHARED = 2
        SHARED_FFN = FFN * N_SHARED
        ROUTED_SCALING = 1.0
        EPS = 1e-20

        def _moe_forward(x, gate_w, w_gate_up, w_down, ws_gate_up, ws_down):
            T = x.shape[0]
            logits = jnp.einsum('th,eh->te', x.astype(jnp.float32), gate_w.astype(jnp.float32))
            scores = jax.nn.softmax(logits, axis=-1)
            topk_w, topk_ids = jax.lax.top_k(scores, TOP_K)
            topk_w = topk_w / (jnp.sum(topk_w, axis=-1, keepdims=True) + EPS)
            topk_w = topk_w * ROUTED_SCALING
            comb = jnp.zeros((T, N_EXPERTS), dtype=x.dtype)
            comb = comb.at[jnp.arange(T)[:, None], topk_ids].add(topk_w.astype(x.dtype))
            gu = jnp.einsum('th,efh->tef', x, w_gate_up)
            g, u = (gu[..., :FFN], gu[..., FFN:])
            act = jax.nn.silu(g) * u
            act = act * comb[:, :, None]
            routed = jnp.einsum('tef,ehf->th', act, w_down)
            sgu = jnp.einsum('th,fh->tf', x, ws_gate_up)
            sg, su = (sgu[..., :SHARED_FFN], sgu[..., SHARED_FFN:])
            shared = jnp.einsum('tf,hf->th', jax.nn.silu(sg) * su, ws_down)
            return routed + shared
        key = jax.random.key(seed)
        k0, k1, k2, k3, k4, k5 = jax.random.split(key, 6)
        hidden_states = jax.random.normal(k0, (1, 32, HIDDEN), dtype=jnp.float32)
        gate_w = jax.random.normal(k1, (N_EXPERTS, HIDDEN), dtype=jnp.float32) * 0.05
        w_gate_up = jax.random.normal(k2, (N_EXPERTS, 2 * FFN, HIDDEN), dtype=jnp.float32) * 0.02
        w_down = jax.random.normal(k3, (N_EXPERTS, HIDDEN, FFN), dtype=jnp.float32) * 0.02
        ws_gate_up = jax.random.normal(k4, (2 * SHARED_FFN, HIDDEN), dtype=jnp.float32) * 0.02
        ws_down = jax.random.normal(k5, (HIDDEN, SHARED_FFN), dtype=jnp.float32) * 0.02
        return {'hidden_states': hidden_states, 'gate_w': gate_w, 'w_gate_up': w_gate_up, 'w_down': w_down, 'ws_gate_up': ws_gate_up, 'ws_down': ws_down}
    _L0_ffn_in = _L0_ffn_setup()
    _d = {'L0_attn_x': _L0_attn_in['x'], 'L0_attn_w_qkv': _L0_attn_in['w_qkv'], 'L0_attn_b_qkv': _L0_attn_in['b_qkv'], 'L0_attn_w_o': _L0_attn_in['w_o'], 'L0_attn_b_o': _L0_attn_in['b_o'], 'L0_ffn_gate_w': _L0_ffn_in['gate_w'], 'L0_ffn_w_gate_up': _L0_ffn_in['w_gate_up'], 'L0_ffn_w_down': _L0_ffn_in['w_down'], 'L0_ffn_ws_gate_up': _L0_ffn_in['ws_gate_up'], 'L0_ffn_ws_down': _L0_ffn_in['ws_down']}
    _x0 = _d['L0_attn_x']
    _d['L0_attn_x'] = jax.random.normal(jax.random.fold_in(jax.random.key(seed), 1), (8, 256, 256), dtype=_x0.dtype)
    del _x0
    return _d

def reference(L0_attn_x, L0_attn_w_qkv, L0_attn_b_qkv, L0_attn_w_o, L0_attn_b_o, L0_ffn_gate_w, L0_ffn_w_gate_up, L0_ffn_w_down, L0_ffn_ws_gate_up, L0_ffn_ws_down):

    def _L0_attn_ref(x, w_qkv, b_qkv, w_o, b_o):
        import jax, jax.numpy as jnp
        import numpy as np
        import math
        EMBED_DIM = 256
        NUM_HEADS = 16
        HEAD_DIM = EMBED_DIM // NUM_HEADS
        BATCH = 4
        SEQ = 256
        B, S, D = x.shape
        qkv = jnp.einsum('bsd,ed->bse', x, w_qkv) + b_qkv
        qkv = qkv.reshape(B, S, 3, NUM_HEADS, HEAD_DIM)
        qkv = jnp.transpose(qkv, (2, 0, 3, 1, 4))
        q, k, v = (qkv[0], qkv[1], qkv[2])
        scores = jnp.einsum('bhqd,bhkd->bhqk', q, k) / math.sqrt(HEAD_DIM)
        probs = jax.nn.softmax(scores, axis=-1)
        out = jnp.einsum('bhqk,bhkd->bhqd', probs, v)
        out = jnp.transpose(out, (0, 2, 1, 3)).reshape(B, S, D)
        return jnp.einsum('bsd,ed->bse', out, w_o) + b_o

    def _L0_ffn_ref(hidden_states, gate_w, w_gate_up, w_down, ws_gate_up, ws_down):
        import jax, jax.numpy as jnp
        import numpy as np
        HIDDEN = 256
        FFN = 176
        N_EXPERTS = 64
        TOP_K = 6
        N_SHARED = 2
        SHARED_FFN = FFN * N_SHARED
        ROUTED_SCALING = 1.0
        EPS = 1e-20

        def _moe_forward(x, gate_w, w_gate_up, w_down, ws_gate_up, ws_down):
            T = x.shape[0]
            logits = jnp.einsum('th,eh->te', x.astype(jnp.float32), gate_w.astype(jnp.float32))
            scores = jax.nn.softmax(logits, axis=-1)
            topk_w, topk_ids = jax.lax.top_k(scores, TOP_K)
            topk_w = topk_w / (jnp.sum(topk_w, axis=-1, keepdims=True) + EPS)
            topk_w = topk_w * ROUTED_SCALING
            comb = jnp.zeros((T, N_EXPERTS), dtype=x.dtype)
            comb = comb.at[jnp.arange(T)[:, None], topk_ids].add(topk_w.astype(x.dtype))
            gu = jnp.einsum('th,efh->tef', x, w_gate_up)
            g, u = (gu[..., :FFN], gu[..., FFN:])
            act = jax.nn.silu(g) * u
            act = act * comb[:, :, None]
            routed = jnp.einsum('tef,ehf->th', act, w_down)
            sgu = jnp.einsum('th,fh->tf', x, ws_gate_up)
            sg, su = (sgu[..., :SHARED_FFN], sgu[..., SHARED_FFN:])
            shared = jnp.einsum('tf,hf->th', jax.nn.silu(sg) * su, ws_down)
            return routed + shared
        B, S, H = hidden_states.shape
        x = hidden_states.reshape(-1, H)
        out = _moe_forward(x, gate_w, w_gate_up, w_down, ws_gate_up, ws_down)
        return out.reshape(B, S, H)
    x = L0_attn_x
    xn = _layernorm(x, axis=-1)
    x = x + _L0_attn_ref(xn, L0_attn_w_qkv, L0_attn_b_qkv, L0_attn_w_o, L0_attn_b_o) + _L0_ffn_ref(xn, L0_ffn_gate_w, L0_ffn_w_gate_up, L0_ffn_w_down, L0_ffn_ws_gate_up, L0_ffn_ws_down)
    return x

_drawn_inputs = setup_inputs


def setup_inputs(seed=0):
    import zlib

    import numpy as np

    out = dict(_drawn_inputs(seed))
    spreads = {'L0_attn_b_qkv': (0.0, 0.607), 'L0_attn_b_o': (0.0, 0.608)}
    factors = {'L0_ffn_gate_w': 8.0,
     'L0_ffn_w_gate_up': 8.0,
     'L0_ffn_w_down': 8.0,
     'L0_ffn_ws_gate_up': 2.95,
     'L0_ffn_ws_down': 2.951}
    for name, (base, spread) in spreads.items():
        noise = np.random.default_rng([zlib.crc32(name.encode()), seed]).standard_normal(out[name].shape)
        drawn = base * np.exp(spread * noise) if base else spread * noise
        out[name] = jnp.asarray(drawn.astype(out[name].dtype))
    for name, factor in factors.items():
        out[name] = (out[name] * factor).astype(out[name].dtype)
    return out
```

```python
import concourse.bass as bass
from concourse import mybir


def block_kernel(nc, x, gate, wqkv, bqk, bvo, wo, wsgu, wsd, wgu, wd, out):
    f32, f32r, bf16, i32, u32 = (mybir.dt.float32, mybir.dt.float32r, mybir.dt.bfloat16,
                                 mybir.dt.int32, mybir.dt.uint32)
    ALU = mybir.AluOpType
    ACT = mybir.ActivationFunctionType
    AX = mybir.AxisListType

    P = 128
    TOK, D = x.shape
    TILES = TOK // P
    B = 8
    SEQ = TOK // B
    H, HD = 16, 16
    DC = D // P
    E = gate.shape[2]
    K = 6
    F = 176
    FH = F // 2
    FS = 2 * F
    SC = FS // FH
    SCALE = float(HD) ** -0.5
    LN_EPS, TOPK_EPS = 1e-5, 1e-20
    SLOTS = 2 * P
    REG = E * SLOTS
    OVT = (TOK * K) // P
    ROW = 272
    C_IDX, C_W, C_TOK = D, D + K, D + 2 * K
    GN, GO = 2 * F, DC * 2 * F
    WN = GO + 2 * D
    LEAD = 24
    HEADS = B * H

    xs_d = nc.dram_tensor("slot_rows", [REG + OVT * P, ROW], f32, kind="Internal").ap()
    qk_d = nc.dram_tensor("qk_parts", [B, 4, 2 * P, SEQ], f32, kind="Internal").ap()
    m_d = nc.dram_tensor("neg_max", [B, H, SEQ], f32, kind="Internal").ap()

    place = [(nc.sbuf_base + 63) // 64 * 64]

    def sb(name, shape, dt, at=None):
        n = 2 if dt == bf16 else 4
        for s in shape[1:]:
            n *= s
        where = place[0] if at is None else at[0]
        t = nc.alloc_sbuf_tensor_at(name, shape, dt, offset=where, align_bytes=32)
        if at is None:
            place[0] += (n + 31) // 32 * 32
            assert place[0] <= nc.sbuf_usable_end, (name, place[0])
        else:
            at[0] += (n + 31) // 32 * 32
            assert at[0] <= at[1], (name, at)
        return t

    def region(nbytes):
        start = place[0]
        place[0] += nbytes
        assert place[0] <= nc.sbuf_usable_end, place[0]
        return start, nbytes

    def within(r, skip=0):
        return [r[0] + skip, r[0] + r[1]]

    ident = sb("ident", [P, P], f32)
    before = sb("before", [P, P], bf16)
    ones = sb("ones", [P, P], bf16)
    iota_e = sb("iota_e", [P, E], f32)
    ecur = sb("ecur", [P, 4], f32)
    bq = sb("bq", [P, 4], f32)
    bv = sb("bv", [P, D], f32)
    mv = sb("mv", [P, TILES, 2], f32)
    st6 = sb("st6", [P, TILES, 6], f32)
    rstd = sb("rstd", [P, TILES, 3], f32)
    posi = sb("posi", [P, TILES * K], i32)
    nov_i = sb("nov_i", [P, 2], i32)
    mx = sb("mx", [P, 2, 2, H], f32)
    mTs = sb("mTs", [H, SEQ], f32r)
    rden = sb("rden", [P, 2, 2, 4], f32)
    wcol = sb("wcol", [P, 4, 2], f32)
    wtmp = sb("wtmp", [P, 2, K], f32)
    ids = sb("ids", [P, 4, 2], i32)
    masksum = sb("masksum", [P, E], bf16)
    ovc = sb("ovc", [P, 2, E], f32)

    base = sb("base", [P, TILES, D], f32)
    r_xe = region(TILES * ROW * 4)
    XE = sb("XE", [P, TILES, ROW], f32, within(r_xe))
    r_xt = region(2 * DC * TOK * 4)
    a = within(r_xt)
    XH = sb("XH", [P, DC, TOK], f32r, a)
    XL = sb("XL", [P, DC, TOK], f32r, a)
    r_raw = region(4 * WN * 4)
    raw = sb("raw", [P, 4 * WN], f32, within(r_raw))
    O_GATE, O_QKV = 0, DC * E
    O_WO = O_QKV + DC * 3 * D
    O_SGU = O_WO + DC * D
    O_SD = O_SGU + DC * 2 * FS
    NST = O_SD + SC * D
    WSH = sb("WSH", [P, NST], f32r)
    WSL = sb("WSL", [P, NST], f32r)
    a = within(r_raw)
    L = sb("L", [P, TILES, E], f32, a)
    mask = sb("mask", [P, TILES, E], bf16, a)
    run = sb("run", [P, TILES, E], f32, a)
    prod = sb("prod", [P, 4 * K, E], f32, a)
    top8 = sb("top8", [P, TILES, 8], f32, within(r_raw, 4 * WN * 4 - 2560))
    r_qk = region(3 * 2 * 8 * SEQ * 4)
    a = within(r_qk)
    QS, KS = [], []
    for s in range(3):
        QS.append(sb(f"QS{s}", [P, 8, SEQ], f32r, a))
        KS.append(sb(f"KS{s}", [P, 8, SEQ], f32r, a))
    a = within(r_qk, 2 * 2 * 8 * SEQ * 4)
    sgS = sb("sgS", [P, 2, FS], f32, a)
    aS = sb("aS", [P, 2, FS], f32, a)
    aSTH = sb("aSTH", [FH, 2, SC * P], f32r, a)
    aSTL = sb("aSTL", [FH, 2, SC * P], f32r, a)
    V = sb("V", [P, 2, 2, H, 32], f32)
    stg = [sb(n, [P, 2, SEQ], f32r) for n in ("qhi", "qlo", "khi", "klo")]
    r_at = region(16384)
    a = within(r_at)
    EX = sb("EX", [P, 3, 2 * SEQ], f32, a)
    OTs = sb("OTs", [P, 2, SEQ], f32, a)
    On = sb("On", [P, 2, 2, D], f32, a)
    OnTH = sb("OnTH", [P, DC, SEQ], f32r, a)
    OnTL = sb("OnTL", [P, DC, SEQ], f32r, a)
    a = within(r_at)
    oh = sb("oh", [P, TILES * K, E], bf16, a)
    fill = sb("fill", [P, 2, ROW], f32, a)
    bo = sb("bo", [P, D], f32, a)
    a = within(r_xt)
    GH = [sb(f"GH{s}", [P, GO], f32r, a) for s in range(2)]
    GL = [sb(f"GL{s}", [P, GO], f32r, a) for s in range(2)]
    DH = [sb(f"DH{s}", [FH, 2 * D], f32r, a) for s in range(2)]
    DL = [sb(f"DL{s}", [FH, 2 * D], f32r, a) for s in range(2)]
    a = within(r_xe)
    xin = sb("xin", [P, 4, 2, ROW], f32, a)
    xTH = [sb(f"xTH{s}", [P, DC, SLOTS], f32r, a) for s in range(2)]
    xTL = [sb(f"xTL{s}", [P, DC, SLOTS], f32r, a) for s in range(2)]
    a = within(r_qk)
    sg = sb("sg", [P, 2, 2, F], f32, a)
    act = sb("act", [P, 2, 2, F], f32, a)
    aTH = [sb(f"aTH{s}", [FH, 2, SLOTS], f32r, a) for s in range(2)]
    aTL = [sb(f"aTL{s}", [FH, 2, SLOTS], f32r, a) for s in range(2)]
    y = sb("y", [P, 4, 2, D], f32, a)
    ov_x = sb("ov_x", [P, ROW], f32, a)
    ov_xT = sb("ov_xT", [P, DC, P], f32, a)
    ov_a = sb("ov_a", [P, 2, F], f32, a)
    ov_aT = sb("ov_aT", [FH, 2, P], f32, a)
    ov_y = sb("ov_y", [P, D], f32, a)
    ov_c = sb("ov_c", [P, 4], f32, a)
    ov_id = sb("ov_id", [P, 2], i32, a)
    ov_cmp = sb("ov_cmp", [P, OVT, E], f32, within(r_xt))
    ov_e = sb("ov_e", [P, OVT], f32, within(r_xe))
    ov_ei = sb("ov_ei", [P, OVT], i32, within(r_xe, OVT * 4 + 32))

    PB = [nc.alloc_psum_tensor(f"bank{i}", [P, 512], f32) for i in range(8)]
    S_B, T_B, OT_B, A_B = (0, 1), (2, 3), (4, 7), (5, 6)

    def sem(name):
        return nc.alloc_semaphore(name)

    x_in = [sem(f"x_in{g}") for g in range(4)]
    ones2_ok = sem("ones2_ok")
    wq_in, w_in0, b_in = sem("wqkv_in"), sem("weights_in"), sem("bias_in")
    const_ok = sem("const_ok")
    var_ok, sqrt_ok, xn_ok = sem("var_ok"), sem("sqrt_ok"), sem("xn_ok")
    chain = sem("vector_chain")
    pchain = sem("pool_chain")
    achain = sem("scalar_chain")
    wsh_ok, wsl_ok = sem("static_hi_ok"), sem("static_lo_ok")
    a_full, a_hi, a_free = sem("a_full"), sem("a_hi"), sem("a_free")
    lg_full, lg_ok, dlt_ok, ex_ok = sem("logits_full"), sem("logits_ok"), sem("delta_ok"), sem("exp_ok")
    sum_ok, base_full = sem("masksum_ok"), sem("rank_base_full")
    route_ok, fill_in = sem("route_ok"), sem("fill_in")
    xbo_ok = sem("x_plus_bo_ok")
    sgu_full, ssilu_ok, sact_ok = sem("shared_gu_full"), sem("shared_silu_ok"), sem("shared_act_ok")
    sat_hi, sat_ok = sem("shared_actT_hi"), sem("shared_actT_ok")
    stg_q, stg_k, qk_w = sem("q_staged"), sem("k_staged"), sem("qk_written")
    qk_in = [sem(f"qk_in{s}") for s in range(3)]
    m_in = [sem(f"m_in{s}") for s in range(3)]
    s_full, max_ok, st_full, exp_ok = sem("s_full"), sem("max_ok"), sem("st_full"), sem("prob_ok")
    pv_ok, ot_ok, norm_ok = sem("pv_ok"), sem("ot_ok"), sem("norm_ok")
    v_ok, m_ok, m_w = sem("v_ok"), sem("m_ok"), sem("m_written")
    ont_ok, base_ok, out_w = sem("onT_ok"), sem("base_ok"), sem("out_written")
    scat_in = sem("rows_scattered")
    w_in = [sem(f"w_in{s}") for s in range(4)]
    r_in = [sem(f"rows_in{s}") for s in range(4)]
    guH_ok, gu_split, wd_split = sem("guH_ok"), sem("gu_split"), sem("wd_split")
    xt_full, xtH_ok, xt_ok = sem("xt_full"), sem("xtH_ok"), sem("xt_ok")
    gu_full, silu_ok, mul_ok = sem("gu_full"), sem("silu_ok"), sem("mul_ok")
    at_full, atH_ok, at_ok = sem("at_full"), sem("atH_ok"), sem("at_ok")
    dn_full, y_ok, scat, y_free = sem("dn_full"), sem("y_ok"), sem("added"), sem("y_free")
    wcol_ok, w_step, dh_ok = sem("wcol_ok"), sem("wcol_step"), sem("down_hi_ok")
    ov_e_ok, ov_in, ov_xT_full, ov_xT_ok = sem("ov_e_ok"), sem("ov_in"), sem("ov_xT_full"), sem("ov_xT_ok")
    ov_gu, ov_silu, ov_mul, ov_at = sem("ov_gu"), sem("ov_silu"), sem("ov_mul"), sem("ov_at")
    ov_s = sem("ov_step")
    ov_at_ok, ov_dn, ov_y_ok, ov_add, ov_w = (sem("ov_at_ok"), sem("ov_dn"), sem("ov_y_ok"),
                                              sem("ov_add"), sem("ov_w"))

    def extra(n):
        b, s = divmod(n, H)
        if s == 1 and b + 3 < B:
            return ("q", b + 3)
        if s == 3 and b + 3 < B:
            return ("k", b + 3)
        if s == 5 and 1 <= b <= B:
            return ("onT", b - 1)
        if s == 8 and 1 <= b <= B:
            return ("o", b - 1)
        if s == 9 and b + 1 < B:
            return ("mT", b + 1)
        if s == 11 and b + 1 < B:
            return ("v", b + 1)
        return None

    def nat(n):
        g = n // 4 - 2
        return ("nt", g) if n % 4 == 0 and 0 <= g < HEADS // 4 else None

    SLOT_END = HEADS + 9
    uses = [("xt", i) for i in range(TILES // 2)]
    uses += [(c, b) for b in range(2) for c in "qk"] + [("v", 0)]
    for t in range(TILES):
        uses += [("sT", t), ("sY", t)]
    uses += [("mT", 0), ("q", 2), ("k", 2)]
    for n in range(SLOT_END):
        uses += [u for u in (nat(n), extra(n)) if u]
    USE = {u: i for i, u in enumerate(uses)}

    def bank_of(u):
        return PB[A_B[USE[u] % 2]]

    def static(w, off, c, width, lo, n):
        s = off + c * width + lo
        return w[:, s:s + n]

    def raw32(ap):
        return ap.bitcast(f32)

    CONSTS, FILL_OK = 2, 1
    x_v = x.rearrange("(t p) c -> p t c", p=P)
    out_v = out[0:TOK, :].rearrange("(t p) c -> p t c", p=P)
    SPARE = out.shape[0] - TOK
    assert SPARE == SLOTS

    def load_w(sp, c, i, e):
        if e is None:
            sp.wait_ge(gu_split, 4 * i + (c - 3))
            sp.wait_ge(wd_split, 4 * i + (c - 3))
        elif e == 0:
            sp.wait_ge(route_ok, 1)
        o = c * WN
        if e is None:
            sg_, sd_ = wgu[bass.ds(4 * i + c, 1), :, :], wd[bass.ds(4 * i + c, 1), :, :]
        else:
            sg_, sd_ = wgu[e:e + 1, :, :], wd[e:e + 1, :, :]
        sp.dma_start(raw[:, o:o + GO], sg_.rearrange("a p n -> (a p) n")).then_inc(w_in[c], 16)
        sp.dma_start(raw[0:FH, o + GO:o + WN], sd_.rearrange("a p n -> (a p) n")).then_inc(w_in[c], 16)

    def load_rows(sp, c, i, e):
        if e is None:
            sp.wait_ge(xt_full, 4 * i + (c - 3))
            sp.wait_ge(wcol_ok, 4 * i + (c - 3))
            src = xs_d[bass.ds((4 * i + c) * SLOTS, SLOTS), :]
        else:
            if e == 0:
                sp.wait_ge(scat_in, 16 * TILES * K)
            src = xs_d[e * SLOTS:(e + 1) * SLOTS, :]
        sp.dma_start(xin[:, c, :, :], src.rearrange("(j p) n -> p j n", p=P)).then_inc(r_in[c], 16)

    block_cm = nc.Block()
    block = block_cm.__enter__()

    @block.sync
    def _(sp):
        sp.dma_start(base[:, 0:4, :], x_v[:, 0:4, :]).then_inc(x_in[0], 16)
        sp.dma_start(raw[:, O_GATE:O_QKV].rearrange("p (c n) -> p c n", c=DC), gate).then_inc(wq_in, 16)
        sp.dma_start(raw[:, O_QKV:O_WO].rearrange("p (c n) -> p c n", c=DC), wqkv).then_inc(wq_in, 16)
        for g in range(1, 4):
            sp.dma_start(base[:, 4 * g:4 * g + 4, :], x_v[:, 4 * g:4 * g + 4, :]).then_inc(x_in[g], 16)
        sp.dma_start(bq[:, :], bqk).then_inc(b_in, 16)
        sp.dma_start(bv[:, :], bvo[0:1, :].broadcast_to([P, D])).then_inc(b_in, 16)
        sp.dma_start(bo[:, :], bvo[1:2, :].broadcast_to([P, D])).then_inc(b_in, 16)
        sp.dma_start(raw[:, O_WO:O_SGU].rearrange("p (c n) -> p c n", c=DC), wo).then_inc(w_in0, 16)
        sp.dma_start(raw[:, O_SGU:O_SD].rearrange("p (c n) -> p c n", c=DC), wsgu).then_inc(w_in0, 16)
        sp.dma_start(raw[0:FH, O_SD:NST].rearrange("p (c n) -> p c n", c=SC), wsd).then_inc(w_in0, 16)

        FILLS = 16
        per = E // FILLS
        xs_v = xs_d[0:REG, :].rearrange("(e j p) c -> p e j c", j=2, p=P)

        def fill_part(i):
            for e in range(per * i, per * i + per):
                sp.dma_start(xs_v[:, e, :, :], fill[:, :, :]).then_inc(fill_in, 16)

        def qk_write(b):
            for w, (s0, ready) in enumerate(((0, stg_q), (2, stg_k))):
                sp.wait_ge(ready, b + 1)
                for s in (s0, s0 + 1):
                    sp.dma_start(qk_d[b, s].rearrange("(k p) q -> p k q", p=P), raw32(stg[s][:, :, :]))\
                      .then_inc(qk_w, 16)

        def qk_read(b):
            s = b % 3
            sp.wait_ge(qk_w, 64 * (b + 1))
            if b == 0:
                sp.wait_ge(const_ok, CONSTS)
            if b == 2:
                sp.wait_ge(ones2_ok, 1)
            if b >= 3:
                sp.wait_ge(st_full, H * (b - 2))
            for par in range(2):
                for dst, parts in ((QS[s], (0, 1, 0)), (KS[s], (2, 2, 3))):
                    for r, part in enumerate(parts):
                        src = qk_d[b, part].rearrange("(k r d) q -> r d k q", r=2, d=HD)[par]
                        lo = 64 * par + HD * r
                        sp.dma_start(raw32(dst[lo:lo + HD, :, :]), src).then_inc(qk_in[s], 16)

        def m_move(b):
            sp.wait_ge(m_ok, b + 1)
            sp.dma_start(m_d[b], raw32(mTs[:, :])).then_inc(m_w, 16)
            sp.wait_ge(m_w, 16 * (b + 1))
            for par in range(2):
                src = m_d[b].rearrange("(k r) q -> r k q", r=2)[par:par + 1]
                lo = 64 * par + 3 * HD
                sp.dma_start(raw32(QS[b % 3][lo:lo + 1, :, :]), src).then_inc(m_in[b % 3], 16)

        sp.wait_ge(const_ok, FILL_OK)
        sp.dma_start(out[TOK:TOK + SPARE, :].rearrange("(j p) c -> p j c", p=P), fill[:, :, 0:D])\
          .then_inc(out_w, 16)
        for i in range(2):
            fill_part(i)
        for b in range(2):
            qk_write(b)
            qk_read(b)
            for i in range(2 + 7 * b, 9 + 7 * b):
                fill_part(i)
        m_move(0)
        qk_write(2)
        qk_read(2)
        for b in range(B + 1):
            if b + 3 < B:
                qk_write(b + 3)
            if b >= 1:
                sp.wait_ge(base_ok, b)
                sp.dma_start(out_v[:, 2 * b - 2:2 * b, :], base[:, 2 * b - 2:2 * b, :]).then_inc(out_w, 16)
            if b + 1 < B:
                m_move(b + 1)
            if b + 3 < B:
                qk_read(b + 3)
            if b == 1:
                for e in range(4):
                    load_w(sp, e, 0, e)
        for e in range(4):
            load_rows(sp, e, 0, e)
        with sp.Fori(1, E // 4, 1) as i:
            for c in range(4):
                load_w(sp, c, i, None)
                load_rows(sp, c, i, None)
        sp.wait_ge(out_w, 16 * (B + 1))
        sp.wait_ge(y_free, E + 1)
        over = sp.value_load(nov_i[0:1, 0:1], min_val=0, max_val=OVT)
        with sp.If(over > 0):
            sp.wait_ge(ov_e_ok, 1)
            with sp.Fori(0, OVT, 1) as j:
                e = sp.value_load(ov_ei[0:1, bass.ds(j, 1)], min_val=0, max_val=E - 1)
                sp.wait_ge(ov_w, j + 1)
                sp.dma_start(raw[:, 0:GO], wgu[bass.ds(e, 1), :, :].rearrange("a p n -> (a p) n"))\
                  .then_inc(ov_in, 16)
                sp.dma_start(raw[0:FH, GO:WN], wd[bass.ds(e, 1), :, :].rearrange("a p n -> (a p) n"))\
                  .then_inc(ov_in, 16)
                sp.dma_start(ov_x[:, :], xs_d[bass.ds(j * P + REG, P), :]).then_inc(ov_in, 16)
            sp.wait_ge(ov_w, OVT + 1)
        sp.wait_ge(out_w, 16 * (B + 1))

    @block.gpsimd
    def _(pool):
        n = [0]

        def link(ins):
            n[0] += 1
            ins.then_inc(pchain, 1)
            pool.wait_ge(pchain, n[0])

        link(pool.memset(fill[:, :, :], 0.0))
        pool.iota(fill[:, :, C_TOK:C_TOK + 1].bitcast(i32), pattern=[[P, 2], [0, 1]], base=TOK,
                  channel_multiplier=1).then_inc(const_ok, 1)
        link(pool.memset(ident[:, :], 0.0))
        link(pool.affine_select(out=ident[:, :], in_=ident[:, :], compare_op=ALU.not_equal, fill=1.0,
                                base=0, pattern=[[-1, P]], channel_multiplier=1))
        link(pool.memset(ones[:, :], 1.0))
        link(pool.affine_select(out=before[:, :], in_=ones[:, :], compare_op=ALU.is_gt, fill=0.0,
                                base=0, pattern=[[1, P]], channel_multiplier=-1))
        link(pool.iota(iota_e[:, :], pattern=[[1, E]], base=0, channel_multiplier=0,
                       allow_small_or_imprecise_dtypes=True))
        link(pool.iota(ecur[:, :], pattern=[[1, 4]], base=-4, channel_multiplier=0,
                       allow_small_or_imprecise_dtypes=True))
        link(pool.memset(XE[:, :, C_TOK + 1:ROW], 0.0))
        link(pool.iota(XE[:, :, C_TOK:C_TOK + 1].bitcast(i32), pattern=[[P, TILES], [0, 1]], base=0,
                       channel_multiplier=1))
        link(pool.memset(V[:, :, :, :, HD:32], 0.0))
        link(pool.memset(V[:, :, :, :, HD:HD + 1], 1.0))
        for s in range(2):
            for lo in (32, 96):
                last = pool.memset(raw32(KS[s][lo:lo + 32, :, :]), 1.0)
        last.then_inc(const_ok, 1)

        pool.wait_ge(b_in, 48)
        pool.wait_ge(xn_ok, TILES)
        for t in range(TILES):
            pool.tensor_tensor(base[:, t, :], base[:, t, :], bo[:, :], ALU.add).then_inc(xbo_ok, 1)

        pool.wait_ge(route_ok, 1)
        over = pool.value_load(nov_i[0:1, 0:1], min_val=0, max_val=OVT)
        with pool.If(over > 0):
            xo_v = xs_d[REG:REG + OVT * P, :].rearrange("(j p) c -> p j c", p=P)
            with pool.Fori(0, OVT, 1) as j:
                pool.dma_start(xo_v[:, bass.ds(j, 1), :], fill[:, 0:1, :]).then_inc(ov_add, 16)
            pool.wait_ge(ov_add, 16 * OVT)
        pool.wait_ge(fill_in, 16 * E)
        for t in range(TILES):
            for k in range(K):
                i = t * K + k
                pool.indirect_dma_start(xs_d, bass.IndirectOffsetOnAxis(ap=posi[:, i:i + 1], axis=0),
                                        XE[:, t, :], None).then_inc(scat_in, 16)

        pool.sem_inc(y_free, 1)

        def add(i, c, first=False, second=False):
            pool.wait_ge(y_ok, 8 * i + (2 * c + 2))
            if first:
                pool.wait_ge(out_w, 16 * (B + 1))
            else:
                pool.wait_ge(scat, 128 * i + 32 * c)
                pool.sem_inc(y_free, 1)
            for j in range(2):
                pool.indirect_dma_start(out, bass.IndirectOffsetOnAxis(ap=ids[:, c, j:j + 1], axis=0),
                                        y[:, c, j, :], None, compute_op=ALU.add).then_inc(scat, 16)

        for c in range(4):
            add(0, c, first=c == 0)
        with pool.Fori(1, E // 4, 1) as i:
            for c in range(4):
                add(i, c)
        pool.wait_ge(scat, 32 * E)
        pool.sem_inc(y_free, 1)
        over = pool.value_load(nov_i[0:1, 0:1], min_val=0, max_val=OVT)
        with pool.If(over > 0):
            pool.sem_inc(ov_w, 1)
            with pool.Fori(0, OVT, 1) as j:
                pool.wait_ge(ov_y_ok, j + 1)
                pool.sem_inc(pchain, 1)
                pool.indirect_dma_start(out, bass.IndirectOffsetOnAxis(ap=ov_id[:, 0:1], axis=0),
                                        ov_y[:, :], None, compute_op=ALU.add).then_inc(ov_add, 16)
                pool.wait_ge(ov_add, 16 * j + 16 * (OVT + 1))
                pool.sem_inc(ov_w, 1)
            pool.wait_ge(ov_w, OVT + 1)
        pool.wait_ge(scat, 32 * E)

    @block.tensor
    def _(pe):
        def product(dst, lh, ll, rh, rl, first=True, last=True):
            pe.matmul(dst, lhsT=lh, rhs=rh, start=first, stop=False)
            pe.matmul(dst, lhsT=lh, rhs=rl, start=False, stop=False)
            return pe.matmul(dst, lhsT=ll, rhs=rh, start=False, stop=last)

        def claim(u):
            if USE[u] >= 2:
                pe.wait_ge(a_free, USE[u] - 1)
            return bank_of(u)

        def xt_tiles(i):
            pe.wait_ge(xn_ok, 2 * i + 2)
            bk = claim(("xt", i))
            for c in range(DC):
                for j in range(2):
                    last = pe.transpose(bk[:, (2 * c + j) * P:(2 * c + j + 1) * P],
                                        in_=XE[:, 2 * i + j, c * P:(c + 1) * P], identity=ident[:, :])
            last.then_inc(a_full, 1)

        def project(which, b):
            u = (which, b)
            bk = claim(u)
            col = 0 if which == "q" else D
            for k in range(2):
                for c in range(DC):
                    last = product(bk[:, k * SEQ:(k + 1) * SEQ],
                                   static(WSH, O_QKV, c, 3 * D, col + k * P, P),
                                   static(WSL, O_QKV, c, 3 * D, col + k * P, P),
                                   XH[:, c, b * SEQ:(b + 1) * SEQ], XL[:, c, b * SEQ:(b + 1) * SEQ],
                                   c == 0, c == DC - 1)
            last.then_inc(a_full, 1)

        def values(b):
            bk = claim(("v", b))
            for j in range(2):
                for c in range(DC):
                    t = slice((2 * b + j) * P, (2 * b + j + 1) * P)
                    last = product(bk[:, j * D:(j + 1) * D], XH[:, c, t], XL[:, c, t],
                                   static(WSH, O_QKV, c, 3 * D, 2 * D, D),
                                   static(WSL, O_QKV, c, 3 * D, 2 * D, D), c == 0, c == DC - 1)
            last.then_inc(a_full, 1)

        def scores(n):
            b, h = divmod(n, H)
            k, lo = h // 2, 64 * (h % 2)
            if h == 0:
                pe.wait_ge(qk_in[b % 3], 192 * (b // 3 + 1))
            if n == 0:
                pe.wait_ge(route_ok, 1)
            if n >= 2:
                pe.wait_ge(max_ok, n - 1)
            for j in range(2):
                last = pe.matmul(PB[S_B[n % 2]][:, j * SEQ:(j + 1) * SEQ],
                                 lhsT=QS[b % 3][lo:lo + 3 * HD, k, j * P:(j + 1) * P],
                                 rhs=KS[b % 3][lo:lo + 3 * HD, k, :], start=True, stop=True)
            last.then_inc(s_full, 1)

        def scores_t(n):
            b, h = divmod(n, H)
            k, lo = h // 2, 64 * (h % 2)
            if h == 0:
                pe.wait_ge(m_in[b % 3], 32 * (b // 3 + 1))
            if n == 0:
                pe.wait_ge(sact_ok, TILES)
            if n >= 2:
                pe.wait_ge(exp_ok, n - 1)
            for j in range(2):
                last = pe.matmul(PB[T_B[n % 2]][:, j * SEQ:(j + 1) * SEQ],
                                 lhsT=KS[b % 3][lo:lo + 3 * HD + 1, k, j * P:(j + 1) * P],
                                 rhs=QS[b % 3][lo:lo + 3 * HD + 1, k, :], start=True, stop=True)
            last.then_inc(st_full, 1)

        def weigh(n):
            b, h = divmod(n, H)
            g = n // 4
            pe.wait_ge(exp_ok, n + 1)
            if h == 0:
                pe.wait_ge(v_ok, b + 1)
            if n % 4 == 0 and g >= 2:
                pe.wait_ge(ot_ok, g - 1)
            lo = 32 * (n % 4)
            for j in range(2):
                last = pe.matmul(PB[OT_B[g % 2]][lo:lo + 32, 0:SEQ],
                                 lhsT=V[:, b % 2, j, h, :], rhs=EX[:, n % 3, j * SEQ:(j + 1) * SEQ],
                                 start=j == 0, stop=j == 1)
            last.then_inc(pv_ok, 1)

        def natural(g):
            pe.wait_ge(ot_ok, g + 1)
            bk = claim(("nt", g))
            for j in range(2):
                last = pe.transpose(bk[:, j * P:(j + 1) * P], in_=OTs[:, g % 2, j * P:(j + 1) * P],
                                    identity=ident[:, :])
            last.then_inc(a_full, 1)

        def neg_max_t(b):
            pe.wait_ge(max_ok, H * (b + 1))
            bk = claim(("mT", b))
            for j in range(2):
                last = pe.transpose(bk[0:H, j * P:(j + 1) * P], in_=mx[:, b % 2, j, :],
                                    identity=ident[:, :])
            last.then_inc(a_full, 1)

        def out_t(b):
            pe.wait_ge(norm_ok, 4 * b + 4)
            bk = claim(("onT", b))
            for c in range(DC):
                for j in range(2):
                    last = pe.transpose(bk[:, (2 * c + j) * P:(2 * c + j + 1) * P],
                                        in_=On[:, b % 2, j, c * P:(c + 1) * P], identity=ident[:, :])
            last.then_inc(a_full, 1)

        def out_proj(b):
            pe.wait_ge(ont_ok, b + 1)
            bk = claim(("o", b))
            for j in range(2):
                for c in range(DC):
                    last = product(bk[:, j * D:(j + 1) * D], OnTH[:, c, j * P:(j + 1) * P],
                                   OnTL[:, c, j * P:(j + 1) * P], static(WSH, O_WO, c, D, 0, D),
                                   static(WSL, O_WO, c, D, 0, D), c == 0, c == DC - 1)
            last.then_inc(a_full, 1)

        pe.wait_ge(const_ok, CONSTS)
        for i in range(TILES // 2):
            xt_tiles(i)
        pe.wait_ge(wsl_ok, 1)
        for t in range(TILES):
            if t % 2 == 0:
                pe.wait_ge(a_free, t // 2 + 1)
            for c in range(DC):
                tt = slice(t * P, (t + 1) * P)
                last = product(PB[T_B[t // 8]][:, (t % 8) * E:(t % 8 + 1) * E], XH[:, c, tt], XL[:, c, tt],
                               static(WSH, O_GATE, c, E, 0, E), static(WSL, O_GATE, c, E, 0, E),
                               c == 0, c == DC - 1)
            if t % 8 == 7:
                last.then_inc(lg_full, 1)
        for b in range(2):
            project("q", b)
            project("k", b)
        values(0)
        pe.wait_ge(sum_ok, 1)
        pe.matmul(PB[S_B[0]][:, 0:E], lhsT=before[:, :], rhs=masksum[:, :], start=True, stop=True)
        pe.matmul(PB[S_B[0]][:, E:2 * E], lhsT=ones[:, :], rhs=masksum[:, :], start=True, stop=True)\
          .then_inc(base_full, 1)

        pe.wait_ge(wsl_ok, 2)
        pe.wait_ge(lg_ok, 2)

        def shared_up(t):
            if t >= 2:
                pe.wait_ge(sact_ok, t - 1)
            for half in range(2):
                bk = PB[(T_B, OT_B)[t % 2][half]]
                for c in range(DC):
                    tt = slice(t * P, (t + 1) * P)
                    last = product(bk[:, 0:FS], XH[:, c, tt], XL[:, c, tt],
                                   static(WSH, O_SGU, c, 2 * FS, half * FS, FS),
                                   static(WSL, O_SGU, c, 2 * FS, half * FS, FS), c == 0, c == DC - 1)
            last.then_inc(sgu_full, 1)

        def shared_down(t):
            pe.wait_ge(sact_ok, t + 1)
            bk = claim(("sT", t))
            for c in range(SC):
                last = pe.transpose(bk[0:FH, c * P:(c + 1) * P], in_=aS[:, t % 2, c * FH:(c + 1) * FH],
                                    identity=ident[:, :])
            last.then_inc(a_full, 1)

        def shared_out(t):
            pe.wait_ge(sat_ok, t + 1)
            bk = claim(("sY", t))
            for c in range(SC):
                last = product(bk[:, 0:D], aSTH[:, t % 2, c * P:(c + 1) * P],
                               aSTL[:, t % 2, c * P:(c + 1) * P],
                               static(WSH, O_SD, c, D, 0, D)[0:FH], static(WSL, O_SD, c, D, 0, D)[0:FH],
                               c == 0, c == SC - 1)
            last.then_inc(a_full, 1)

        shared_up(0)
        n = 0
        for t in range(TILES):
            if t + 1 < TILES:
                shared_up(t + 1)
            shared_down(t)
            while n < min(LEAD, 3 * (t - 6)):
                scores(n)
                n += 1
            shared_out(t)
        neg_max_t(0)
        project("q", 2)
        project("k", 2)

        for n in range(SLOT_END):
            if n < HEADS:
                scores_t(n)
            if n + LEAD < HEADS:
                scores(n + LEAD)
            if 2 <= n < HEADS + 2:
                weigh(n - 2)
            if nat(n):
                natural(nat(n)[1])
            u = extra(n)
            if u:
                kind, b = u
                if kind in "qk":
                    project(kind, b)
                elif kind == "v":
                    values(b)
                elif kind == "mT":
                    neg_max_t(b)
                elif kind == "onT":
                    out_t(b)
                else:
                    out_proj(b)

        pe.wait_ge(max_ok, HEADS)
        pe.wait_ge(exp_ok, HEADS)
        pe.wait_ge(norm_ok, HEADS // 4)
        pe.wait_ge(ot_ok, HEADS // 4)
        pe.wait_ge(a_free, len(uses))
        X_B, AT_B, Y_B = A_B[0], A_B[1], OT_B

        def wait(s, v):
            if not (isinstance(v, int) and v <= 0):
                pe.wait_ge(s, v)

        def rows_t(i, c):
            wait(r_in[c % 4], 16 * (i + c // 4) + 16)
            wait(xt_ok, 4 * i + c)
            for k in range(DC):
                for j in range(2):
                    last = pe.transpose(PB[X_B][:, (2 * k + j) * P:(2 * k + j + 1) * P],
                                        in_=xin[:, c % 4, j, k * P:(k + 1) * P], identity=ident[:, :])
            last.then_inc(xt_full, 1)

        def up(i, c, j):
            s = c % 2
            wait(xt_ok, 4 * i + c + 1)
            wait(gu_split, 4 * i + c + 1)
            wait(mul_ok, 8 * i + 2 * (c - 2) + j + 1)
            for k in range(DC):
                last = product(PB[2 * s + j][:, 0:GN], xTH[s][:, k, j * P:(j + 1) * P],
                               xTL[s][:, k, j * P:(j + 1) * P], GH[s][:, k * GN:(k + 1) * GN],
                               GL[s][:, k * GN:(k + 1) * GN], k == 0, k == DC - 1)
            last.then_inc(gu_full, 1)

        def act_t(i, c):
            wait(mul_ok, 8 * i + 2 * c + 2)
            wait(at_ok, 4 * i + c)
            for k in range(2):
                for j in range(2):
                    last = pe.transpose(PB[AT_B][0:FH, (2 * k + j) * P:(2 * k + j + 1) * P],
                                        in_=act[:, c % 2, j, k * FH:(k + 1) * FH], identity=ident[:, :])
            last.then_inc(at_full, 1)

        def down(i, c):
            s = c % 2
            wait(at_ok, 4 * i + c + 1)
            wait(wd_split, 4 * i + c + 1)
            wait(y_ok, 8 * i + 2 * (c - 2) + 2)
            for j in range(2):
                for k in range(2):
                    last = product(PB[Y_B[s]][:, j * D:(j + 1) * D], aTH[s][:, k, j * P:(j + 1) * P],
                                   aTL[s][:, k, j * P:(j + 1) * P], DH[s][:, k * D:(k + 1) * D],
                                   DL[s][:, k * D:(k + 1) * D], k == 0, k == 1)
            last.then_inc(dn_full, 1)

        def step(i, c, first=False, last=False):
            up(i, c, 0)
            if not first:
                act_t(i, c - 1)
            if not last:
                rows_t(i, c + 1)
            up(i, c, 1)
            if not first:
                down(i, c - 1)

        rows_t(0, 0)
        for c in range(4):
            step(0, c, first=c == 0)
        with pe.Fori(1, E // 4 - 1, 1) as i:
            for c in range(4):
                step(i, c)
        for c in range(4):
            step(E // 4 - 1, c, last=c == 3)
        act_t(E // 4 - 1, 3)
        down(E // 4 - 1, 3)

        over = pe.value_load(nov_i[0:1, 0:1], min_val=0, max_val=OVT)
        with pe.If(over > 0):
            with pe.Fori(0, OVT, 1) as j:
                pe.wait_ge(ov_in, 48 * j + 48)
                for k in range(DC):
                    last = pe.transpose(PB[0][:, k * P:(k + 1) * P], in_=ov_x[:, k * P:(k + 1) * P],
                                        identity=ident[:, :])
                last.then_inc(ov_xT_full, 1)
                pe.wait_ge(ov_xT_ok, j + 1)
                for k in range(DC):
                    last = pe.matmul(PB[1][:, 0:GN], lhsT=ov_xT[:, k, :], rhs=raw[:, k * GN:(k + 1) * GN],
                                     start=k == 0, stop=k == DC - 1)
                last.then_inc(ov_gu, 1)
                pe.wait_ge(ov_mul, j + 1)
                for k in range(2):
                    last = pe.transpose(PB[2][0:FH, k * P:(k + 1) * P], in_=ov_a[:, 1, k * FH:(k + 1) * FH],
                                        identity=ident[:, :])
                last.then_inc(ov_at, 1)
                pe.wait_ge(ov_at_ok, j + 1)
                for k in range(2):
                    last = pe.matmul(PB[3][:, 0:D], lhsT=ov_aT[:, k, :],
                                     rhs=raw[0:FH, GO + k * D:GO + (k + 1) * D], start=k == 0, stop=k == 1)
                last.then_inc(ov_dn, 1)
            pe.wait_ge(ov_mul, OVT)

    @block.scalar
    def _(sc):
        def high(u, dst, src):
            sc.wait_ge(a_full, USE[u] + 1)
            return nc.scalar.activation(dst, src, ACT.Copy)

        sc.wait_ge(wq_in, 32)
        nc.scalar.activation(WSH[:, O_GATE:O_WO], raw[:, O_GATE:O_WO], ACT.Copy).then_inc(wsh_ok, 1)

        def square_root(g):
            sc.wait_ge(var_ok, g + 1)
            nc.scalar.activation(rstd[:, 4 * g:4 * g + 4, 1], rstd[:, 4 * g:4 * g + 4, 0], ACT.Sqrt)\
              .then_inc(sqrt_ok, 1)

        def xt_high(i):
            u = ("xt", i)
            high(u, XH[:, :, 2 * i * P:(2 * i + 2) * P],
                 bank_of(u)[:, :].rearrange("p (c n) -> p c n", c=DC)).then_inc(a_hi, 1)

        square_root(0)
        square_root(1)
        square_root(2)
        xt_high(0)
        xt_high(1)
        square_root(3)
        xt_high(2)
        xt_high(3)
        sc.wait_ge(w_in0, 48)
        nc.scalar.activation(WSH[:, O_WO:O_SD], raw[:, O_WO:O_SD], ACT.Copy)
        nc.scalar.activation(WSH[0:FH, O_SD:NST], raw[0:FH, O_SD:NST], ACT.Copy).then_inc(wsh_ok, 1)
        for i in range(4, TILES // 2):
            xt_high(i)
        for g in range(2):
            sc.wait_ge(lg_full, g + 1)
            if g == 0:
                sc.wait_ge(wsl_ok, 2)
            nc.scalar.activation(L[:, 8 * g:8 * g + 8, :],
                                 PB[T_B[g]][:, :].rearrange("p (t e) -> p t e", t=8), ACT.Copy)\
              .then_inc(lg_ok, 1)

        def stage(which, b):
            u = (which, b)
            s = 0 if which == "q" else 2
            if b >= 1:
                sc.wait_ge(qk_w, 64 * b)
            sc.wait_ge(a_full, USE[u] + 1)
            for k in range(2):
                last = nc.scalar.activation(stg[s][:, k, :], bank_of(u)[:, k * SEQ:(k + 1) * SEQ],
                                            ACT.Identity, bias=bq[:, s + k:s + k + 1])
            last.then_inc(a_hi, 1)

        sc.wait_ge(b_in, 48)
        for b in range(2):
            stage("q", b)
            stage("k", b)
        sc.wait_ge(dlt_ok, 1)
        nc.scalar.activation(run[:, :, :], run[:, :, :], ACT.Exp)
        nc.scalar.activation(XE[:, :, C_W:C_W + K], XE[:, :, C_W:C_W + K], ACT.Exp).then_inc(ex_ok, 1)

        def shared_act(t):
            sc.wait_ge(sgu_full, t + 1)
            if t >= 2:
                sc.wait_ge(sact_ok, t - 1)
            nc.scalar.activation(sgS[:, t % 2, :], PB[(T_B, OT_B)[t % 2][0]][:, 0:FS], ACT.Silu)\
              .then_inc(ssilu_ok, 1)

        def shared_actT(t):
            u = ("sT", t)
            if t >= 2:
                sc.wait_ge(a_full, USE[("sY", t - 2)] + 1)
            high(u, aSTH[:, t % 2, :], bank_of(u)[0:FH, :]).then_inc(sat_hi, 1)

        shared_act(0)
        for t in range(TILES):
            if t + 1 < TILES:
                shared_act(t + 1)
            shared_actT(t)

        def prob(n):
            sc.wait_ge(st_full, n + 1)
            if n >= 3:
                sc.wait_ge(pv_ok, n - 2)
            elif n == 0:
                sc.wait_ge(route_ok, 1)
            nc.scalar.activation(EX[:, n % 3, :], PB[T_B[n % 2]][:, :], ACT.Exp, scale=SCALE)\
              .then_inc(exp_ok, 1)

        def take_out(g):
            sc.wait_ge(pv_ok, 4 * g + 4)
            if g >= 2:
                sc.wait_ge(a_full, USE[("nt", g - 2)] + 1)
            if g == 0:
                sc.wait_ge(fill_in, 16 * E)
            nc.scalar.activation(OTs[:, g % 2, :], PB[OT_B[g % 2]][:, 0:SEQ], ACT.Copy)\
              .then_inc(ot_ok, 1)

        stage("q", 2)
        stage("k", 2)
        for n in range(SLOT_END):
            if n < HEADS:
                prob(n)
            if n >= 5 and (n - 5) % 4 == 0 and (n - 5) // 4 < HEADS // 4:
                take_out((n - 5) // 4)
            u = extra(n)
            if u and u[0] in "qk":
                stage(*u)
            elif u and u[0] == "onT":
                if u[1] >= 1:
                    sc.wait_ge(a_full, USE[("o", u[1] - 1)] + 1)
                high(u, OnTH[:, :, :], bank_of(u)[:, :].rearrange("p (c n) -> p c n", c=DC))\
                    .then_inc(a_hi, 1)

        def wait(s, v):
            if not (isinstance(v, int) and v <= 0):
                sc.wait_ge(s, v)

        def gate_high(i, c):
            wait(w_in[c % 4], 32 * (i + c // 4) + 32)
            wait(gu_full, 8 * i + 2 * (c - 2) + 2)
            o = (c % 4) * WN
            nc.scalar.activation(GH[c % 2][:, :], raw[:, o:o + GO], ACT.Copy).then_inc(guH_ok, 1)

        def silu(i, c, j):
            wait(gu_full, 8 * i + 2 * c + j + 1)
            nc.scalar.activation(sg[:, c % 2, j, :], PB[2 * (c % 2) + j][:, 0:F], ACT.Silu)\
              .then_inc(silu_ok, 1)

        def act_high(i, c):
            wait(at_full, 4 * i + c + 1)
            wait(dn_full, 4 * i + c - 1)
            nc.scalar.activation(aTH[c % 2][:, :, :],
                                 PB[A_B[1]][0:FH, :].rearrange("p (k n) -> p k n", k=2), ACT.Copy)\
              .then_inc(atH_ok, 1)

        def rows_high(i, c):
            wait(xt_full, 4 * i + c + 1)
            wait(gu_full, 8 * i + 2 * (c - 2) + 2)
            nc.scalar.activation(xTH[c % 2][:, :, :],
                                 PB[A_B[0]][:, :].rearrange("p (k n) -> p k n", k=DC), ACT.Copy)\
              .then_inc(xtH_ok, 1)

        def weighted(i, c):
            for j in range(2):
                if j == 0:
                    wait(dn_full, 4 * i + c + 1)
                    wait(wcol_ok, 4 * i + c + 1)
                    wait(y_free, 4 * i + c - 2)
                nc.scalar.activation(y[:, c % 4, j, :], PB[OT_B[c % 2]][:, j * D:(j + 1) * D],
                                     ACT.Copy, scale=wcol[:, c % 4, j:j + 1]).then_inc(y_ok, 1)

        def step(i, c, first=False, last=False):
            if not last:
                gate_high(i, c + 1)
            silu(i, c, 0)
            if not first:
                act_high(i, c - 1)
            if not last:
                rows_high(i, c + 1)
            silu(i, c, 1)
            if not first:
                weighted(i, c - 1)

        sc.wait_ge(a_full, USE[("v", B - 1)] + 1)
        gate_high(0, 0)
        rows_high(0, 0)
        for c in range(4):
            step(0, c, first=c == 0)
        with sc.Fori(1, E // 4 - 1, 1) as i:
            for c in range(4):
                step(i, c)
        for c in range(4):
            step(E // 4 - 1, c, last=c == 3)
        act_high(E // 4 - 1, 3)
        weighted(E // 4 - 1, 3)

        over = sc.value_load(nov_i[0:1, 0:1], min_val=0, max_val=OVT)
        with sc.If(over > 0):
            with sc.Fori(0, OVT, 1) as j:
                sc.wait_ge(ov_gu, j + 1)
                nc.scalar.activation(ov_a[:, 0, :], PB[1][:, 0:F], ACT.Silu).then_inc(ov_silu, 1)
            sc.wait_ge(ov_gu, OVT)

    @block.vector
    def _(ve):
        n_ = [0]

        def link(ins):
            n_[0] += 1
            ins.then_inc(chain, 1)
            ve.wait_ge(chain, n_[0])

        def low(dst, src, hi):
            return nc.vector.tensor_tensor(dst, src, raw32(hi), ALU.subtract)

        def stats(g):
            ve.wait_ge(x_in[g], 16)
            for t in range(4 * g, 4 * g + 4):
                last = nc.vector.bn_stats(st6[:, t, :], base[:, t, :])
            link(last)
            for t in range(4 * g, 4 * g + 4):
                last = nc.vector.bn_aggr(mv[:, t, :], st6[:, t, :])
            link(last)
            nc.vector.tensor_scalar_add(rstd[:, 4 * g:4 * g + 4, 0], mv[:, 4 * g:4 * g + 4, 1], LN_EPS)\
              .then_inc(var_ok, 1)

        def normalise(g):
            ve.wait_ge(sqrt_ok, g + 1)
            link(nc.vector.reciprocal(rstd[:, 4 * g:4 * g + 4, 2], rstd[:, 4 * g:4 * g + 4, 1]))
            for t in range(4 * g, 4 * g + 4):
                nc.vector.tensor_scalar(XE[:, t, 0:D], base[:, t, :], mv[:, t, 0:1], rstd[:, t, 2:3],
                                        ALU.subtract, ALU.mult).then_inc(xn_ok, 1)

        def low_of_a(u, dst, src, hi, hi_sem, hi_val):
            ve.wait_ge(hi_sem, hi_val)
            return low(dst, src, hi).then_inc(a_free, 1)

        hi_n = [0]

        def xt_low(i):
            u = ("xt", i)
            hi_n[0] += 1
            s = slice(2 * i * P, (2 * i + 2) * P)
            low_of_a(u, XL[:, :, s], bank_of(u)[:, :].rearrange("p (c n) -> p c n", c=DC), XH[:, :, s],
                     a_hi, hi_n[0])

        def stage_low(which, b):
            u = (which, b)
            s = 0 if which == "q" else 2
            hi_n[0] += 1
            ve.wait_ge(a_hi, hi_n[0])
            for k in range(2):
                last = nc.vector.scalar_tensor_tensor(out=stg[s + 1][:, k, :],
                                                      in0=bank_of(u)[:, k * SEQ:(k + 1) * SEQ],
                                                      scalar=bq[:, s + k:s + k + 1],
                                                      in1=raw32(stg[s][:, k, :]), op0=ALU.add,
                                                      op1=ALU.subtract)
            last.then_inc(stg_q if which == "q" else stg_k, 1)
            ve.wait_ge(stg_q if which == "q" else stg_k, b + 1)
            ve.sem_inc(a_free, 1)

        def values(b):
            u = ("v", b)
            ve.wait_ge(a_full, USE[u] + 1)
            if b >= 2:
                ve.wait_ge(pv_ok, H * (b - 1))
            nc.vector.tensor_tensor(V[:, b % 2, :, :, 0:HD],
                                    bank_of(u)[:, :].rearrange("p (t h d) -> p t h d", t=2, h=H),
                                    bv[:, :].rearrange("p (a h d) -> p a h d", a=1, h=H)
                                    .broadcast_to([P, 2, H, HD]), ALU.add).then_inc(v_ok, 1)
            ve.wait_ge(v_ok, b + 1)
            ve.sem_inc(a_free, 1)

        ve.wait_ge(const_ok, CONSTS)
        stats(0)
        stats(1)
        normalise(0)
        ve.wait_ge(wsh_ok, 1)
        low(WSL[:, O_GATE:O_WO], raw[:, O_GATE:O_WO], WSH[:, O_GATE:O_WO]).then_inc(wsl_ok, 1)
        normalise(1)
        stats(2)
        xt_low(0)
        xt_low(1)
        normalise(2)
        stats(3)
        xt_low(2)
        xt_low(3)
        normalise(3)
        ve.wait_ge(wsh_ok, 2)
        low(WSL[:, O_WO:O_SD], raw[:, O_WO:O_SD], WSH[:, O_WO:O_SD])
        low(WSL[0:FH, O_SD:NST], raw[0:FH, O_SD:NST], WSH[0:FH, O_SD:NST]).then_inc(wsl_ok, 1)
        for i in range(4, TILES // 2):
            xt_low(i)

        idx8 = prod[:, 0:2, :].rearrange("p a (b c) -> p (a b) c", c=8).bitcast(u32)
        for t in range(TILES):
            if t % 8 == 0:
                ve.wait_ge(lg_ok, t // 8 + 1)
            link(nc.vector.max(top8[:, t, :], L[:, t, :]))
            last = nc.vector.max_index(idx8[:, t, :], top8[:, t, :], L[:, t, :])
        link(last)
        link(nc.vector.tensor_copy(XE[:, :, C_IDX:C_IDX + K], idx8[:, :, 0:K]))
        nc.vector.tensor_tensor(run[:, :, :], L[:, :, :], top8[:, :, 0:1].broadcast_to([P, TILES, E]),
                                ALU.subtract)
        nc.vector.tensor_tensor(XE[:, :, C_W:C_W + K], top8[:, :, 0:K],
                                top8[:, :, 0:1].broadcast_to([P, TILES, K]), ALU.subtract)\
          .then_inc(dlt_ok, 1)
        for g in range(4):
            link(nc.vector.tensor_tensor(
                oh[:, 4 * g * K:4 * (g + 1) * K, :].rearrange("p (t k) e -> p t k e", k=K),
                iota_e[:, :].rearrange("p (a b e) -> p a b e", a=1, b=1).broadcast_to([P, 4, K, E]),
                XE[:, 4 * g:4 * g + 4, C_IDX:C_IDX + K].rearrange("p t (k a) -> p t k a", a=1)
                .broadcast_to([P, 4, K, E]), ALU.is_equal))
            if g == 1:
                stage_low("q", 0)
                stage_low("k", 0)
        stage_low("q", 1)
        stage_low("k", 1)
        values(0)
        with nc.allow_low_precision("counts up to 16 are exact"):
            link(nc.vector.tensor_reduce(mask[:, :, :], oh[:, :, :].rearrange("p (t k) e -> p t e k", k=K),
                                         AX.X, ALU.add))
            nc.vector.tensor_reduce(masksum[:, :], mask[:, :, :].rearrange("p t e -> p e t"), AX.X,
                                    ALU.add).then_inc(sum_ok, 1)
        ve.wait_ge(ex_ok, 1)
        w6 = XE[:, :, C_W:C_W + K]
        link(nc.vector.tensor_reduce(top8[:, :, 0], run[:, :, :], AX.X, ALU.add))
        link(nc.vector.reciprocal(top8[:, :, 1], top8[:, :, 0]))
        link(nc.vector.tensor_tensor(w6, w6, top8[:, :, 1:2].broadcast_to([P, TILES, K]), ALU.mult))
        link(nc.vector.tensor_reduce(top8[:, :, 2], w6, AX.X, ALU.add))
        link(nc.vector.tensor_scalar_add(top8[:, :, 3], top8[:, :, 2], TOPK_EPS))
        link(nc.vector.reciprocal(top8[:, :, 4], top8[:, :, 3]))
        link(nc.vector.tensor_tensor(w6, w6, top8[:, :, 4:5].broadcast_to([P, TILES, K]), ALU.mult))
        ve.wait_ge(base_full, 1)
        link(nc.vector.tensor_copy(run[:, 0, :], PB[S_B[0]][:, 0:E]))
        for t in range(1, TILES):
            link(nc.vector.tensor_tensor(run[:, t, :], run[:, t - 1, :], mask[:, t - 1, :], ALU.add))
        tiles_i = L[:, 0, :].bitcast(i32)
        link(nc.vector.tensor_scalar(tiles_i, PB[S_B[0]][:, E:2 * E], float(SLOTS - P + 1), 0.0,
                                     ALU.subtract, ALU.max))
        link(nc.vector.tensor_scalar(tiles_i, tiles_i, 7, None, ALU.logical_shift_right))
        link(nc.vector.tensor_copy(ovc[:, 0, :], tiles_i))
        link(nc.vector.tensor_copy(L[:, 1, :], ovc[:, 0, :]))
        cur, sh = 0, 1
        while sh < E:
            nc.vector.tensor_copy(ovc[:, 1 - cur, 0:sh], ovc[:, cur, 0:sh])
            link(nc.vector.tensor_tensor(ovc[:, 1 - cur, sh:E], ovc[:, cur, sh:E], ovc[:, cur, 0:E - sh],
                                         ALU.add))
            cur, sh = 1 - cur, 2 * sh
        OVC = cur
        nc.vector.tensor_copy(nov_i[:, 0:1], ovc[:, OVC, E - 1:E])
        link(nc.vector.tensor_tensor(L[:, 2, :], ovc[:, OVC, :], L[:, 1, :], ALU.subtract))
        link(nc.vector.tensor_scalar(L[:, 3, :], L[:, 2, :], float(P), float(REG - SLOTS), ALU.mult, ALU.add))
        link(nc.vector.scalar_tensor_tensor(out=L[:, 4, :], in0=iota_e[:, :], scalar=-float(SLOTS),
                                            in1=L[:, 3, :], op0=ALU.mult, op1=ALU.add))
        corr = L[:, 5:5 + 8, :]
        for g in range(2):
            r = run[:, 8 * g:8 * g + 8, :]
            link(nc.vector.scalar_tensor_tensor(out=corr, in0=r, scalar=float(SLOTS),
                                                in1=L[:, 4:5, :].broadcast_to([P, 8, E]),
                                                op0=ALU.is_ge, op1=ALU.mult))
            link(nc.vector.tensor_tensor(r, r, corr, ALU.add))
        for g in range(4):
            link(nc.vector.tensor_tensor(
                prod[:, :, :].rearrange("p (t k) e -> p t k e", k=K),
                oh[:, 4 * g * K:4 * (g + 1) * K, :].rearrange("p (t k) e -> p t k e", k=K),
                run[:, 4 * g:4 * g + 4, :].rearrange("p t (a e) -> p t a e", a=1)
                .broadcast_to([P, 4, K, E]), ALU.mult))
            link(nc.vector.tensor_reduce(L[:, 13, 0:4 * K], prod[:, :, :], AX.X, ALU.add))
            link(nc.vector.scalar_tensor_tensor(
                out=posi[:, 4 * g * K:4 * (g + 1) * K].rearrange("p (t k) -> p t k", k=K),
                in0=XE[:, 4 * g:4 * g + 4, C_IDX:C_IDX + K], scalar=float(SLOTS),
                in1=L[:, 13, 0:4 * K].rearrange("p (t k) -> p t k", k=K), op0=ALU.mult, op1=ALU.add))
        ve.sem_inc(route_ok, 1)

        def shared_mul(t):
            ve.wait_ge(ssilu_ok, t + 1)
            if t >= 2:
                ve.wait_ge(a_full, USE[("sT", t - 2)] + 1)
            nc.vector.tensor_tensor(aS[:, t % 2, :], sgS[:, t % 2, :], PB[(T_B, OT_B)[t % 2][1]][:, 0:FS],
                                    ALU.mult).then_inc(sact_ok, 1)

        def shared_low(t):
            u = ("sT", t)
            ve.wait_ge(sat_hi, t + 1)
            low(aSTL[:, t % 2, :], bank_of(u)[0:FH, :], aSTH[:, t % 2, :]).then_inc(sat_ok, 1)
            ve.wait_ge(sat_ok, t + 1)
            ve.sem_inc(a_free, 1)

        def shared_add(t):
            u = ("sY", t)
            ve.wait_ge(a_full, USE[u] + 1)
            ve.wait_ge(xbo_ok, t + 1)
            nc.vector.tensor_tensor(base[:, t, :], bank_of(u)[:, 0:D], base[:, t, :], ALU.add)\
              .then_inc(a_free, 1)

        def maximum(n):
            b, h = divmod(n, H)
            ve.wait_ge(s_full, n + 1)
            if h == 0 and b >= 2:
                ve.wait_ge(m_ok, b - 1)
            nc.vector.tensor_reduce(mx[:, b % 2, :, h], PB[S_B[n % 2]][:, :]
                                    .rearrange("p (j n) -> p j n", j=2), AX.X, ALU.max, negate=True)\
              .then_inc(max_ok, 1)

        shared_mul(0)
        n = 0
        for t in range(TILES):
            if t + 1 < TILES:
                shared_mul(t + 1)
            shared_low(t)
            while n < min(LEAD, 3 * (t - 6)):
                maximum(n)
                n += 1
            shared_add(t)

        def neg_max(b):
            u = ("mT", b)
            ve.wait_ge(a_full, USE[u] + 1)
            if b >= 1:
                ve.wait_ge(m_w, 16 * b)
            nc.vector.tensor_copy(mTs[:, :], bank_of(u)[0:H, 0:SEQ]).then_inc(m_ok, 1)
            ve.wait_ge(m_ok, b + 1)
            ve.sem_inc(a_free, 1)

        def norm(g):
            b = g // 4
            ve.wait_ge(a_full, USE[("nt", g)] + 1)
            src = bank_of(("nt", g))[:, 0:SEQ].rearrange("p (j h d) -> p j h d", j=2, h=4)
            link(nc.vector.reciprocal(rden[:, g % 2, :, :], src[:, :, :, HD]))
            if g % 4 == 0 and b >= 2:
                ve.wait_ge(a_full, USE[("onT", b - 2)] + 1)
            nc.vector.tensor_tensor(
                On[:, b % 2, :, (g % 4) * 64:(g % 4 + 1) * 64].rearrange("p j (h d) -> p j h d", h=4),
                src[:, :, :, 0:HD],
                rden[:, g % 2, :, :].rearrange("p j (h a) -> p j h a", a=1).broadcast_to([P, 2, 4, HD]),
                ALU.mult).then_inc(norm_ok, 1)
            ve.wait_ge(norm_ok, g + 1)
            ve.sem_inc(a_free, 1)

        nc.vector.memset(raw32(KS[2][32:64, :, :]), 1.0)
        nc.vector.memset(raw32(KS[2][96:128, :, :]), 1.0).then_inc(ones2_ok, 1)
        neg_max(0)
        stage_low("q", 2)
        stage_low("k", 2)
        for n in range(SLOT_END):
            if n + LEAD < HEADS:
                maximum(n + LEAD)
            if nat(n):
                norm(nat(n)[1])
            u = extra(n)
            if u:
                kind, b = u
                if kind in "qk":
                    stage_low(kind, b)
                elif kind == "v":
                    values(b)
                elif kind == "mT":
                    neg_max(b)
                elif kind == "onT":
                    hi_n[0] += 1
                    ve.wait_ge(a_hi, hi_n[0])
                    low(OnTL[:, :, :], bank_of(u)[:, :].rearrange("p (c n) -> p c n", c=DC), OnTH[:, :, :])\
                        .then_inc(ont_ok, 1)
                    ve.wait_ge(ont_ok, b + 1)
                    ve.sem_inc(a_free, 1)
                else:
                    ve.wait_ge(a_full, USE[u] + 1)
                    bs = base[:, 2 * b:2 * b + 2, :]
                    nc.vector.tensor_tensor(bs, bank_of(u)[:, :].rearrange("p (j n) -> p j n", j=2), bs,
                                            ALU.add).then_inc(base_ok, 1)
                    ve.wait_ge(base_ok, b + 1)
                    ve.sem_inc(a_free, 1)

        def wait(s, v):
            if not (isinstance(v, int) and v <= 0):
                ve.wait_ge(s, v)

        def gate_low(i, c):
            wait(guH_ok, 4 * i + c + 1)
            o = (c % 4) * WN
            low(GL[c % 2][:, :], raw[:, o:o + GO], GH[c % 2][:, :]).then_inc(gu_split, 1)

        def mul(i, c, j):
            wait(silu_ok, 8 * i + 2 * c + j + 1)
            wait(at_full, 4 * i + c - 1)
            nc.vector.tensor_tensor(act[:, c % 2, j, :], sg[:, c % 2, j, :],
                                    PB[2 * (c % 2) + j][:, F:2 * F], ALU.mult).then_inc(mul_ok, 1)

        def act_low(i, c):
            wait(atH_ok, 4 * i + c + 1)
            low(aTL[c % 2][:, :, :], PB[A_B[1]][0:FH, :].rearrange("p (k n) -> p k n", k=2),
                aTH[c % 2][:, :, :]).then_inc(at_ok, 1)

        def rows_low(i, c):
            wait(xtH_ok, 4 * i + c + 1)
            low(xTL[c % 2][:, :, :], PB[A_B[0]][:, :].rearrange("p (k n) -> p k n", k=DC),
                xTH[c % 2][:, :, :]).then_inc(xt_ok, 1)

        def down_split(i, c):
            wait(w_in[c % 4], 32 * (i + c // 4) + 32)
            wait(dn_full, 4 * i + c - 1)
            o = (c % 4) * WN
            src = raw[0:FH, o + GO:o + WN]
            nc.vector.tensor_copy(DH[c % 2][:, :], src).then_inc(dh_ok, 1)
            wait(dh_ok, 4 * i + c + 1)
            low(DL[c % 2][:, :], src, DH[c % 2][:, :]).then_inc(wd_split, 1)

        def weights_of(i, c):
            s = c % 4
            wait(r_in[s], 16 * (i + c // 4) + 16)
            wait(y_free, 4 * i + c - 2)
            nc.vector.tensor_copy(ids[:, s, :], xin[:, s, :, C_TOK].bitcast(i32))
            nc.vector.tensor_scalar_add(ecur[:, s:s + 1], ecur[:, s:s + 1], 4.0).then_inc(w_step, 1)
            wait(w_step, 8 * i + 2 * c + 1)
            nc.vector.scalar_tensor_tensor(out=wtmp[:, :, :], in0=xin[:, s, :, C_IDX:C_IDX + K],
                                           scalar=ecur[:, s:s + 1], in1=xin[:, s, :, C_W:C_W + K],
                                           op0=ALU.is_equal, op1=ALU.mult).then_inc(w_step, 1)
            wait(w_step, 8 * i + 2 * c + 2)
            nc.vector.tensor_reduce(wcol[:, s, :], wtmp[:, :, :], AX.X, ALU.add).then_inc(wcol_ok, 1)

        def step(i, c, first=False, last=False):
            if not last:
                gate_low(i, c + 1)
            mul(i, c, 0)
            if not first:
                act_low(i, c - 1)
            if not last:
                rows_low(i, c + 1)
            mul(i, c, 1)
            down_split(i, c)
            if not last:
                weights_of(i, c + 1)

        gate_low(0, 0)
        rows_low(0, 0)
        weights_of(0, 0)
        for c in range(4):
            step(0, c, first=c == 0)
        with ve.Fori(1, E // 4 - 1, 1) as i:
            for c in range(4):
                step(i, c)
        for c in range(4):
            step(E // 4 - 1, c, last=c == 3)
        act_low(E // 4 - 1, 3)

        over = ve.value_load(nov_i[0:1, 0:1], min_val=0, max_val=OVT)
        with ve.If(over > 0):
            ve.wait_ge(y_free, E + 1)
            link(nc.vector.memset(ov_cmp[:, 0, 0:1], 0.0))
            for j in range(OVT):
                last = nc.vector.tensor_scalar(ov_cmp[:, j, :], ovc[:, OVC, :], float(j), None, ALU.is_le)
            link(last)
            link(nc.vector.tensor_reduce(ov_e[:, :], ov_cmp[:, :, :], AX.X, ALU.add))
            link(nc.vector.tensor_scalar_min(ov_e[:, :], ov_e[:, :], float(E - 1)))
            nc.vector.tensor_copy(ov_ei[:, :], ov_e[:, :]).then_inc(ov_e_ok, 1)
            ve.wait_ge(ov_e_ok, 1)
            with ve.Fori(0, OVT, 1) as j:
                ve.wait_ge(ov_xT_full, j + 1)
                nc.vector.tensor_copy(ov_xT[:, :, :], PB[0][:, 0:DC * P].rearrange("p (k n) -> p k n", k=DC))\
                  .then_inc(ov_xT_ok, 1)
                nc.vector.tensor_copy(ov_c[:, 0:1], ov_e[:, bass.ds(j, 1)]).then_inc(ov_s, 1)
                ve.wait_ge(ov_s, 3 * j + 1)
                nc.vector.scalar_tensor_tensor(out=wtmp[:, 0, :], in0=ov_x[:, C_IDX:C_IDX + K],
                                               scalar=ov_c[:, 0:1], in1=ov_x[:, C_W:C_W + K],
                                               op0=ALU.is_equal, op1=ALU.mult).then_inc(ov_s, 1)
                ve.wait_ge(ov_s, 3 * j + 2)
                nc.vector.tensor_reduce(ov_c[:, 1:2], wtmp[:, 0, :], AX.X, ALU.add).then_inc(ov_s, 1)
                nc.vector.tensor_copy(ov_id[:, 0:1], ov_x[:, C_TOK:C_TOK + 1].bitcast(i32))
                ve.wait_ge(ov_silu, j + 1)
                nc.vector.tensor_tensor(ov_a[:, 1, :], ov_a[:, 0, :], PB[1][:, F:2 * F], ALU.mult)\
                  .then_inc(ov_mul, 1)
                ve.wait_ge(ov_at, j + 1)
                nc.vector.tensor_copy(ov_aT[:, :, :], PB[2][0:FH, 0:2 * P].rearrange("p (k n) -> p k n", k=2))\
                  .then_inc(ov_at_ok, 1)
                ve.wait_ge(ov_dn, j + 1)
                ve.wait_ge(ov_s, 3 * j + 3)
                nc.vector.tensor_scalar(ov_y[:, :], PB[3][:, 0:D], ov_c[:, 1:2], None, ALU.mult)\
                  .then_inc(ov_y_ok, 1)
            ve.wait_ge(ov_dn, OVT)

    block_cm.__exit__(None, None, None)


def kernel(**inputs):
    import numpy as np
    import concourse.bacc as bacc
    from concourse.bass_utils import run_bass_kernel_spmd

    def rows(w, p=128):
        return np.ascontiguousarray(w.reshape(-1, p, w.shape[1]).transpose(1, 0, 2))

    a = {k[3:]: np.asarray(v) for k, v in inputs.items()}
    x = a["attn_x"].reshape(-1, a["attn_x"].shape[-1])
    D = x.shape[1]
    b = a["attn_b_qkv"]
    gu, dn = a["ffn_w_gate_up"], a["ffn_w_down"]
    E, F = gu.shape[0], dn.shape[2]
    arrays = {
        "x": np.ascontiguousarray(x),
        "gate": rows(a["ffn_gate_w"].T),
        "wqkv": rows(a["attn_w_qkv"].T),
        "bqk": np.ascontiguousarray(b[:2 * D].reshape(4, 128).T),
        "bvo": np.stack([b[2 * D:], a["attn_b_o"]]),
        "wo": rows(a["attn_w_o"].T),
        "wsgu": rows(a["ffn_ws_gate_up"].T),
        "wsd": rows(a["ffn_ws_down"].T, F // 2),
        "wgu": np.ascontiguousarray(gu.reshape(E, 2 * F, 2, 128).transpose(0, 3, 2, 1)).reshape(E, 128, 4 * F),
        "wd": np.ascontiguousarray(dn.reshape(E, D, 2, F // 2).transpose(0, 3, 2, 1)).reshape(E, F // 2, 2 * D),
    }
    nc = bacc.Bacc("TRN2", target_bir_lowering=False, num_devices=1)
    ts = [nc.dram_tensor(k, v.shape, mybir.dt.from_np(v.dtype), kind="ExternalInput").ap()
          for k, v in arrays.items()]
    out = nc.dram_tensor("out", (x.shape[0] + 256, D), mybir.dt.float32, kind="ExternalOutput").ap()
    block_kernel(nc, *ts, out)
    r = run_bass_kernel_spmd(nc, [arrays], core_ids=[0])
    return r.results[0]["out"][:x.shape[0]].reshape(a["attn_x"].shape)
```

```python
import concourse.bass as bass
from concourse import mybir


def block_kernel(nc, x, gate, wqkv, bqk, bvo, wo, wsgu, wsd, wgu, wd, out):
    f32, f32r, bf16, i32, u32 = (mybir.dt.float32, mybir.dt.float32r, mybir.dt.bfloat16,
                                 mybir.dt.int32, mybir.dt.uint32)
    ALU = mybir.AluOpType
    ACT = mybir.ActivationFunctionType
    AX = mybir.AxisListType

    P = 128
    TOK, D = x.shape
    TILES = TOK // P
    B = 8
    SEQ = TOK // B
    H, HD = 16, 16
    DC = D // P
    E = gate.shape[2]
    K = 6
    F = 176
    FH = F // 2
    FS = 2 * F
    SC = FS // FH
    SCALE = float(HD) ** -0.5
    LN_EPS, TOPK_EPS = 1e-5, 1e-20
    SLOTS = 2 * P
    REG = E * SLOTS
    OVT = (TOK * K) // P
    ROW = 272
    C_IDX, C_W, C_TOK = D, D + K, D + 2 * K
    GN, GO = 2 * F, DC * 2 * F
    WN = GO + 2 * D
    LEAD = 24
    HEADS = B * H
    RANK_STEP, LEAD_FROM = 5, TILES - LEAD // 3

    xs_d = nc.dram_tensor("slot_rows", [REG + OVT * P, ROW], f32, kind="Internal").ap()
    qk_d = nc.dram_tensor("qk_parts", [B, 4, 2 * P, SEQ], f32, kind="Internal").ap()
    m_d = nc.dram_tensor("neg_max", [B, H, SEQ], f32, kind="Internal").ap()

    place = [(nc.sbuf_base + 63) // 64 * 64]

    def sb(name, shape, dt, at=None):
        n = 2 if dt == bf16 else 4
        for s in shape[1:]:
            n *= s
        where = place[0] if at is None else at[0]
        t = nc.alloc_sbuf_tensor_at(name, shape, dt, offset=where, align_bytes=32)
        if at is None:
            place[0] += (n + 31) // 32 * 32
            assert place[0] <= nc.sbuf_usable_end, (name, place[0])
        else:
            at[0] += (n + 31) // 32 * 32
            assert at[0] <= at[1], (name, at)
        return t

    def region(nbytes):
        start = place[0]
        place[0] += nbytes
        assert place[0] <= nc.sbuf_usable_end, place[0]
        return start, nbytes

    def within(r, skip=0):
        return [r[0] + skip, r[0] + r[1]]

    ident = sb("ident", [P, P], f32)
    before = sb("before", [P, P], bf16)
    ones = sb("ones", [P, P], bf16)
    iota_e = sb("iota_e", [P, E], f32)
    ecur = sb("ecur", [P, 4], f32)
    bq = sb("bq", [P, 4], f32)
    bv = sb("bv", [P, D], f32)
    mv = sb("mv", [P, TILES, 2], f32)
    st6 = sb("st6", [P, TILES, 6], f32)
    rstd = sb("rstd", [P, TILES, 3], f32)
    posi = sb("posi", [P, TILES * K], i32)
    nov_i = sb("nov_i", [P, 2], i32)
    mx = sb("mx", [P, 2, 2, H], f32)
    mTs = sb("mTs", [H, SEQ], f32r)
    rden = sb("rden", [P, 2, 2, 4], f32)
    wcol = sb("wcol", [P, 4, 2], f32)
    wtmp = sb("wtmp", [P, 2, K], f32)
    ids = sb("ids", [P, 4, 2], i32)
    masksum = sb("masksum", [P, E], bf16)
    ovc = sb("ovc", [P, 2, E], f32)

    base = sb("base", [P, TILES, D], f32)
    r_xe = region(TILES * ROW * 4)
    XE = sb("XE", [P, TILES, ROW], f32, within(r_xe))
    r_xt = region(2 * DC * TOK * 4)
    a = within(r_xt)
    XH = sb("XH", [P, DC, TOK], f32r, a)
    XL = sb("XL", [P, DC, TOK], f32r, a)
    r_raw = region(4 * WN * 4)
    raw = sb("raw", [P, 4 * WN], f32, within(r_raw))
    O_GATE, O_QKV = 0, DC * E
    O_WO = O_QKV + DC * 3 * D
    O_SGU = O_WO + DC * D
    O_SD = O_SGU + DC * 2 * FS
    NST = O_SD + SC * D
    WSH = sb("WSH", [P, NST], f32r)
    WSL = sb("WSL", [P, NST], f32r)
    a = within(r_raw)
    L = sb("L", [P, TILES, E], f32, a)
    mask = sb("mask", [P, TILES, E], bf16, a)
    run = sb("run", [P, TILES, E], f32, a)
    idx8 = sb("idx8", [P, TILES, 8], u32, a)
    prod = sb("prod", [P, 2, 2 * K, E], f32, a)
    top8 = sb("top8", [P, TILES, 8], f32, a)
    r_qk = region(3 * 2 * 8 * SEQ * 4)
    a = within(r_qk)
    QS, KS = [], []
    for s in range(3):
        QS.append(sb(f"QS{s}", [P, 8, SEQ], f32r, a))
        KS.append(sb(f"KS{s}", [P, 8, SEQ], f32r, a))
    LT = sb("LT", [E, TOK], f32, within(r_qk, 2 * 8 * SEQ * 4))
    a = within(r_qk, 2 * 2 * 8 * SEQ * 4)
    sgS = sb("sgS", [P, 2, FS], f32, a)
    aS = sb("aS", [P, 2, FS], f32, a)
    aSTH = sb("aSTH", [FH, 2, SC * P], f32r, a)
    aSTL = sb("aSTL", [FH, 2, SC * P], f32r, a)
    V = sb("V", [P, 2, 2, H, 32], f32)
    stg = [sb(n, [P, 2, SEQ], f32r) for n in ("qhi", "qlo", "khi", "klo")]
    r_at = region(16384)
    a = within(r_at)
    EX = sb("EX", [P, 3, 2 * SEQ], f32, a)
    OTs = sb("OTs", [P, 2, SEQ], f32, a)
    On = sb("On", [P, 2, 2, D], f32, a)
    OnTH = sb("OnTH", [P, DC, SEQ], f32r, a)
    OnTL = sb("OnTL", [P, DC, SEQ], f32r, a)
    a = within(r_at)
    oh = sb("oh", [P, TILES * K, E], bf16, a)
    fill = sb("fill", [P, 2, ROW], f32, a)
    bo = sb("bo", [P, D], f32, a)
    a = within(r_xt)
    GH = [sb(f"GH{s}", [P, GO], f32r, a) for s in range(2)]
    GL = [sb(f"GL{s}", [P, GO], f32r, a) for s in range(2)]
    DH = [sb(f"DH{s}", [FH, 2 * D], f32r, a) for s in range(2)]
    DL = [sb(f"DL{s}", [FH, 2 * D], f32r, a) for s in range(2)]
    a = within(r_xe)
    xin = sb("xin", [P, 4, 2, ROW], f32, a)
    xTH = [sb(f"xTH{s}", [P, DC, SLOTS], f32r, a) for s in range(2)]
    xTL = [sb(f"xTL{s}", [P, DC, SLOTS], f32r, a) for s in range(2)]
    a = within(r_qk)
    sg = sb("sg", [P, 2, 2, F], f32, a)
    act = sb("act", [P, 2, 2, F], f32, a)
    aTH = [sb(f"aTH{s}", [FH, 2, SLOTS], f32r, a) for s in range(2)]
    aTL = [sb(f"aTL{s}", [FH, 2, SLOTS], f32r, a) for s in range(2)]
    y = sb("y", [P, 4, 2, D], f32, a)
    ov_x = sb("ov_x", [P, ROW], f32, a)
    ov_xT = sb("ov_xT", [P, DC, P], f32, a)
    ov_a = sb("ov_a", [P, 2, F], f32, a)
    ov_aT = sb("ov_aT", [FH, 2, P], f32, a)
    ov_y = sb("ov_y", [P, D], f32, a)
    ov_c = sb("ov_c", [P, 4], f32, a)
    ov_id = sb("ov_id", [P, 2], i32, a)
    ov_cmp = sb("ov_cmp", [P, OVT, E], f32, within(r_xt))
    ov_e = sb("ov_e", [P, OVT], f32, within(r_xe))
    ov_ei = sb("ov_ei", [P, OVT], i32, within(r_xe, OVT * 4 + 32))

    PB = [nc.alloc_psum_tensor(f"bank{i}", [P, 512], f32) for i in range(8)]
    S_B, T_B, OT_B, A_B = (0, 1), (2, 3), (4, 7), (5, 6)
    RT_B = S_B + OT_B
    GT = TILES // 4

    def sem(name):
        return nc.alloc_semaphore(name)

    x_in = [sem(f"x_in{g}") for g in range(4)]
    ones2_ok = sem("ones2_ok")
    wq_in, w_in0, b_in = sem("wqkv_in"), sem("weights_in"), sem("bias_in")
    const_ok = sem("const_ok")
    var_ok, sqrt_ok, xn_ok = sem("var_ok"), sem("sqrt_ok"), sem("xn_ok")
    chain = sem("vector_chain")
    pchain = sem("pool_chain")
    achain = sem("scalar_chain")
    wsh_ok, wsl_ok, wsl2_ok = sem("static_hi_ok"), sem("qkv_lo_ok"), sem("other_lo_ok")
    lt_full, lt_ok = sem("logitsT_full"), sem("logitsT_ok")
    run_ok, prod_ok, prod_free = sem("ranks_ok"), sem("rank_product_ok"), sem("rank_product_used")
    rank_read = sem("rank_base_read")
    a_full, a_hi, a_free = sem("a_full"), sem("a_hi"), sem("a_free")
    lg_full, lg_ok, dlt_ok, ex_ok = sem("logits_full"), sem("logits_ok"), sem("delta_ok"), sem("exp_ok")
    sum_ok, base_full = sem("masksum_ok"), sem("rank_base_full")
    route_ok, fill_in, fill_free = sem("route_ok"), sem("fill_in"), sem("fill_free")
    xbo_ok = sem("x_plus_bo_ok")
    sgu_full, ssilu_ok, sact_ok = sem("shared_gu_full"), sem("shared_silu_ok"), sem("shared_act_ok")
    sat_hi, sat_ok = sem("shared_actT_hi"), sem("shared_actT_ok")
    stg_q, stg_k, qk_w = sem("q_staged"), sem("k_staged"), sem("qk_written")
    qk_in = [sem(f"qk_in{s}") for s in range(3)]
    m_in = [sem(f"m_in{s}") for s in range(3)]
    s_full, max_ok, st_full, exp_ok = sem("s_full"), sem("max_ok"), sem("st_full"), sem("prob_ok")
    pv_ok, ot_ok, norm_ok = sem("pv_ok"), sem("ot_ok"), sem("norm_ok")
    v_ok, m_ok, m_w = sem("v_ok"), sem("m_ok"), sem("m_written")
    ont_ok, base_ok, out_w = sem("onT_ok"), sem("base_ok"), sem("out_written")
    scat_in = sem("rows_scattered")
    w_in = [sem(f"w_in{s}") for s in range(4)]
    r_in = [sem(f"rows_in{s}") for s in range(4)]
    guH_ok, gu_split, wd_split = sem("guH_ok"), sem("gu_split"), sem("wd_split")
    xt_full, xtH_ok, xt_ok = sem("xt_full"), sem("xtH_ok"), sem("xt_ok")
    gu_full, silu_ok, mul_ok = sem("gu_full"), sem("silu_ok"), sem("mul_ok")
    at_full, atH_ok, at_ok = sem("at_full"), sem("atH_ok"), sem("at_ok")
    dn_full, y_ok, scat, y_free = sem("dn_full"), sem("y_ok"), sem("added"), sem("y_free")
    wcol_ok, w_step, dh_ok = sem("wcol_ok"), sem("wcol_step"), sem("down_hi_ok")
    ov_e_ok, ov_in, ov_xT_full, ov_xT_ok = sem("ov_e_ok"), sem("ov_in"), sem("ov_xT_full"), sem("ov_xT_ok")
    ov_gu, ov_silu, ov_mul, ov_at = sem("ov_gu"), sem("ov_silu"), sem("ov_mul"), sem("ov_at")
    ov_s = sem("ov_step")
    ov_at_ok, ov_dn, ov_y_ok, ov_add, ov_w = (sem("ov_at_ok"), sem("ov_dn"), sem("ov_y_ok"),
                                              sem("ov_add"), sem("ov_w"))

    def extra(n):
        b, s = divmod(n, H)
        if s == 1 and b + 3 < B:
            return ("q", b + 3)
        if s == 3 and b + 3 < B:
            return ("k", b + 3)
        if s == 5 and 1 <= b <= B:
            return ("onT", b - 1)
        if s == 8 and 1 <= b <= B:
            return ("o", b - 1)
        if s == 9 and b + 1 < B:
            return ("mT", b + 1)
        if s == 11 and b + 1 < B:
            return ("v", b + 1)
        return None

    def nat(n):
        g = n // 4 - 2
        return ("nt", g) if n % 4 == 0 and 0 <= g < HEADS // 4 else None

    SLOT_END = HEADS + 9
    uses = [("xt", i) for i in range(TILES // 2)]
    uses += [(c, b) for b in range(2) for c in "qk"] + [("v", 0)]
    for t in range(TILES):
        uses += [("sT", t)] + ([("sY", t - 1)] if t else [])
    uses += [("sY", TILES - 1), ("mT", 0), ("q", 2), ("k", 2)]
    for n in range(SLOT_END):
        uses += [u for u in (nat(n), extra(n)) if u]
    USE = {u: i for i, u in enumerate(uses)}

    def bank_of(u):
        return PB[A_B[USE[u] % 2]]

    def static(w, off, c, width, lo, n):
        s = off + c * width + lo
        return w[:, s:s + n]

    def raw32(ap):
        return ap.bitcast(f32)

    IDENT_OK, FILL_OK, CONSTS = 1, 2, 3
    x_v = x.rearrange("(t p) c -> p t c", p=P)
    out_v = out[0:TOK, :].rearrange("(t p) c -> p t c", p=P)
    SPARE = out.shape[0] - TOK
    assert SPARE == SLOTS

    def load_w(sp, c, i, e):
        if e is None:
            sp.wait_ge(gu_split, 4 * i + (c - 3))
            sp.wait_ge(wd_split, 4 * i + (c - 3))
        elif e == 0:
            sp.wait_ge(route_ok, 1)
        o = c * WN
        if e is None:
            sg_, sd_ = wgu[bass.ds(4 * i + c, 1), :, :], wd[bass.ds(4 * i + c, 1), :, :]
        else:
            sg_, sd_ = wgu[e:e + 1, :, :], wd[e:e + 1, :, :]
        sp.dma_start(raw[:, o:o + GO], sg_.rearrange("a p n -> (a p) n")).then_inc(w_in[c], 16)
        sp.dma_start(raw[0:FH, o + GO:o + WN], sd_.rearrange("a p n -> (a p) n")).then_inc(w_in[c], 16)

    def load_rows(sp, c, i, e):
        if e is None:
            sp.wait_ge(xt_full, 4 * i + (c - 3))
            sp.wait_ge(wcol_ok, 4 * i + (c - 3))
            src = xs_d[bass.ds((4 * i + c) * SLOTS, SLOTS), :]
        else:
            if e == 0:
                sp.wait_ge(scat_in, 16 * TILES * K)
            src = xs_d[e * SLOTS:(e + 1) * SLOTS, :]
        sp.dma_start(xin[:, c, :, :], src.rearrange("(j p) n -> p j n", p=P)).then_inc(r_in[c], 16)

    block_cm = nc.Block()
    block = block_cm.__enter__()

    @block.sync
    def _(sp):
        sp.dma_start(base[:, 0:4, :], x_v[:, 0:4, :]).then_inc(x_in[0], 16)
        sp.dma_start(raw[:, O_GATE:O_QKV].rearrange("p (c n) -> p c n", c=DC), gate).then_inc(wq_in, 16)
        sp.dma_start(raw[:, O_QKV:O_WO].rearrange("p (c n) -> p c n", c=DC), wqkv).then_inc(wq_in, 16)
        for g in range(1, 4):
            sp.dma_start(base[:, 4 * g:4 * g + 4, :], x_v[:, 4 * g:4 * g + 4, :]).then_inc(x_in[g], 16)
        sp.dma_start(bq[:, :], bqk).then_inc(b_in, 16)
        sp.dma_start(bv[:, :], bvo[0:1, :].broadcast_to([P, D])).then_inc(b_in, 16)
        sp.dma_start(bo[:, :], bvo[1:2, :].broadcast_to([P, D])).then_inc(b_in, 16)
        sp.dma_start(raw[:, O_WO:O_SGU].rearrange("p (c n) -> p c n", c=DC), wo).then_inc(w_in0, 16)
        sp.dma_start(raw[:, O_SGU:O_SD].rearrange("p (c n) -> p c n", c=DC), wsgu).then_inc(w_in0, 16)
        sp.dma_start(raw[0:FH, O_SD:NST].rearrange("p (c n) -> p c n", c=SC), wsd).then_inc(w_in0, 16)

        FILLS = 16
        per = E // FILLS
        xs_v = xs_d[0:REG, :].rearrange("(e j p) c -> p e j c", j=2, p=P)

        def fill_part(i):
            for e in range(per * i, per * i + per):
                sp.dma_start(xs_v[:, e, :, :], fill[:, :, :]).then_inc(fill_in, 16)

        def qk_write(b):
            for w, (s0, ready) in enumerate(((0, stg_q), (2, stg_k))):
                sp.wait_ge(ready, b + 1)
                for s in (s0, s0 + 1):
                    sp.dma_start(qk_d[b, s].rearrange("(k p) q -> p k q", p=P), raw32(stg[s][:, :, :]))\
                      .then_inc(qk_w, 16)

        def qk_read(b):
            s = b % 3
            sp.wait_ge(qk_w, 64 * (b + 1))
            if b == 0:
                sp.wait_ge(const_ok, CONSTS)
            if b == 2:
                sp.wait_ge(ones2_ok, 1)
            if b >= 3:
                sp.wait_ge(st_full, H * (b - 2))
            for par in range(2):
                for dst, parts in ((QS[s], (0, 1, 0)), (KS[s], (2, 2, 3))):
                    for r, part in enumerate(parts):
                        src = qk_d[b, part].rearrange("(k r d) q -> r d k q", r=2, d=HD)[par]
                        lo = 64 * par + HD * r
                        sp.dma_start(raw32(dst[lo:lo + HD, :, :]), src).then_inc(qk_in[s], 16)

        def m_move(b):
            sp.wait_ge(m_ok, b + 1)
            sp.dma_start(m_d[b], raw32(mTs[:, :])).then_inc(m_w, 16)
            sp.wait_ge(m_w, 16 * (b + 1))
            for par in range(2):
                src = m_d[b].rearrange("(k r) q -> r k q", r=2)[par:par + 1]
                lo = 64 * par + 3 * HD
                sp.dma_start(raw32(QS[b % 3][lo:lo + 1, :, :]), src).then_inc(m_in[b % 3], 16)

        sp.wait_ge(const_ok, FILL_OK)
        sp.dma_start(out[TOK:TOK + SPARE, :].rearrange("(j p) c -> p j c", p=P), fill[:, :, 0:D])\
          .then_inc(out_w, 16)
        for i in range(2):
            fill_part(i)
        for b in range(2):
            qk_write(b)
            qk_read(b)
            for i in range(2 + 7 * b, 9 + 7 * b):
                fill_part(i)
        m_move(0)
        qk_write(2)
        qk_read(2)
        for b in range(B + 1):
            if b + 3 < B:
                qk_write(b + 3)
            if b >= 1:
                sp.wait_ge(base_ok, b)
                sp.dma_start(out_v[:, 2 * b - 2:2 * b, :], base[:, 2 * b - 2:2 * b, :]).then_inc(out_w, 16)
            if b + 1 < B:
                m_move(b + 1)
            if b + 3 < B:
                qk_read(b + 3)
            if b == 1:
                for e in range(4):
                    load_w(sp, e, 0, e)
        for e in range(4):
            load_rows(sp, e, 0, e)
        with sp.Fori(1, E // 4, 1) as i:
            for c in range(4):
                load_w(sp, c, i, None)
                load_rows(sp, c, i, None)
        sp.wait_ge(out_w, 16 * (B + 1))
        sp.wait_ge(y_free, E + 1)
        over = sp.value_load(nov_i[0:1, 0:1], min_val=0, max_val=OVT)
        with sp.If(over > 0):
            sp.wait_ge(ov_e_ok, 1)
            with sp.Fori(0, OVT, 1) as j:
                with sp.If(over > j):
                    e = sp.value_load(ov_ei[0:1, bass.ds(j, 1)], min_val=0, max_val=E - 1)
                    sp.wait_ge(ov_w, j + 1)
                    sp.dma_start(raw[:, 0:GO], wgu[bass.ds(e, 1), :, :].rearrange("a p n -> (a p) n"))\
                      .then_inc(ov_in, 16)
                    sp.dma_start(raw[0:FH, GO:WN], wd[bass.ds(e, 1), :, :].rearrange("a p n -> (a p) n"))\
                      .then_inc(ov_in, 16)
                    sp.dma_start(ov_x[:, :], xs_d[bass.ds(j * P + REG, P), :]).then_inc(ov_in, 16)
            sp.wait_ge(ov_w, OVT + 1)
        sp.wait_ge(out_w, 16 * (B + 1))

    @block.gpsimd
    def _(pool):
        n = [0]

        def link(ins):
            n[0] += 1
            ins.then_inc(pchain, 1)
            pool.wait_ge(pchain, n[0])

        link(pool.memset(ident[:, :], 0.0))
        pool.affine_select(out=ident[:, :], in_=ident[:, :], compare_op=ALU.not_equal, fill=1.0,
                           base=0, pattern=[[-1, P]], channel_multiplier=1).then_inc(const_ok, 1)
        link(pool.memset(fill[:, :, :], 0.0))
        pool.iota(fill[:, :, C_TOK:C_TOK + 1].bitcast(i32), pattern=[[P, 2], [0, 1]], base=TOK,
                  channel_multiplier=1).then_inc(const_ok, 1)
        link(pool.memset(ones[:, :], 1.0))
        link(pool.affine_select(out=before[:, :], in_=ones[:, :], compare_op=ALU.is_gt, fill=0.0,
                                base=0, pattern=[[1, P]], channel_multiplier=-1))
        link(pool.iota(iota_e[:, :], pattern=[[1, E]], base=0, channel_multiplier=0,
                       allow_small_or_imprecise_dtypes=True))
        link(pool.iota(ecur[:, :], pattern=[[1, 4]], base=-4, channel_multiplier=0,
                       allow_small_or_imprecise_dtypes=True))
        link(pool.memset(XE[:, :, C_TOK + 1:ROW], 0.0))
        link(pool.iota(XE[:, :, C_TOK:C_TOK + 1].bitcast(i32), pattern=[[P, TILES], [0, 1]], base=0,
                       channel_multiplier=1))
        link(pool.memset(V[:, :, :, :, HD:32], 0.0))
        link(pool.memset(V[:, :, :, :, HD:HD + 1], 1.0))
        for s in range(2):
            for lo in (32, 96):
                last = pool.memset(raw32(KS[s][lo:lo + 32, :, :]), 1.0)
        last.then_inc(const_ok, 1)

        pool.wait_ge(wsh_ok, 2)
        pool.wait_ge(const_ok, CONSTS)
        link(pool.tensor_tensor(WSL[:, O_WO:O_SD], raw[:, O_WO:O_SD], raw32(WSH[:, O_WO:O_SD]),
                                ALU.subtract))
        pool.tensor_tensor(WSL[0:FH, O_SD:NST], raw[0:FH, O_SD:NST], raw32(WSH[0:FH, O_SD:NST]),
                           ALU.subtract).then_inc(wsl2_ok, 1)
        pool.wait_ge(wsl2_ok, 1)

        pool.wait_ge(b_in, 48)
        pool.wait_ge(xn_ok, TILES)
        for t in range(TILES):
            pool.tensor_tensor(base[:, t, :], base[:, t, :], bo[:, :], ALU.add).then_inc(xbo_ok, 1)

        pool.wait_ge(run_ok, 1)
        for g in range(TILES // 2):
            if g >= 2:
                pool.wait_ge(prod_free, g - 1)
            pool.tensor_tensor(
                prod[:, g % 2, :, :].rearrange("p (t k) e -> p t k e", k=K),
                oh[:, 2 * g * K:2 * (g + 1) * K, :].rearrange("p (t k) e -> p t k e", k=K),
                run[:, 2 * g:2 * g + 2, :].rearrange("p t (a e) -> p t a e", a=1)
                .broadcast_to([P, 2, K, E]), ALU.mult).then_inc(prod_ok, 1)

        pool.wait_ge(route_ok, 1)
        over = pool.value_load(nov_i[0:1, 0:1], min_val=0, max_val=OVT)
        with pool.If(over > 0):
            xo_v = xs_d[REG:REG + OVT * P, :].rearrange("(j p) c -> p j c", p=P)
            with pool.Fori(0, OVT, 1) as j:
                pool.dma_start(xo_v[:, bass.ds(j, 1), :], fill[:, 0:1, :]).then_inc(ov_add, 16)
            pool.wait_ge(ov_add, 16 * OVT)
        pool.sem_inc(fill_free, 1)
        pool.wait_ge(fill_in, 16 * E)
        for t in range(TILES):
            for k in range(K):
                i = t * K + k
                pool.indirect_dma_start(xs_d, bass.IndirectOffsetOnAxis(ap=posi[:, i:i + 1], axis=0),
                                        XE[:, t, :], None).then_inc(scat_in, 16)

        pool.sem_inc(y_free, 1)

        def add(i, c, first=False, second=False):
            pool.wait_ge(y_ok, 8 * i + (2 * c + 2))
            if first:
                pool.wait_ge(out_w, 16 * (B + 1))
            else:
                pool.wait_ge(scat, 128 * i + 32 * c)
                pool.sem_inc(y_free, 1)
            for j in range(2):
                pool.indirect_dma_start(out, bass.IndirectOffsetOnAxis(ap=ids[:, c, j:j + 1], axis=0),
                                        y[:, c, j, :], None, compute_op=ALU.add).then_inc(scat, 16)

        for c in range(4):
            add(0, c, first=c == 0)
        with pool.Fori(1, E // 4, 1) as i:
            for c in range(4):
                add(i, c)
        pool.wait_ge(scat, 32 * E)
        pool.sem_inc(y_free, 1)
        over = pool.value_load(nov_i[0:1, 0:1], min_val=0, max_val=OVT)
        with pool.If(over > 0):
            pool.sem_inc(ov_w, 1)
            with pool.Fori(0, OVT, 1) as j:
                with pool.If(over > j):
                    pool.wait_ge(ov_y_ok, j + 1)
                    pool.sem_inc(pchain, 1)
                    pool.indirect_dma_start(out, bass.IndirectOffsetOnAxis(ap=ov_id[:, 0:1], axis=0),
                                            ov_y[:, :], None, compute_op=ALU.add).then_inc(ov_add, 16)
                    pool.wait_ge(ov_add, 16 * j + 16 * (OVT + 1))
                pool.sem_inc(ov_w, 1)
            pool.wait_ge(ov_w, OVT + 1)
        pool.wait_ge(scat, 32 * E)

    @block.tensor
    def _(pe):
        def product(dst, lh, ll, rh, rl, first=True, last=True):
            pe.matmul(dst, lhsT=lh, rhs=rh, start=first, stop=False)
            pe.matmul(dst, lhsT=lh, rhs=rl, start=False, stop=False)
            return pe.matmul(dst, lhsT=ll, rhs=rh, start=False, stop=last)

        def claim(u):
            if USE[u] >= 2:
                pe.wait_ge(a_free, USE[u] - 1)
            return bank_of(u)

        def xt_tiles(i):
            pe.wait_ge(xn_ok, 2 * i + 2)
            bk = claim(("xt", i))
            for c in range(DC):
                for j in range(2):
                    last = pe.transpose(bk[:, (2 * c + j) * P:(2 * c + j + 1) * P],
                                        in_=XE[:, 2 * i + j, c * P:(c + 1) * P], identity=ident[:, :])
            last.then_inc(a_full, 1)

        def project(which, b):
            u = (which, b)
            bk = claim(u)
            col = 0 if which == "q" else D
            for k in range(2):
                for c in range(DC):
                    last = product(bk[:, k * SEQ:(k + 1) * SEQ],
                                   static(WSH, O_QKV, c, 3 * D, col + k * P, P),
                                   static(WSL, O_QKV, c, 3 * D, col + k * P, P),
                                   XH[:, c, b * SEQ:(b + 1) * SEQ], XL[:, c, b * SEQ:(b + 1) * SEQ],
                                   c == 0, c == DC - 1)
            last.then_inc(a_full, 1)

        def values(b):
            bk = claim(("v", b))
            for j in range(2):
                for c in range(DC):
                    t = slice((2 * b + j) * P, (2 * b + j + 1) * P)
                    last = product(bk[:, j * D:(j + 1) * D], XH[:, c, t], XL[:, c, t],
                                   static(WSH, O_QKV, c, 3 * D, 2 * D, D),
                                   static(WSL, O_QKV, c, 3 * D, 2 * D, D), c == 0, c == DC - 1)
            last.then_inc(a_full, 1)

        def scores(n):
            b, h = divmod(n, H)
            k, lo = h // 2, 64 * (h % 2)
            if h == 0:
                pe.wait_ge(qk_in[b % 3], 192 * (b // 3 + 1))
            if n == 0:
                pe.wait_ge(rank_read, 1)
            if n >= 2:
                pe.wait_ge(max_ok, n - 1)
            for j in range(2):
                last = pe.matmul(PB[S_B[n % 2]][:, j * SEQ:(j + 1) * SEQ],
                                 lhsT=QS[b % 3][lo:lo + 3 * HD, k, j * P:(j + 1) * P],
                                 rhs=KS[b % 3][lo:lo + 3 * HD, k, :], start=True, stop=True)
            last.then_inc(s_full, 1)

        def scores_t(n):
            b, h = divmod(n, H)
            k, lo = h // 2, 64 * (h % 2)
            if h == 0:
                pe.wait_ge(m_in[b % 3], 32 * (b // 3 + 1))
            if n == 0:
                pe.wait_ge(sact_ok, TILES)
            if n >= 2:
                pe.wait_ge(exp_ok, n - 1)
            for j in range(2):
                last = pe.matmul(PB[T_B[n % 2]][:, j * SEQ:(j + 1) * SEQ],
                                 lhsT=KS[b % 3][lo:lo + 3 * HD + 1, k, j * P:(j + 1) * P],
                                 rhs=QS[b % 3][lo:lo + 3 * HD + 1, k, :], start=True, stop=True)
            last.then_inc(st_full, 1)

        def weigh(n):
            b, h = divmod(n, H)
            g = n // 4
            pe.wait_ge(exp_ok, n + 1)
            if h == 0:
                pe.wait_ge(v_ok, b + 1)
            if n % 4 == 0 and g >= 2:
                pe.wait_ge(ot_ok, g - 1)
            lo = 32 * (n % 4)
            for j in range(2):
                last = pe.matmul(PB[OT_B[g % 2]][lo:lo + 32, 0:SEQ],
                                 lhsT=V[:, b % 2, j, h, :], rhs=EX[:, n % 3, j * SEQ:(j + 1) * SEQ],
                                 start=j == 0, stop=j == 1)
            last.then_inc(pv_ok, 1)

        def natural(g):
            pe.wait_ge(ot_ok, g + 1)
            bk = claim(("nt", g))
            for j in range(2):
                last = pe.transpose(bk[:, j * P:(j + 1) * P], in_=OTs[:, g % 2, j * P:(j + 1) * P],
                                    identity=ident[:, :])
            last.then_inc(a_full, 1)

        def neg_max_t(b):
            pe.wait_ge(max_ok, H * (b + 1))
            bk = claim(("mT", b))
            for j in range(2):
                last = pe.transpose(bk[0:H, j * P:(j + 1) * P], in_=mx[:, b % 2, j, :],
                                    identity=ident[:, :])
            last.then_inc(a_full, 1)

        def out_t(b):
            pe.wait_ge(norm_ok, 4 * b + 4)
            bk = claim(("onT", b))
            for c in range(DC):
                for j in range(2):
                    last = pe.transpose(bk[:, (2 * c + j) * P:(2 * c + j + 1) * P],
                                        in_=On[:, b % 2, j, c * P:(c + 1) * P], identity=ident[:, :])
            last.then_inc(a_full, 1)

        def out_proj(b):
            pe.wait_ge(ont_ok, b + 1)
            bk = claim(("o", b))
            for j in range(2):
                for c in range(DC):
                    last = product(bk[:, j * D:(j + 1) * D], OnTH[:, c, j * P:(j + 1) * P],
                                   OnTL[:, c, j * P:(j + 1) * P], static(WSH, O_WO, c, D, 0, D),
                                   static(WSL, O_WO, c, D, 0, D), c == 0, c == DC - 1)
            last.then_inc(a_full, 1)

        def router(g):
            pe.wait_ge(a_free, 2 * g + 2)
            tt = slice(g * GT * P, (g + 1) * GT * P)
            for c in range(DC):
                last = product(PB[RT_B[g]][0:E, :], static(WSH, O_GATE, c, E, 0, E),
                               static(WSL, O_GATE, c, E, 0, E), XH[:, c, tt], XL[:, c, tt],
                               c == 0, c == DC - 1)
            last.then_inc(lt_full, 1)

        def logits(g):
            pe.wait_ge(lt_ok, g + 1)
            for t in range(GT * g, GT * g + GT):
                last = pe.transpose(PB[T_B[t // 8]][:, (t % 8) * E:(t % 8 + 1) * E],
                                    in_=LT[:, t * P:(t + 1) * P], identity=ident[0:E, 0:E])
            if g % 2:
                last.then_inc(lg_full, 1)

        def rank_base():
            pe.wait_ge(sum_ok, 1)
            pe.matmul(PB[S_B[0]][:, 0:E], lhsT=before[:, :], rhs=masksum[:, :], start=True, stop=True)
            pe.matmul(PB[S_B[0]][:, E:2 * E], lhsT=ones[:, :], rhs=masksum[:, :], start=True, stop=True)\
              .then_inc(base_full, 1)

        pe.wait_ge(const_ok, IDENT_OK)
        for i in range(4):
            xt_tiles(i)
        pe.wait_ge(wsl_ok, 1)
        router(0)
        xt_tiles(4)
        xt_tiles(5)
        router(1)
        logits(0)
        xt_tiles(6)
        xt_tiles(7)
        router(2)
        logits(1)
        router(3)
        project("q", 0)
        logits(2)
        logits(3)
        project("k", 0)
        project("q", 1)
        project("k", 1)
        values(0)

        pe.wait_ge(wsl2_ok, 1)
        pe.wait_ge(lg_ok, 2)

        def shared_up(t, half):
            if t >= 2:
                pe.wait_ge(sact_ok, t - 1)
            bk = PB[(T_B, OT_B)[t % 2][half]]
            for c in range(DC):
                tt = slice(t * P, (t + 1) * P)
                last = product(bk[:, 0:FS], XH[:, c, tt], XL[:, c, tt],
                               static(WSH, O_SGU, c, 2 * FS, half * FS, FS),
                               static(WSL, O_SGU, c, 2 * FS, half * FS, FS), c == 0, c == DC - 1)
            last.then_inc(sgu_full, 1)

        def shared_down(t):
            pe.wait_ge(sact_ok, t + 1)
            bk = claim(("sT", t))
            for c in range(SC):
                last = pe.transpose(bk[0:FH, c * P:(c + 1) * P], in_=aS[:, t % 2, c * FH:(c + 1) * FH],
                                    identity=ident[:, :])
            last.then_inc(a_full, 1)

        def shared_out(t):
            pe.wait_ge(sat_ok, t + 1)
            bk = claim(("sY", t))
            for c in range(SC):
                last = product(bk[:, 0:D], aSTH[:, t % 2, c * P:(c + 1) * P],
                               aSTL[:, t % 2, c * P:(c + 1) * P],
                               static(WSH, O_SD, c, D, 0, D)[0:FH], static(WSL, O_SD, c, D, 0, D)[0:FH],
                               c == 0, c == SC - 1)
            last.then_inc(a_full, 1)

        shared_up(0, 0)
        shared_up(0, 1)
        n = 0
        for t in range(TILES):
            if t + 1 < TILES:
                shared_up(t + 1, 0)
            if t >= LEAD_FROM:
                scores(n)
            if t + 1 < TILES:
                shared_up(t + 1, 1)
            if t >= LEAD_FROM:
                scores(n + 1)
            shared_down(t)
            if t == RANK_STEP:
                rank_base()
            if t >= LEAD_FROM:
                scores(n + 2)
                n += 3
            if t:
                shared_out(t - 1)
        shared_out(TILES - 1)
        neg_max_t(0)
        project("q", 2)
        project("k", 2)

        for n in range(SLOT_END):
            if n < HEADS:
                scores_t(n)
            if n + LEAD < HEADS:
                scores(n + LEAD)
            if 2 <= n < HEADS + 2:
                weigh(n - 2)
            if nat(n):
                natural(nat(n)[1])
            u = extra(n)
            if u:
                kind, b = u
                if kind in "qk":
                    project(kind, b)
                elif kind == "v":
                    values(b)
                elif kind == "mT":
                    neg_max_t(b)
                elif kind == "onT":
                    out_t(b)
                else:
                    out_proj(b)

        pe.wait_ge(max_ok, HEADS)
        pe.wait_ge(exp_ok, HEADS)
        pe.wait_ge(norm_ok, HEADS // 4)
        pe.wait_ge(ot_ok, HEADS // 4)
        pe.wait_ge(a_free, len(uses))
        X_B, AT_B, Y_B = A_B[0], A_B[1], OT_B

        def wait(s, v):
            if not (isinstance(v, int) and v <= 0):
                pe.wait_ge(s, v)

        def rows_t(i, c):
            wait(r_in[c % 4], 16 * (i + c // 4) + 16)
            wait(xt_ok, 4 * i + c)
            for k in range(DC):
                for j in range(2):
                    last = pe.transpose(PB[X_B][:, (2 * k + j) * P:(2 * k + j + 1) * P],
                                        in_=xin[:, c % 4, j, k * P:(k + 1) * P], identity=ident[:, :])
            last.then_inc(xt_full, 1)

        def up(i, c, j):
            s = c % 2
            wait(xt_ok, 4 * i + c + 1)
            wait(gu_split, 4 * i + c + 1)
            wait(mul_ok, 8 * i + 2 * (c - 2) + j + 1)
            for k in range(DC):
                last = product(PB[2 * s + j][:, 0:GN], xTH[s][:, k, j * P:(j + 1) * P],
                               xTL[s][:, k, j * P:(j + 1) * P], GH[s][:, k * GN:(k + 1) * GN],
                               GL[s][:, k * GN:(k + 1) * GN], k == 0, k == DC - 1)
            last.then_inc(gu_full, 1)

        def act_t(i, c):
            wait(mul_ok, 8 * i + 2 * c + 2)
            wait(at_ok, 4 * i + c)
            for k in range(2):
                for j in range(2):
                    last = pe.transpose(PB[AT_B][0:FH, (2 * k + j) * P:(2 * k + j + 1) * P],
                                        in_=act[:, c % 2, j, k * FH:(k + 1) * FH], identity=ident[:, :])
            last.then_inc(at_full, 1)

        def down(i, c):
            s = c % 2
            wait(at_ok, 4 * i + c + 1)
            wait(wd_split, 4 * i + c + 1)
            wait(y_ok, 8 * i + 2 * (c - 2) + 2)
            for j in range(2):
                for k in range(2):
                    last = product(PB[Y_B[s]][:, j * D:(j + 1) * D], aTH[s][:, k, j * P:(j + 1) * P],
                                   aTL[s][:, k, j * P:(j + 1) * P], DH[s][:, k * D:(k + 1) * D],
                                   DL[s][:, k * D:(k + 1) * D], k == 0, k == 1)
            last.then_inc(dn_full, 1)

        def step(i, c, first=False, last=False):
            if not first:
                act_t(i, c - 1)
            up(i, c, 0)
            if not last:
                rows_t(i, c + 1)
            up(i, c, 1)
            if not first:
                down(i, c - 1)

        rows_t(0, 0)
        for c in range(4):
            step(0, c, first=c == 0)
        with pe.Fori(1, E // 4 - 1, 1) as i:
            for c in range(4):
                step(i, c)
        for c in range(4):
            step(E // 4 - 1, c, last=c == 3)
        act_t(E // 4 - 1, 3)
        down(E // 4 - 1, 3)

        over = pe.value_load(nov_i[0:1, 0:1], min_val=0, max_val=OVT)
        with pe.If(over > 0):
            with pe.Fori(0, OVT, 1) as j:
                with pe.If(over > j):
                    pe.wait_ge(ov_in, 48 * j + 48)
                    for k in range(DC):
                        last = pe.transpose(PB[0][:, k * P:(k + 1) * P], in_=ov_x[:, k * P:(k + 1) * P],
                                            identity=ident[:, :])
                    last.then_inc(ov_xT_full, 1)
                    pe.wait_ge(ov_xT_ok, j + 1)
                    for k in range(DC):
                        last = pe.matmul(PB[1][:, 0:GN], lhsT=ov_xT[:, k, :], rhs=raw[:, k * GN:(k + 1) * GN],
                                         start=k == 0, stop=k == DC - 1)
                    last.then_inc(ov_gu, 1)
                    pe.wait_ge(ov_mul, j + 1)
                    for k in range(2):
                        last = pe.transpose(PB[2][0:FH, k * P:(k + 1) * P], in_=ov_a[:, 1, k * FH:(k + 1) * FH],
                                            identity=ident[:, :])
                    last.then_inc(ov_at, 1)
                    pe.wait_ge(ov_at_ok, j + 1)
                    for k in range(2):
                        last = pe.matmul(PB[3][:, 0:D], lhsT=ov_aT[:, k, :],
                                         rhs=raw[0:FH, GO + k * D:GO + (k + 1) * D], start=k == 0, stop=k == 1)
                    last.then_inc(ov_dn, 1)
            pe.wait_ge(ov_w, OVT + 1)

    @block.scalar
    def _(sc):
        def high(u, dst, src):
            sc.wait_ge(a_full, USE[u] + 1)
            return nc.scalar.activation(dst, src, ACT.Copy)

        sc.wait_ge(wq_in, 32)
        nc.scalar.activation(WSH[:, O_GATE:O_WO], raw[:, O_GATE:O_WO], ACT.Copy).then_inc(wsh_ok, 1)

        def square_root(g):
            sc.wait_ge(var_ok, g + 1)
            nc.scalar.activation(rstd[:, 4 * g:4 * g + 4, 1], rstd[:, 4 * g:4 * g + 4, 0], ACT.Sqrt)\
              .then_inc(sqrt_ok, 1)

        def xt_high(i):
            u = ("xt", i)
            high(u, XH[:, :, 2 * i * P:(2 * i + 2) * P],
                 bank_of(u)[:, :].rearrange("p (c n) -> p c n", c=DC)).then_inc(a_hi, 1)

        def logits_t(g):
            sc.wait_ge(lt_full, g + 1)
            nc.scalar.activation(LT[:, g * GT * P:(g + 1) * GT * P], PB[RT_B[g]][0:E, :], ACT.Copy)\
              .then_inc(lt_ok, 1)

        def logits(g):
            sc.wait_ge(lg_full, g + 1)
            if g == 0:
                sc.wait_ge(wsl2_ok, 1)
                sc.wait_ge(wsl_ok, 1)
            nc.scalar.activation(L[:, 8 * g:8 * g + 8, :],
                                 PB[T_B[g]][:, :].rearrange("p (t e) -> p t e", t=8), ACT.Copy)\
              .then_inc(lg_ok, 1)

        square_root(0)
        square_root(1)
        xt_high(0)
        xt_high(1)
        sc.wait_ge(w_in0, 48)
        nc.scalar.activation(WSH[:, O_WO:O_SD], raw[:, O_WO:O_SD], ACT.Copy)
        nc.scalar.activation(WSH[0:FH, O_SD:NST], raw[0:FH, O_SD:NST], ACT.Copy).then_inc(wsh_ok, 1)
        square_root(2)
        xt_high(2)
        xt_high(3)
        square_root(3)
        logits_t(0)
        xt_high(4)
        xt_high(5)
        logits_t(1)
        xt_high(6)
        xt_high(7)
        logits(0)
        logits_t(2)
        logits_t(3)

        def stage(which, b):
            u = (which, b)
            s = 0 if which == "q" else 2
            if b >= 1:
                sc.wait_ge(qk_w, 64 * b)
            sc.wait_ge(a_full, USE[u] + 1)
            for k in range(2):
                last = nc.scalar.activation(stg[s][:, k, :], bank_of(u)[:, k * SEQ:(k + 1) * SEQ],
                                            ACT.Identity, bias=bq[:, s + k:s + k + 1])
            last.then_inc(a_hi, 1)

        sc.wait_ge(b_in, 48)
        stage("q", 0)
        logits(1)
        stage("k", 0)
        stage("q", 1)
        stage("k", 1)
        sc.wait_ge(dlt_ok, 1)
        nc.scalar.activation(run[:, :, :], run[:, :, :], ACT.Exp)
        nc.scalar.activation(XE[:, :, C_W:C_W + K], XE[:, :, C_W:C_W + K], ACT.Exp).then_inc(ex_ok, 1)

        def shared_act(t):
            sc.wait_ge(sgu_full, 2 * t + 1)
            if t >= 2:
                sc.wait_ge(sact_ok, t - 1)
            nc.scalar.activation(sgS[:, t % 2, :], PB[(T_B, OT_B)[t % 2][0]][:, 0:FS], ACT.Silu)\
              .then_inc(ssilu_ok, 1)

        def shared_actT(t):
            u = ("sT", t)
            if t >= 2:
                sc.wait_ge(a_full, USE[("sY", t - 2)] + 1)
            high(u, aSTH[:, t % 2, :], bank_of(u)[0:FH, :]).then_inc(sat_hi, 1)

        shared_act(0)
        for t in range(TILES):
            if t + 1 < TILES:
                shared_act(t + 1)
            shared_actT(t)

        def prob(n):
            sc.wait_ge(st_full, n + 1)
            if n >= 3:
                sc.wait_ge(pv_ok, n - 2)
            elif n == 0:
                sc.wait_ge(route_ok, 1)
            nc.scalar.activation(EX[:, n % 3, :], PB[T_B[n % 2]][:, :], ACT.Exp, scale=SCALE)\
              .then_inc(exp_ok, 1)

        def take_out(g):
            sc.wait_ge(pv_ok, 4 * g + 4)
            if g >= 2:
                sc.wait_ge(a_full, USE[("nt", g - 2)] + 1)
            if g == 0:
                sc.wait_ge(fill_in, 16 * E)
            nc.scalar.activation(OTs[:, g % 2, :], PB[OT_B[g % 2]][:, 0:SEQ], ACT.Copy)\
              .then_inc(ot_ok, 1)

        stage("q", 2)
        stage("k", 2)
        for n in range(SLOT_END):
            if n < HEADS:
                prob(n)
            if n >= 5 and (n - 5) % 4 == 0 and (n - 5) // 4 < HEADS // 4:
                take_out((n - 5) // 4)
            u = extra(n)
            if u and u[0] in "qk":
                stage(*u)
            elif u and u[0] == "onT":
                if u[1] == 0:
                    sc.wait_ge(fill_free, 1)
                else:
                    sc.wait_ge(a_full, USE[("o", u[1] - 1)] + 1)
                high(u, OnTH[:, :, :], bank_of(u)[:, :].rearrange("p (c n) -> p c n", c=DC))\
                    .then_inc(a_hi, 1)

        def wait(s, v):
            if not (isinstance(v, int) and v <= 0):
                sc.wait_ge(s, v)

        def gate_high(i, c):
            wait(w_in[c % 4], 32 * (i + c // 4) + 32)
            wait(gu_full, 8 * i + 2 * (c - 2) + 2)
            o = (c % 4) * WN
            nc.scalar.activation(GH[c % 2][:, :], raw[:, o:o + GO], ACT.Copy).then_inc(guH_ok, 1)

        def silu(i, c, j):
            wait(gu_full, 8 * i + 2 * c + j + 1)
            nc.scalar.activation(sg[:, c % 2, j, :], PB[2 * (c % 2) + j][:, 0:F], ACT.Silu)\
              .then_inc(silu_ok, 1)

        def act_high(i, c):
            wait(at_full, 4 * i + c + 1)
            wait(dn_full, 4 * i + c - 1)
            nc.scalar.activation(aTH[c % 2][:, :, :],
                                 PB[A_B[1]][0:FH, :].rearrange("p (k n) -> p k n", k=2), ACT.Copy)\
              .then_inc(atH_ok, 1)

        def rows_high(i, c):
            wait(xt_full, 4 * i + c + 1)
            wait(gu_full, 8 * i + 2 * (c - 2) + 2)
            nc.scalar.activation(xTH[c % 2][:, :, :],
                                 PB[A_B[0]][:, :].rearrange("p (k n) -> p k n", k=DC), ACT.Copy)\
              .then_inc(xtH_ok, 1)

        def down_high(i, c):
            wait(w_in[c % 4], 32 * (i + c // 4) + 32)
            wait(dn_full, 4 * i + c - 1)
            o = (c % 4) * WN
            nc.scalar.activation(DH[c % 2][:, :], raw[0:FH, o + GO:o + WN], ACT.Copy).then_inc(dh_ok, 1)

        def weighted(i, c):
            for j in range(2):
                if j == 0:
                    wait(dn_full, 4 * i + c + 1)
                    wait(wcol_ok, 4 * i + c + 1)
                    wait(y_free, 4 * i + c - 2)
                nc.scalar.activation(y[:, c % 4, j, :], PB[OT_B[c % 2]][:, j * D:(j + 1) * D],
                                     ACT.Copy, scale=wcol[:, c % 4, j:j + 1]).then_inc(y_ok, 1)

        def step(i, c, first=False, last=False, tail=False):
            if not first:
                act_high(i, c - 1)
            silu(i, c, 0)
            if not last:
                rows_high(i, c + 1)
            silu(i, c, 1)
            if not tail or c < 2:
                gate_high(i, c + 2)
            down_high(i, c)
            if not first:
                weighted(i, c - 1)

        sc.wait_ge(a_full, USE[("v", B - 1)] + 1)
        gate_high(0, 0)
        gate_high(0, 1)
        rows_high(0, 0)
        for c in range(4):
            step(0, c, first=c == 0)
        with sc.Fori(1, E // 4 - 1, 1) as i:
            for c in range(4):
                step(i, c)
        for c in range(4):
            step(E // 4 - 1, c, last=c == 3, tail=True)
        act_high(E // 4 - 1, 3)
        weighted(E // 4 - 1, 3)

        over = sc.value_load(nov_i[0:1, 0:1], min_val=0, max_val=OVT)
        with sc.If(over > 0):
            with sc.Fori(0, OVT, 1) as j:
                with sc.If(over > j):
                    sc.wait_ge(ov_gu, j + 1)
                    nc.scalar.activation(ov_a[:, 0, :], PB[1][:, 0:F], ACT.Silu).then_inc(ov_silu, 1)
            sc.wait_ge(ov_w, OVT + 1)

    @block.vector
    def _(ve):
        n_ = [0]

        def link(ins):
            n_[0] += 1
            ins.then_inc(chain, 1)
            ve.wait_ge(chain, n_[0])

        def low(dst, src, hi):
            return nc.vector.tensor_tensor(dst, src, raw32(hi), ALU.subtract)

        def stats(g):
            ve.wait_ge(x_in[g], 16)
            for t in range(4 * g, 4 * g + 4):
                last = nc.vector.bn_stats(st6[:, t, :], base[:, t, :])
            link(last)
            for t in range(4 * g, 4 * g + 4):
                last = nc.vector.bn_aggr(mv[:, t, :], st6[:, t, :])
            link(last)
            nc.vector.tensor_scalar_add(rstd[:, 4 * g:4 * g + 4, 0], mv[:, 4 * g:4 * g + 4, 1], LN_EPS)\
              .then_inc(var_ok, 1)

        def normalise(g):
            ve.wait_ge(sqrt_ok, g + 1)
            link(nc.vector.reciprocal(rstd[:, 4 * g:4 * g + 4, 2], rstd[:, 4 * g:4 * g + 4, 1]))
            for t in range(4 * g, 4 * g + 4):
                nc.vector.tensor_scalar(XE[:, t, 0:D], base[:, t, :], mv[:, t, 0:1], rstd[:, t, 2:3],
                                        ALU.subtract, ALU.mult).then_inc(xn_ok, 1)

        def low_of_a(u, dst, src, hi, hi_sem, hi_val):
            ve.wait_ge(hi_sem, hi_val)
            return low(dst, src, hi).then_inc(a_free, 1)

        hi_n = [0]

        def xt_low(i):
            u = ("xt", i)
            hi_n[0] += 1
            s = slice(2 * i * P, (2 * i + 2) * P)
            low_of_a(u, XL[:, :, s], bank_of(u)[:, :].rearrange("p (c n) -> p c n", c=DC), XH[:, :, s],
                     a_hi, hi_n[0])

        def stage_low(which, b):
            u = (which, b)
            s = 0 if which == "q" else 2
            hi_n[0] += 1
            ve.wait_ge(a_hi, hi_n[0])
            for k in range(2):
                last = nc.vector.scalar_tensor_tensor(out=stg[s + 1][:, k, :],
                                                      in0=bank_of(u)[:, k * SEQ:(k + 1) * SEQ],
                                                      scalar=bq[:, s + k:s + k + 1],
                                                      in1=raw32(stg[s][:, k, :]), op0=ALU.add,
                                                      op1=ALU.subtract)
            last.then_inc(stg_q if which == "q" else stg_k, 1)
            ve.wait_ge(stg_q if which == "q" else stg_k, b + 1)
            ve.sem_inc(a_free, 1)

        def values(b):
            u = ("v", b)
            ve.wait_ge(a_full, USE[u] + 1)
            if b == 0:
                ve.wait_ge(const_ok, CONSTS)
            if b >= 2:
                ve.wait_ge(pv_ok, H * (b - 1))
            nc.vector.tensor_tensor(V[:, b % 2, :, :, 0:HD],
                                    bank_of(u)[:, :].rearrange("p (t h d) -> p t h d", t=2, h=H),
                                    bv[:, :].rearrange("p (a h d) -> p a h d", a=1, h=H)
                                    .broadcast_to([P, 2, H, HD]), ALU.add).then_inc(v_ok, 1)
            ve.wait_ge(v_ok, b + 1)
            ve.sem_inc(a_free, 1)

        stats(0)
        normalise(0)
        stats(1)
        ve.wait_ge(wsh_ok, 1)
        low(WSL[:, O_GATE:O_WO], raw[:, O_GATE:O_WO], WSH[:, O_GATE:O_WO]).then_inc(wsl_ok, 1)
        normalise(1)
        stats(2)
        xt_low(0)
        xt_low(1)
        normalise(2)
        stats(3)
        xt_low(2)
        xt_low(3)
        normalise(3)
        xt_low(4)
        xt_low(5)
        xt_low(6)
        xt_low(7)

        w6 = XE[:, :, C_W:C_W + K]

        def largest(g):
            ve.wait_ge(lg_ok, g + 1)
            for t in range(8 * g, 8 * g + 8):
                last = nc.vector.max(top8[:, t, :], L[:, t, :])
            link(last)
            for t in range(8 * g, 8 * g + 8):
                last = nc.vector.max_index(idx8[:, t, :], top8[:, t, :], L[:, t, :])
            link(last)

        def differences():
            nc.vector.tensor_tensor(run[:, :, :], L[:, :, :], top8[:, :, 0:1].broadcast_to([P, TILES, E]),
                                    ALU.subtract)
            nc.vector.tensor_tensor(w6, top8[:, :, 0:K], top8[:, :, 0:1].broadcast_to([P, TILES, K]),
                                    ALU.subtract).then_inc(dlt_ok, 1)

        def one_hot(g):
            link(nc.vector.tensor_tensor(
                oh[:, 4 * g * K:4 * (g + 1) * K, :].rearrange("p (t k) e -> p t k e", k=K),
                iota_e[:, :].rearrange("p (a b e) -> p a b e", a=1, b=1).broadcast_to([P, 4, K, E]),
                XE[:, 4 * g:4 * g + 4, C_IDX:C_IDX + K].rearrange("p t (k a) -> p t k a", a=1)
                .broadcast_to([P, 4, K, E]), ALU.is_equal))

        def masks(g):
            t = slice(8 * g, 8 * g + 8)
            with nc.allow_low_precision("counts up to 16 are exact"):
                link(nc.vector.tensor_reduce(
                    mask[:, t, :], oh[:, 8 * g * K:8 * (g + 1) * K, :].rearrange("p (t k) e -> p t e k", k=K),
                    AX.X, ALU.add))

        def mask_sum():
            with nc.allow_low_precision("counts up to 16 are exact"):
                nc.vector.tensor_reduce(masksum[:, :], mask[:, :, :].rearrange("p t e -> p e t"), AX.X,
                                        ALU.add).then_inc(sum_ok, 1)

        def softmax():
            ve.wait_ge(ex_ok, 1)
            link(nc.vector.tensor_reduce(top8[:, :, 0], run[:, :, :], AX.X, ALU.add))
            link(nc.vector.reciprocal(top8[:, :, 1], top8[:, :, 0]))
            link(nc.vector.tensor_tensor(w6, w6, top8[:, :, 1:2].broadcast_to([P, TILES, K]), ALU.mult))
            link(nc.vector.tensor_reduce(top8[:, :, 2], w6, AX.X, ALU.add))
            link(nc.vector.tensor_scalar_add(top8[:, :, 3], top8[:, :, 2], TOPK_EPS))
            link(nc.vector.reciprocal(top8[:, :, 4], top8[:, :, 3]))
            link(nc.vector.tensor_tensor(w6, w6, top8[:, :, 4:5].broadcast_to([P, TILES, K]), ALU.mult))

        tiles_i = L[:, 0, :].bitcast(i32)

        def ranks(first, end):
            if first == 0:
                ve.wait_ge(base_full, 1)
                nc.vector.tensor_copy(run[:, 0, :], PB[S_B[0]][:, 0:E])
                link(nc.vector.tensor_scalar(tiles_i, PB[S_B[0]][:, E:2 * E], float(SLOTS - P + 1), 0.0,
                                             ALU.subtract, ALU.max))
                ve.sem_inc(rank_read, 1)
            for t in range(max(first, 1), end):
                link(nc.vector.tensor_tensor(run[:, t, :], run[:, t - 1, :], mask[:, t - 1, :], ALU.add))

        OVC = (E - 1).bit_length() % 2

        def overflow():
            link(nc.vector.tensor_scalar(tiles_i, tiles_i, 7, None, ALU.logical_shift_right))
            link(nc.vector.tensor_copy(ovc[:, 0, :], tiles_i))
            link(nc.vector.tensor_copy(L[:, 1, :], ovc[:, 0, :]))
            cur, sh = 0, 1
            while sh < E:
                nc.vector.tensor_copy(ovc[:, 1 - cur, 0:sh], ovc[:, cur, 0:sh])
                link(nc.vector.tensor_tensor(ovc[:, 1 - cur, sh:E], ovc[:, cur, sh:E],
                                             ovc[:, cur, 0:E - sh], ALU.add))
                cur, sh = 1 - cur, 2 * sh
            assert cur == OVC
            nc.vector.tensor_copy(nov_i[:, 0:1], ovc[:, OVC, E - 1:E])
            link(nc.vector.tensor_tensor(L[:, 2, :], ovc[:, OVC, :], L[:, 1, :], ALU.subtract))
            link(nc.vector.tensor_scalar(L[:, 3, :], L[:, 2, :], float(P), float(REG - SLOTS), ALU.mult,
                                         ALU.add))
            link(nc.vector.scalar_tensor_tensor(out=L[:, 4, :], in0=iota_e[:, :], scalar=-float(SLOTS),
                                                in1=L[:, 3, :], op0=ALU.mult, op1=ALU.add))

        def correct():
            corr = L[:, 5:5 + 8, :]
            for g in range(2):
                r = run[:, 8 * g:8 * g + 8, :]
                link(nc.vector.scalar_tensor_tensor(out=corr, in0=r, scalar=float(SLOTS),
                                                    in1=L[:, 4:5, :].broadcast_to([P, 8, E]),
                                                    op0=ALU.is_ge, op1=ALU.mult))
                link(nc.vector.tensor_tensor(r, r, corr, ALU.add))
            ve.sem_inc(run_ok, 1)

        def slots(g):
            ve.wait_ge(prod_ok, g + 1)
            nc.vector.tensor_reduce(L[:, 13, 0:2 * K], prod[:, g % 2, :, :], AX.X, ALU.add)\
              .then_inc(prod_free, 1)
            ve.wait_ge(prod_free, g + 1)
            link(nc.vector.scalar_tensor_tensor(
                out=posi[:, 2 * g * K:2 * (g + 1) * K].rearrange("p (t k) -> p t k", k=K),
                in0=XE[:, 2 * g:2 * g + 2, C_IDX:C_IDX + K], scalar=float(SLOTS),
                in1=L[:, 13, 0:2 * K].rearrange("p (t k) -> p t k", k=K), op0=ALU.mult, op1=ALU.add))
            if g == TILES // 2 - 1:
                ve.sem_inc(route_ok, 1)

        def routing(t):
            if t in (0, 2):
                one_hot(t)
                one_hot(t + 1)
            elif t in (1, 3):
                masks(t // 2)
            elif t == RANK_STEP - 1:
                mask_sum()
                softmax()
            elif t == RANK_STEP + 1:
                ranks(0, 8)
            elif t == RANK_STEP + 2:
                ranks(8, TILES)
            elif t == RANK_STEP + 3:
                overflow()
                correct()
            elif RANK_STEP + 4 <= t < RANK_STEP + 8:
                for g in range(2):
                    slots(2 * (t - RANK_STEP - 4) + g)

        largest(0)
        stage_low("q", 0)
        largest(1)
        nc.vector.tensor_copy(XE[:, :, C_IDX:C_IDX + K], idx8[:, :, 0:K])
        differences()
        stage_low("k", 0)
        stage_low("q", 1)
        stage_low("k", 1)
        values(0)

        def shared_mul(t):
            ve.wait_ge(ssilu_ok, t + 1)
            ve.wait_ge(sgu_full, 2 * t + 2)
            if t >= 2:
                ve.wait_ge(a_full, USE[("sT", t - 2)] + 1)
            nc.vector.tensor_tensor(aS[:, t % 2, :], sgS[:, t % 2, :], PB[(T_B, OT_B)[t % 2][1]][:, 0:FS],
                                    ALU.mult).then_inc(sact_ok, 1)

        def shared_low(t):
            u = ("sT", t)
            ve.wait_ge(sat_hi, t + 1)
            low(aSTL[:, t % 2, :], bank_of(u)[0:FH, :], aSTH[:, t % 2, :]).then_inc(sat_ok, 1)
            ve.wait_ge(sat_ok, t + 1)
            ve.sem_inc(a_free, 1)

        def shared_add(t):
            u = ("sY", t)
            ve.wait_ge(a_full, USE[u] + 1)
            ve.wait_ge(xbo_ok, t + 1)
            nc.vector.tensor_tensor(base[:, t, :], bank_of(u)[:, 0:D], base[:, t, :], ALU.add)\
              .then_inc(a_free, 1)

        def maximum(n):
            b, h = divmod(n, H)
            ve.wait_ge(s_full, n + 1)
            if h == 0 and b >= 2:
                ve.wait_ge(m_ok, b - 1)
            nc.vector.tensor_reduce(mx[:, b % 2, :, h], PB[S_B[n % 2]][:, :]
                                    .rearrange("p (j n) -> p j n", j=2), AX.X, ALU.max, negate=True)\
              .then_inc(max_ok, 1)

        shared_mul(0)
        n = 0
        for t in range(TILES):
            if t >= LEAD_FROM:
                maximum(n)
            if t + 1 < TILES:
                shared_mul(t + 1)
            if t >= LEAD_FROM:
                maximum(n + 1)
            shared_low(t)
            if t:
                shared_add(t - 1)
            if t >= LEAD_FROM:
                maximum(n + 2)
                n += 3
            routing(t)
        shared_add(TILES - 1)

        def neg_max(b):
            u = ("mT", b)
            ve.wait_ge(a_full, USE[u] + 1)
            if b >= 1:
                ve.wait_ge(m_w, 16 * b)
            nc.vector.tensor_copy(mTs[:, :], bank_of(u)[0:H, 0:SEQ]).then_inc(m_ok, 1)
            ve.wait_ge(m_ok, b + 1)
            ve.sem_inc(a_free, 1)

        def norm(g):
            b = g // 4
            ve.wait_ge(a_full, USE[("nt", g)] + 1)
            src = bank_of(("nt", g))[:, 0:SEQ].rearrange("p (j h d) -> p j h d", j=2, h=4)
            link(nc.vector.reciprocal(rden[:, g % 2, :, :], src[:, :, :, HD]))
            if g % 4 == 0 and b >= 2:
                ve.wait_ge(a_full, USE[("onT", b - 2)] + 1)
            nc.vector.tensor_tensor(
                On[:, b % 2, :, (g % 4) * 64:(g % 4 + 1) * 64].rearrange("p j (h d) -> p j h d", h=4),
                src[:, :, :, 0:HD],
                rden[:, g % 2, :, :].rearrange("p j (h a) -> p j h a", a=1).broadcast_to([P, 2, 4, HD]),
                ALU.mult).then_inc(norm_ok, 1)
            ve.wait_ge(norm_ok, g + 1)
            ve.sem_inc(a_free, 1)

        nc.vector.memset(raw32(KS[2][32:64, :, :]), 1.0)
        nc.vector.memset(raw32(KS[2][96:128, :, :]), 1.0).then_inc(ones2_ok, 1)
        neg_max(0)
        stage_low("q", 2)
        stage_low("k", 2)
        for n in range(SLOT_END):
            if n + LEAD < HEADS:
                maximum(n + LEAD)
            if nat(n):
                norm(nat(n)[1])
            u = extra(n)
            if u:
                kind, b = u
                if kind in "qk":
                    stage_low(kind, b)
                elif kind == "v":
                    values(b)
                elif kind == "mT":
                    neg_max(b)
                elif kind == "onT":
                    hi_n[0] += 1
                    ve.wait_ge(a_hi, hi_n[0])
                    low(OnTL[:, :, :], bank_of(u)[:, :].rearrange("p (c n) -> p c n", c=DC), OnTH[:, :, :])\
                        .then_inc(ont_ok, 1)
                    ve.wait_ge(ont_ok, b + 1)
                    ve.sem_inc(a_free, 1)
                else:
                    ve.wait_ge(a_full, USE[u] + 1)
                    bs = base[:, 2 * b:2 * b + 2, :]
                    nc.vector.tensor_tensor(bs, bank_of(u)[:, :].rearrange("p (j n) -> p j n", j=2), bs,
                                            ALU.add).then_inc(base_ok, 1)
                    ve.wait_ge(base_ok, b + 1)
                    ve.sem_inc(a_free, 1)

        def wait(s, v):
            if not (isinstance(v, int) and v <= 0):
                ve.wait_ge(s, v)

        def gate_low(i, c):
            wait(guH_ok, 4 * i + c + 1)
            o = (c % 4) * WN
            low(GL[c % 2][:, :], raw[:, o:o + GO], GH[c % 2][:, :]).then_inc(gu_split, 1)

        def mul(i, c, j):
            wait(silu_ok, 8 * i + 2 * c + j + 1)
            wait(at_full, 4 * i + c - 1)
            nc.vector.tensor_tensor(act[:, c % 2, j, :], sg[:, c % 2, j, :],
                                    PB[2 * (c % 2) + j][:, F:2 * F], ALU.mult).then_inc(mul_ok, 1)

        def act_low(i, c):
            wait(atH_ok, 4 * i + c + 1)
            low(aTL[c % 2][:, :, :], PB[A_B[1]][0:FH, :].rearrange("p (k n) -> p k n", k=2),
                aTH[c % 2][:, :, :]).then_inc(at_ok, 1)

        def rows_low(i, c):
            wait(xtH_ok, 4 * i + c + 1)
            low(xTL[c % 2][:, :, :], PB[A_B[0]][:, :].rearrange("p (k n) -> p k n", k=DC),
                xTH[c % 2][:, :, :]).then_inc(xt_ok, 1)

        def down_low(i, c):
            wait(dh_ok, 4 * i + c + 1)
            o = (c % 4) * WN
            low(DL[c % 2][:, :], raw[0:FH, o + GO:o + WN], DH[c % 2][:, :]).then_inc(wd_split, 1)

        def weights_of(i, c):
            s = c % 4
            wait(r_in[s], 16 * (i + c // 4) + 16)
            wait(y_free, 4 * i + c - 2)
            nc.vector.tensor_copy(ids[:, s, :], xin[:, s, :, C_TOK].bitcast(i32))
            nc.vector.tensor_scalar_add(ecur[:, s:s + 1], ecur[:, s:s + 1], 4.0).then_inc(w_step, 1)
            wait(w_step, 8 * i + 2 * c + 1)
            nc.vector.scalar_tensor_tensor(out=wtmp[:, :, :], in0=xin[:, s, :, C_IDX:C_IDX + K],
                                           scalar=ecur[:, s:s + 1], in1=xin[:, s, :, C_W:C_W + K],
                                           op0=ALU.is_equal, op1=ALU.mult).then_inc(w_step, 1)
            wait(w_step, 8 * i + 2 * c + 2)
            nc.vector.tensor_reduce(wcol[:, s, :], wtmp[:, :, :], AX.X, ALU.add).then_inc(wcol_ok, 1)

        def step(i, c, first=False, last=False, tail=False):
            if not first:
                act_low(i, c - 1)
            mul(i, c, 0)
            if not last:
                rows_low(i, c + 1)
            mul(i, c, 1)
            if not tail or c < 2:
                gate_low(i, c + 2)
            down_low(i, c)
            if not last:
                weights_of(i, c + 1)

        gate_low(0, 0)
        gate_low(0, 1)
        rows_low(0, 0)
        weights_of(0, 0)
        for c in range(4):
            step(0, c, first=c == 0)
        with ve.Fori(1, E // 4 - 1, 1) as i:
            for c in range(4):
                step(i, c)
        for c in range(4):
            step(E // 4 - 1, c, last=c == 3, tail=True)
        act_low(E // 4 - 1, 3)

        over = ve.value_load(nov_i[0:1, 0:1], min_val=0, max_val=OVT)
        with ve.If(over > 0):
            ve.wait_ge(y_free, E + 1)
            link(nc.vector.memset(ov_cmp[:, 0, 0:1], 0.0))
            for j in range(OVT):
                last = nc.vector.tensor_scalar(ov_cmp[:, j, :], ovc[:, OVC, :], float(j), None, ALU.is_le)
            link(last)
            link(nc.vector.tensor_reduce(ov_e[:, :], ov_cmp[:, :, :], AX.X, ALU.add))
            link(nc.vector.tensor_scalar_min(ov_e[:, :], ov_e[:, :], float(E - 1)))
            nc.vector.tensor_copy(ov_ei[:, :], ov_e[:, :]).then_inc(ov_e_ok, 1)
            ve.wait_ge(ov_e_ok, 1)
            with ve.Fori(0, OVT, 1) as j:
                with ve.If(over > j):
                    ve.wait_ge(ov_xT_full, j + 1)
                    nc.vector.tensor_copy(ov_xT[:, :, :], PB[0][:, 0:DC * P].rearrange("p (k n) -> p k n", k=DC))\
                      .then_inc(ov_xT_ok, 1)
                    nc.vector.tensor_copy(ov_c[:, 0:1], ov_e[:, bass.ds(j, 1)]).then_inc(ov_s, 1)
                    ve.wait_ge(ov_s, 3 * j + 1)
                    nc.vector.scalar_tensor_tensor(out=wtmp[:, 0, :], in0=ov_x[:, C_IDX:C_IDX + K],
                                                   scalar=ov_c[:, 0:1], in1=ov_x[:, C_W:C_W + K],
                                                   op0=ALU.is_equal, op1=ALU.mult).then_inc(ov_s, 1)
                    ve.wait_ge(ov_s, 3 * j + 2)
                    nc.vector.tensor_reduce(ov_c[:, 1:2], wtmp[:, 0, :], AX.X, ALU.add).then_inc(ov_s, 1)
                    nc.vector.tensor_copy(ov_id[:, 0:1], ov_x[:, C_TOK:C_TOK + 1].bitcast(i32))
                    ve.wait_ge(ov_silu, j + 1)
                    nc.vector.tensor_tensor(ov_a[:, 1, :], ov_a[:, 0, :], PB[1][:, F:2 * F], ALU.mult)\
                      .then_inc(ov_mul, 1)
                    ve.wait_ge(ov_at, j + 1)
                    nc.vector.tensor_copy(ov_aT[:, :, :], PB[2][0:FH, 0:2 * P].rearrange("p (k n) -> p k n", k=2))\
                      .then_inc(ov_at_ok, 1)
                    ve.wait_ge(ov_dn, j + 1)
                    ve.wait_ge(ov_s, 3 * j + 3)
                    nc.vector.tensor_scalar(ov_y[:, :], PB[3][:, 0:D], ov_c[:, 1:2], None, ALU.mult)\
                      .then_inc(ov_y_ok, 1)
            ve.wait_ge(ov_w, OVT + 1)

    block_cm.__exit__(None, None, None)


def kernel(**inputs):
    import numpy as np
    import concourse.bacc as bacc
    from concourse.bass_utils import run_bass_kernel_spmd

    def rows(w, p=128):
        return np.ascontiguousarray(w.reshape(-1, p, w.shape[1]).transpose(1, 0, 2))

    a = {k[3:]: np.asarray(v) for k, v in inputs.items()}
    x = a["attn_x"].reshape(-1, a["attn_x"].shape[-1])
    D = x.shape[1]
    b = a["attn_b_qkv"]
    gu, dn = a["ffn_w_gate_up"], a["ffn_w_down"]
    E, F = gu.shape[0], dn.shape[2]
    arrays = {
        "x": np.ascontiguousarray(x),
        "gate": rows(a["ffn_gate_w"].T),
        "wqkv": rows(a["attn_w_qkv"].T),
        "bqk": np.ascontiguousarray(b[:2 * D].reshape(4, 128).T),
        "bvo": np.stack([b[2 * D:], a["attn_b_o"]]),
        "wo": rows(a["attn_w_o"].T),
        "wsgu": rows(a["ffn_ws_gate_up"].T),
        "wsd": rows(a["ffn_ws_down"].T, F // 2),
        "wgu": np.ascontiguousarray(gu.reshape(E, 2 * F, 2, 128).transpose(0, 3, 2, 1)).reshape(E, 128, 4 * F),
        "wd": np.ascontiguousarray(dn.reshape(E, D, 2, F // 2).transpose(0, 3, 2, 1)).reshape(E, F // 2, 2 * D),
    }
    nc = bacc.Bacc("TRN2", target_bir_lowering=False, num_devices=1)
    ts = [nc.dram_tensor(k, v.shape, mybir.dt.from_np(v.dtype), kind="ExternalInput").ap()
          for k, v in arrays.items()]
    out = nc.dram_tensor("out", (x.shape[0] + 256, D), mybir.dt.float32, kind="ExternalOutput").ap()
    block_kernel(nc, *ts, out)
    r = run_bass_kernel_spmd(nc, [arrays], core_ids=[0])
    return r.results[0]["out"][:x.shape[0]].reshape(a["attn_x"].shape)
```

```python
import concourse.bass as bass
from concourse import mybir


def block_kernel(nc, x, gate, wqkv, bqk, bvo, wo, wsgu, wsd, wgu, wd, out):
    f32, f32r, bf16, i32, u32 = (mybir.dt.float32, mybir.dt.float32r, mybir.dt.bfloat16,
                                 mybir.dt.int32, mybir.dt.uint32)
    ALU = mybir.AluOpType
    ACT = mybir.ActivationFunctionType
    AX = mybir.AxisListType

    P = 128
    TOK, D = x.shape
    TILES = TOK // P
    B = 8
    SEQ = TOK // B
    H, HD = 16, 16
    DC = D // P
    E = gate.shape[2]
    K = 6
    F = 176
    FH = F // 2
    FS = 2 * F
    SC = -(-FS // P)
    SH = wsd.shape[0]
    SCALE = float(HD) ** -0.5
    LN_EPS, TOPK_EPS = 1e-5, 1e-20
    SLOTS = 2 * P
    REG = E * SLOTS
    BODY = 8
    OVT = (TOK * K) // P
    ROW = 272
    C_IDX, C_W, C_TOK = D, D + K, D + 2 * K
    GN, GO = 2 * F, DC * 2 * F
    WN = GO + 2 * D
    LEAD = 23
    HEADS = B * H
    LEAD_FROM = 4
    BESIDE = {0: ("q", 1), 2: ("k", 1), 7: ("rk", 0), 11: ("q", 2), 12: ("k", 2), 14: ("mT", 0)}

    xs_d = nc.dram_tensor("slot_rows", [REG + OVT * P, ROW], f32, kind="Internal").ap()
    qk_d = nc.dram_tensor("qk_parts", [B, 4, 2 * P, SEQ], f32, kind="Internal").ap()
    m_d = nc.dram_tensor("neg_max", [B, H, SEQ], f32, kind="Internal").ap()

    place = [(nc.sbuf_base + 63) // 64 * 64]

    def sb(name, shape, dt, at=None):
        n = 2 if dt == bf16 else 4
        for s in shape[1:]:
            n *= s
        where = place[0] if at is None else at[0]
        t = nc.alloc_sbuf_tensor_at(name, shape, dt, offset=where, align_bytes=32)
        if at is None:
            place[0] += (n + 31) // 32 * 32
            assert place[0] <= nc.sbuf_usable_end, (name, place[0])
        else:
            at[0] += (n + 31) // 32 * 32
            assert at[0] <= at[1], (name, at)
        return t

    def region(nbytes):
        start = place[0]
        place[0] += nbytes
        assert place[0] <= nc.sbuf_usable_end, place[0]
        return start, nbytes

    def within(r, skip=0):
        return [r[0] + skip, r[0] + r[1]]

    ident = sb("ident", [P, P], f32)
    before = sb("before", [P, P], bf16)
    ones = sb("ones", [P, P], bf16)
    iota_e = sb("iota_e", [P, E], f32)
    ecur = sb("ecur", [P, 4], f32)
    bq = sb("bq", [P, 4], f32)
    bv = sb("bv", [P, D], f32)
    mv = sb("mv", [P, TILES, 2], f32)
    st6 = sb("st6", [P, TILES, 6], f32)
    rstd = sb("rstd", [P, TILES, 3], f32)
    posi = sb("posi", [P, TILES * K], i32)
    nov_i = sb("nov_i", [P, 2], i32)
    mx = sb("mx", [P, 2, 2, H], f32)
    mTs = sb("mTs", [H, SEQ], f32r)
    rden = sb("rden", [P, 2, 2, 4], f32)
    wcol = sb("wcol", [P, 4, 2], f32)
    wtmp = sb("wtmp", [P, 2, K], f32)
    ids = sb("ids", [P, 4, 2], i32)
    masksum = sb("masksum", [P, E], bf16)
    ovc = sb("ovc", [P, 2, E], f32)

    base = sb("base", [P, TILES, D], f32)
    r_xe = region(TILES * ROW * 4)
    XE = sb("XE", [P, TILES, ROW], f32, within(r_xe))
    r_xt = region(2 * DC * TOK * 4)
    a = within(r_xt)
    XH = sb("XH", [P, DC, TOK], f32r, a)
    XL = sb("XL", [P, DC, TOK], f32r, a)
    r_raw = region(4 * WN * 4)
    raw = sb("raw", [P, 4 * WN], f32, within(r_raw))
    O_GATE, O_QKV = 0, DC * E
    O_WO = O_QKV + DC * 3 * D
    O_SGU = O_WO + DC * D
    O_SD = O_SGU + DC * 2 * FS
    NST = O_SD + SC * D
    r_ws = [region(NST * 4) for _ in range(2)]
    WSH = sb("WSH", [P, NST], f32r, within(r_ws[0]))
    WSL = sb("WSL", [P, NST], f32r, within(r_ws[1]))
    EX = [sb(f"EX{s}", [P, 4, 2 * SEQ], f32, within(r_ws[s], O_SGU * 4)) for s in range(2)]
    a = within(r_raw)
    L = sb("L", [P, TILES, E], f32, a)
    mask = sb("mask", [P, TILES, E], bf16, a)
    run = sb("run", [P, TILES, E], f32, a)
    idx8 = sb("idx8", [P, TILES, 8], u32, a)
    prod = sb("prod", [P, 2, 2 * K, E], f32, a)
    top8 = sb("top8", [P, TILES, 8], f32, a)
    r_qk = region(3 * 2 * 8 * SEQ * 4)
    a = within(r_qk)
    QS, KS = [], []
    for s in range(3):
        QS.append(sb(f"QS{s}", [P, 8, SEQ], f32r, a))
        KS.append(sb(f"KS{s}", [P, 8, SEQ], f32r, a))
    LT = sb("LT", [E, TOK], f32, within(r_qk, 2 * 8 * SEQ * 4))
    a = within(r_qk, 2 * 2 * 8 * SEQ * 4)
    sgS = sb("sgS", [P, 2, FS], f32, a)
    aS = sb("aS", [P, 2, SC * SH], f32, a)
    aSTH = sb("aSTH", [SH, 2, SC * P], f32r, a)
    aSTL = sb("aSTL", [SH, 2, SC * P], f32r, a)
    V = sb("V", [P, 2, 2, H, 32], f32)
    stg = [sb(n, [P, 2, SEQ], f32r) for n in ("qhi", "qlo", "khi", "klo")]
    r_at = region(16384)
    a = within(r_at)
    OTs = sb("OTs", [P, 2, SEQ], f32, a)
    On = sb("On", [P, 2, 2, D], f32, a)
    OnTH = sb("OnTH", [P, DC, SEQ], f32r, a)
    OnTL = sb("OnTL", [P, DC, SEQ], f32r, a)
    a = within(r_at)
    oh = sb("oh", [P, TILES * K, E], bf16, a)
    fill = sb("fill", [P, 2, ROW], f32, a)
    bo = sb("bo", [P, D], f32, a)
    a = within(r_xt)
    GH = [sb(f"GH{s}", [P, GO], f32r, a) for s in range(2)]
    GL = [sb(f"GL{s}", [P, GO], f32r, a) for s in range(2)]
    DH = [sb(f"DH{s}", [FH, 2 * D], f32r, a) for s in range(2)]
    DL = [sb(f"DL{s}", [FH, 2 * D], f32r, a) for s in range(2)]
    a = within(r_xe)
    xin = sb("xin", [P, 4, 2, ROW], f32, a)
    xTH = [sb(f"xTH{s}", [P, DC, SLOTS], f32r, a) for s in range(2)]
    xTL = [sb(f"xTL{s}", [P, DC, SLOTS], f32r, a) for s in range(2)]
    a = within(r_qk)
    sg = sb("sg", [P, 2, 2, F], f32, a)
    act = sb("act", [P, 2, 2, F], f32, a)
    aTH = [sb(f"aTH{s}", [FH, 2, SLOTS], f32r, a) for s in range(2)]
    aTL = [sb(f"aTL{s}", [FH, 2, SLOTS], f32r, a) for s in range(2)]
    y = sb("y", [P, 4, 2, D], f32, a)
    ov_x = sb("ov_x", [P, ROW], f32, a)
    ov_xT = sb("ov_xT", [P, DC, P], f32, a)
    ov_a = sb("ov_a", [P, 2, F], f32, a)
    ov_aT = sb("ov_aT", [FH, 2, P], f32, a)
    ov_y = sb("ov_y", [P, D], f32, a)
    ov_c = sb("ov_c", [P, 4], f32, a)
    ov_id = sb("ov_id", [P, 2], i32, a)
    ov_cmp = sb("ov_cmp", [P, OVT, E], f32, within(r_xt))
    ov_e = sb("ov_e", [P, OVT], f32, within(r_xe))
    ov_ei = sb("ov_ei", [P, OVT], i32, within(r_xe, OVT * 4 + 32))

    PB = [nc.alloc_psum_tensor(f"bank{i}", [P, 512], f32) for i in range(8)]
    S_B, T_B, OT_B, A_B = (0, 1), (2, 3), (4, 7), (5, 6)
    RT_B = S_B + OT_B
    GT = TILES // 4

    def sem(name):
        return nc.alloc_semaphore(name)

    x_in = [sem(f"x_in{g}") for g in range(4)]
    wq_in, w_in0, b_in = sem("wqkv_in"), sem("weights_in"), sem("bias_in")
    const_ok = sem("const_ok")
    var_ok, sqrt_ok, xn_ok = sem("var_ok"), sem("sqrt_ok"), sem("xn_ok")
    chain = sem("vector_chain")
    pchain = sem("pool_chain")
    wsh_ok, wsl_ok, wsl2_ok = sem("static_hi_ok"), sem("qkv_lo_ok"), sem("other_lo_ok")
    lt_full, lt_ok = sem("logitsT_full"), sem("logitsT_ok")
    run_ok, prod_ok, prod_free = sem("ranks_ok"), sem("rank_product_ok"), sem("rank_product_used")
    rank_read, oh_ok, mask_ok, tile_ranks_ok = (sem("rank_base_read"), sem("onehot_ok"), sem("mask_ok"),
                                                sem("tile_ranks_ok"))
    a_full, a_hi, a_free = sem("a_full"), sem("a_hi"), sem("a_free")
    lg_full, lg_ok, dlt_ok, ex_ok = sem("logits_full"), sem("logits_ok"), sem("delta_ok"), sem("exp_ok")
    sum_ok = sem("masksum_ok")
    route_ok, fill_in, fill_free = sem("route_ok"), sem("fill_in"), sem("fill_free")
    xbo_ok = sem("x_plus_bo_ok")
    sgu_full, ssilu_ok, sact_ok = sem("shared_gu_full"), sem("shared_silu_ok"), sem("shared_act_ok")
    sat_hi, sat_ok = sem("shared_actT_hi"), sem("shared_actT_ok")
    stg_q, stg_k, qk_w = sem("q_staged"), sem("k_staged"), sem("qk_written")
    qk_in = [sem(f"qk_in{s}") for s in range(3)]
    m_in = [sem(f"m_in{s}") for s in range(3)]
    s_full, max_ok, st_full, exp_ok = sem("s_full"), sem("max_ok"), sem("st_full"), sem("prob_ok")
    pv_ok, ot_ok, norm_ok = sem("pv_ok"), sem("ot_ok"), sem("norm_ok")
    v_ok, m_ok, m_w = sem("v_ok"), sem("m_ok"), sem("m_written")
    ont_ok, base_ok, out_w = sem("onT_ok"), sem("base_ok"), sem("out_written")
    scat_in = sem("rows_scattered")
    w_in = [sem(f"w_in{s}") for s in range(4)]
    r_in = [sem(f"rows_in{s}") for s in range(4)]
    guH_ok, gu_split, wd_split = sem("guH_ok"), sem("gu_split"), sem("wd_split")
    xt_full, xtH_ok, xt_ok = sem("xt_full"), sem("xtH_ok"), sem("xt_ok")
    gu_full, silu_ok, mul_ok = sem("gu_full"), sem("silu_ok"), sem("mul_ok")
    at_full, atH_ok, at_ok = sem("at_full"), sem("atH_ok"), sem("at_ok")
    dn_full, y_ok, scat, y_free = sem("dn_full"), sem("y_ok"), sem("added"), sem("y_free")
    wcol_ok, w_step, dh_ok = sem("wcol_ok"), sem("wcol_step"), sem("down_hi_ok")
    ov_e_ok, ov_in, ov_xT_full, ov_xT_ok = sem("ov_e_ok"), sem("ov_in"), sem("ov_xT_full"), sem("ov_xT_ok")
    ov_gu, ov_silu, ov_mul, ov_at = sem("ov_gu"), sem("ov_silu"), sem("ov_mul"), sem("ov_at")
    ov_s = sem("ov_step")
    ov_at_ok, ov_dn, ov_y_ok, ov_add, ov_w = (sem("ov_at_ok"), sem("ov_dn"), sem("ov_y_ok"),
                                              sem("ov_add"), sem("ov_w"))

    def extra(n):
        b, s = divmod(n, H)
        kind, b = {2: ("q", b + 3), 3: ("k", b + 3), 7: ("onT", b - 1), 9: ("mT", b + 1), 11: ("o", b - 1),
                   14: ("v", b + 1)}.get(s, (None, 0))
        return (kind, b) if kind and 0 <= b < B else None

    def nat(n):
        g = n // 4 - 2
        return ("nt", g) if n % 4 == 0 and 0 <= g < HEADS // 4 else None

    def lead_heads(t):
        first = 2 * (t - LEAD_FROM)
        return range(first, min(first + 2, LEAD)) if t >= LEAD_FROM else range(0)

    ONES_ROWS = (3 * HD, 64 + 3 * HD)

    def s_bank(n):
        return PB[S_B[n % 2] if n < LEAD else (S_B + OT_B[1:])[(n - LEAD) % 3]]

    G0_SLOT, X0_SLOT, UP0_SLOT = HEADS - 16, HEADS - 6, HEADS + 3

    def x_bank(i, c):
        return PB[(S_B[1], T_B[0])[c] if isinstance(i, int) and i == 0 and c < 2 else A_B[0]]

    def slot_uses(n):
        return [u for u in (nat(n), extra(n)) if u]

    SLOT_END = HEADS + 13
    uses = [("xt", i) for i in range(TILES // 2)]
    uses += [("q", 0), ("k", 0), ("v", 0)]
    for t in range(TILES):
        uses += [("sT", t)] + ([BESIDE[t]] if t in BESIDE else []) + ([("sY", t - 1)] if t else [])
    uses += [("sY", TILES - 1)]
    for n in range(SLOT_END):
        uses += slot_uses(n)
    USE = {u: i for i, u in enumerate(uses)}

    def bank_of(u):
        return PB[A_B[USE[u] % 2]]

    def static(w, off, c, width, lo, n):
        s = off + c * width + lo
        return w[:, s:s + n]

    def raw32(ap):
        return ap.bitcast(f32)

    IDENT_OK, FILL_OK, CONSTS = 1, 2, 3
    x_v = x.rearrange("(t p) c -> p t c", p=P)
    out_v = out[0:TOK, :].rearrange("(t p) c -> p t c", p=P)
    SPARE = out.shape[0] - TOK
    assert SPARE == SLOTS

    def load_w(sp, c, i, e):
        if e is None:
            sp.wait_ge(gu_split, BODY * i + (c - 3))
            sp.wait_ge(wd_split, BODY * i + (c - 3))
        elif e == 0:
            sp.wait_ge(route_ok, 1)
        o = c % 4 * WN
        if e is None:
            sg_, sd_ = wgu[bass.ds(BODY * i + c, 1), :, :], wd[bass.ds(BODY * i + c, 1), :, :]
        else:
            sg_, sd_ = wgu[e:e + 1, :, :], wd[e:e + 1, :, :]
        sp.dma_start(raw[:, o:o + GO], sg_.rearrange("a p n -> (a p) n")).then_inc(w_in[c % 4], 16)
        sp.dma_start(raw[0:FH, o + GO:o + WN], sd_.rearrange("a p n -> (a p) n")).then_inc(w_in[c % 4], 16)

    def load_rows(sp, c, i, e):
        if e is None:
            sp.wait_ge(xt_full, BODY * i + (c - 3))
            sp.wait_ge(wcol_ok, BODY * i + (c - 3))
            src = xs_d[bass.ds((BODY * i + c) * SLOTS, SLOTS), :]
        else:
            if e == 0:
                sp.wait_ge(scat_in, 16 * TILES * K)
            src = xs_d[e * SLOTS:(e + 1) * SLOTS, :]
        sp.dma_start(xin[:, c % 4, :, :], src.rearrange("(j p) n -> p j n", p=P)).then_inc(r_in[c % 4], 16)

    block_cm = nc.Block()
    block = block_cm.__enter__()

    @block.sync
    def _(sp):
        sp.dma_start(base[:, 0:4, :], x_v[:, 0:4, :]).then_inc(x_in[0], 16)
        sp.dma_start(raw[:, O_GATE:O_QKV].rearrange("p (c n) -> p c n", c=DC), gate).then_inc(wq_in, 16)
        sp.dma_start(raw[:, O_QKV:O_WO].rearrange("p (c n) -> p c n", c=DC), wqkv).then_inc(wq_in, 16)
        for g in range(1, 4):
            sp.dma_start(base[:, 4 * g:4 * g + 4, :], x_v[:, 4 * g:4 * g + 4, :]).then_inc(x_in[g], 16)
        sp.dma_start(bq[:, :], bqk).then_inc(b_in, 16)
        sp.dma_start(bv[:, :], bvo[0:1, :].broadcast_to([P, D])).then_inc(b_in, 16)
        sp.dma_start(bo[:, :], bvo[1:2, :].broadcast_to([P, D])).then_inc(b_in, 16)
        sp.dma_start(raw[:, O_WO:O_SGU].rearrange("p (c n) -> p c n", c=DC), wo).then_inc(w_in0, 16)
        sp.dma_start(raw[:, O_SGU:O_SD].rearrange("p (c n) -> p c n", c=DC), wsgu).then_inc(w_in0, 16)
        sp.dma_start(raw[0:SH, O_SD:NST].rearrange("p (c n) -> p c n", c=SC), wsd).then_inc(w_in0, 16)

        FILLS = 16
        per = E // FILLS
        xs_v = xs_d[0:REG, :].rearrange("(e j p) c -> p e j c", j=2, p=P)

        def fill_part(i):
            for e in range(per * i, per * i + per):
                sp.dma_start(xs_v[:, e, :, :], fill[:, :, :]).then_inc(fill_in, 16)

        def qk_write(b):
            for w, (s0, ready) in enumerate(((0, stg_q), (2, stg_k))):
                sp.wait_ge(ready, b + 1)
                for s in (s0, s0 + 1):
                    sp.dma_start(qk_d[b, s].rearrange("(k p) q -> p k q", p=P), raw32(stg[s][:, :, :]))\
                      .then_inc(qk_w, 16)

        def qk_read(b):
            s = b % 3
            sp.wait_ge(qk_w, 64 * (b + 1))
            if b == 0:
                sp.wait_ge(const_ok, CONSTS)
            if b == 2:
                sp.wait_ge(a_full, USE[("sY", TILES - 1)] + 1)
                for row in ONES_ROWS:
                    sp.dma_start(raw32(KS[2][row:row + 1, :, :]), raw32(KS[0][row:row + 1, :, :]))\
                      .then_inc(qk_in[2], 16)
            if b >= 3:
                sp.wait_ge(st_full, H * (b - 2))
            for par in range(2):
                for dst, parts in ((QS[s], (0, 1, 0)), (KS[s], (2, 2, 3))):
                    for r, part in enumerate(parts):
                        src = qk_d[b, part].rearrange("(k r d) q -> r d k q", r=2, d=HD)[par]
                        lo = 64 * par + HD * r
                        sp.dma_start(raw32(dst[lo:lo + HD, :, :]), src).then_inc(qk_in[s], 16)

        def m_move(b):
            sp.wait_ge(m_ok, b + 1)
            sp.dma_start(m_d[b], raw32(mTs[:, :])).then_inc(m_w, 16)
            sp.wait_ge(m_w, 16 * (b + 1))
            for par in range(2):
                src = m_d[b].rearrange("(k r) q -> r k q", r=2)[par:par + 1]
                lo = 64 * par + 3 * HD
                sp.dma_start(raw32(QS[b % 3][lo:lo + 1, :, :]), src).then_inc(m_in[b % 3], 16)

        sp.wait_ge(const_ok, FILL_OK)
        sp.dma_start(out[TOK:TOK + SPARE, :].rearrange("(j p) c -> p j c", p=P), fill[:, :, 0:D])\
          .then_inc(out_w, 16)
        for b in range(2):
            for i in range(6 * b, 6 * b + 6):
                fill_part(i)
            qk_write(b)
            qk_read(b)
        for i in range(12, FILLS):
            fill_part(i)
        qk_write(2)
        m_move(0)
        qk_read(2)
        for b in range(B + 1):
            if b + 3 < B:
                qk_write(b + 3)
            if b + 1 < B:
                m_move(b + 1)
            if b == B - 1:
                for e in range(4):
                    load_rows(sp, e, 0, e)
            if b >= 1:
                sp.wait_ge(base_ok, b)
                sp.dma_start(out_v[:, 2 * b - 2:2 * b, :], base[:, 2 * b - 2:2 * b, :]).then_inc(out_w, 16)
            if b + 3 < B:
                qk_read(b + 3)
            if b in (B // 2, B // 2 + 1):
                for e in range(2 * b - B, 2 * b - B + 2):
                    load_w(sp, e, 0, e)
        for c in range(4, BODY):
            load_w(sp, c, 0, None)
            load_rows(sp, c, 0, None)
        with sp.Fori(1, E // BODY, 1) as i:
            for c in range(BODY):
                load_w(sp, c, i, None)
                load_rows(sp, c, i, None)
        sp.wait_ge(out_w, 16 * (B + 1))
        sp.wait_ge(y_free, E + 1)
        over = sp.value_load(nov_i[0:1, 0:1], min_val=0, max_val=OVT)
        with sp.If(over > 0):
            sp.wait_ge(ov_e_ok, 1)
            with sp.Fori(0, OVT, 1) as j:
                with sp.If(over > j):
                    e = sp.value_load(ov_ei[0:1, bass.ds(j, 1)], min_val=0, max_val=E - 1)
                    sp.wait_ge(ov_w, j + 1)
                    sp.dma_start(raw[:, 0:GO], wgu[bass.ds(e, 1), :, :].rearrange("a p n -> (a p) n"))\
                      .then_inc(ov_in, 16)
                    sp.dma_start(raw[0:FH, GO:WN], wd[bass.ds(e, 1), :, :].rearrange("a p n -> (a p) n"))\
                      .then_inc(ov_in, 16)
                    sp.dma_start(ov_x[:, :], xs_d[bass.ds(j * P + REG, P), :]).then_inc(ov_in, 16)
            sp.wait_ge(ov_w, OVT + 1)
        sp.wait_ge(out_w, 16 * (B + 1))

    @block.gpsimd
    def _(pool):
        n = [0]

        def link(ins):
            n[0] += 1
            ins.then_inc(pchain, 1)
            pool.wait_ge(pchain, n[0])

        link(pool.memset(ident[:, :], 0.0))
        pool.affine_select(out=ident[:, :], in_=ident[:, :], compare_op=ALU.not_equal, fill=1.0,
                           base=0, pattern=[[-1, P]], channel_multiplier=1).then_inc(const_ok, 1)
        link(pool.memset(fill[:, :, :], 0.0))
        pool.iota(fill[:, :, C_TOK:C_TOK + 1].bitcast(i32), pattern=[[P, 2], [0, 1]], base=TOK,
                  channel_multiplier=1).then_inc(const_ok, 1)
        link(pool.memset(ones[:, :], 1.0))
        link(pool.affine_select(out=before[:, :], in_=ones[:, :], compare_op=ALU.is_gt, fill=0.0,
                                base=0, pattern=[[1, P]], channel_multiplier=-1))
        link(pool.iota(iota_e[:, :], pattern=[[1, E]], base=0, channel_multiplier=0,
                       allow_small_or_imprecise_dtypes=True))
        link(pool.iota(ecur[:, :], pattern=[[1, 4]], base=-4, channel_multiplier=0,
                       allow_small_or_imprecise_dtypes=True))
        link(pool.memset(XE[:, :, C_TOK + 1:ROW], 0.0))
        link(pool.iota(XE[:, :, C_TOK:C_TOK + 1].bitcast(i32), pattern=[[P, TILES], [0, 1]], base=0,
                       channel_multiplier=1))
        link(pool.memset(aS[:, :, FS:SC * SH], 0.0))
        link(pool.memset(V[:, :, :, :, HD:32], 0.0))
        link(pool.memset(V[:, :, :, :, HD:HD + 1], 1.0))
        for s in range(2):
            for lo in (32, 96):
                last = pool.memset(raw32(KS[s][lo:lo + 32, :, :]), 1.0)
        last.then_inc(const_ok, 1)

        pool.wait_ge(wsh_ok, 2)
        pool.wait_ge(const_ok, CONSTS)
        link(pool.tensor_tensor(WSL[:, O_WO:O_SD], raw[:, O_WO:O_SD], raw32(WSH[:, O_WO:O_SD]),
                                ALU.subtract))
        pool.tensor_tensor(WSL[0:SH, O_SD:NST], raw[0:SH, O_SD:NST], raw32(WSH[0:SH, O_SD:NST]),
                           ALU.subtract).then_inc(wsl2_ok, 1)
        pool.wait_ge(wsl2_ok, 1)

        pool.wait_ge(b_in, 48)
        pool.wait_ge(xn_ok, TILES)
        for t in range(TILES):
            pool.tensor_tensor(base[:, t, :], base[:, t, :], bo[:, :], ALU.add).then_inc(xbo_ok, 1)

        mask_v = oh[:, :, :].rearrange("p (t k) e -> p k t e", k=K)
        for g in range(2):
            t = slice(8 * g, 8 * g + 8)
            pool.wait_ge(oh_ok, g + 1)
            acc = mask_v[:, 0, t, :]
            for k in range(1, K):
                add = pool.tensor_tensor(mask[:, t, :], acc, mask_v[:, k, t, :], ALU.add)
                acc = mask[:, t, :]
                if k < K - 1:
                    link(add)
            add.then_inc(mask_ok, 1)
        pool.wait_ge(rank_read, 1)
        for t in range(1, TILES):
            link(pool.tensor_tensor(run[:, t, :], run[:, t - 1, :], mask[:, t - 1, :], ALU.add))
        pool.sem_inc(tile_ranks_ok, 1)
        for g in range(TILES // 2):
            pool.wait_ge(run_ok, g // 4 + 1)
            if g >= 2:
                pool.wait_ge(prod_free, g - 1)
            pool.tensor_tensor(
                prod[:, g % 2, :, :].rearrange("p (t k) e -> p t k e", k=K),
                oh[:, 2 * g * K:2 * (g + 1) * K, :].rearrange("p (t k) e -> p t k e", k=K),
                run[:, 2 * g:2 * g + 2, :].rearrange("p t (a e) -> p t a e", a=1)
                .broadcast_to([P, 2, K, E]), ALU.mult).then_inc(prod_ok, 1)

        pool.wait_ge(route_ok, 1)
        over = pool.value_load(nov_i[0:1, 0:1], min_val=0, max_val=OVT)
        with pool.If(over > 0):
            xo_v = xs_d[REG:REG + OVT * P, :].rearrange("(j p) c -> p j c", p=P)
            with pool.Fori(0, OVT, 1) as j:
                pool.dma_start(xo_v[:, bass.ds(j, 1), :], fill[:, 0:1, :]).then_inc(ov_add, 16)
            pool.wait_ge(ov_add, 16 * OVT)
        pool.sem_inc(fill_free, 1)
        pool.wait_ge(fill_in, 16 * E)
        for t in range(TILES):
            for k in range(K):
                i = t * K + k
                pool.indirect_dma_start(xs_d, bass.IndirectOffsetOnAxis(ap=posi[:, i:i + 1], axis=0),
                                        XE[:, t, :], None).then_inc(scat_in, 16)

        pool.sem_inc(y_free, 1)

        def add(i, c, first=False, second=False):
            pool.wait_ge(y_ok, 2 * BODY * i + (2 * c + 2))
            if first:
                pool.wait_ge(out_w, 16 * (B + 1))
            else:
                pool.wait_ge(scat, 32 * BODY * i + 32 * c)
                pool.sem_inc(y_free, 1)
            for j in range(2):
                pool.indirect_dma_start(out, bass.IndirectOffsetOnAxis(ap=ids[:, c % 4, j:j + 1], axis=0),
                                        y[:, c % 4, j, :], None, compute_op=ALU.add).then_inc(scat, 16)

        for c in range(BODY):
            add(0, c, first=c == 0)
        with pool.Fori(1, E // BODY, 1) as i:
            for c in range(BODY):
                add(i, c)
        pool.wait_ge(scat, 32 * E)
        pool.sem_inc(y_free, 1)
        over = pool.value_load(nov_i[0:1, 0:1], min_val=0, max_val=OVT)
        with pool.If(over > 0):
            pool.sem_inc(ov_w, 1)
            with pool.Fori(0, OVT, 1) as j:
                with pool.If(over > j):
                    pool.wait_ge(ov_y_ok, j + 1)
                    pool.sem_inc(pchain, 1)
                    pool.indirect_dma_start(out, bass.IndirectOffsetOnAxis(ap=ov_id[:, 0:1], axis=0),
                                            ov_y[:, :], None, compute_op=ALU.add).then_inc(ov_add, 16)
                    pool.wait_ge(ov_add, 16 * j + 16 * (OVT + 1))
                pool.sem_inc(ov_w, 1)
            pool.wait_ge(ov_w, OVT + 1)
        pool.wait_ge(scat, 32 * E)

    @block.tensor
    def _(pe):
        def product(dst, lh, ll, rh, rl, first=True, last=True):
            pe.matmul(dst, lhsT=lh, rhs=rh, start=first, stop=False)
            pe.matmul(dst, lhsT=lh, rhs=rl, start=False, stop=False)
            return pe.matmul(dst, lhsT=ll, rhs=rh, start=False, stop=last)

        def claim(u):
            if USE[u] >= 2:
                pe.wait_ge(a_free, USE[u] - 1)
            return bank_of(u)

        def xt_tiles(i):
            pe.wait_ge(xn_ok, 2 * i + 2)
            bk = claim(("xt", i))
            for c in range(DC):
                for j in range(2):
                    last = pe.transpose(bk[:, (2 * c + j) * P:(2 * c + j + 1) * P],
                                        in_=XE[:, 2 * i + j, c * P:(c + 1) * P], identity=ident[:, :])
            last.then_inc(a_full, 1)

        def project(which, b):
            u = (which, b)
            bk = claim(u)
            col = 0 if which == "q" else D
            for k in range(2):
                for c in range(DC):
                    last = product(bk[:, k * SEQ:(k + 1) * SEQ],
                                   static(WSH, O_QKV, c, 3 * D, col + k * P, P),
                                   static(WSL, O_QKV, c, 3 * D, col + k * P, P),
                                   XH[:, c, b * SEQ:(b + 1) * SEQ], XL[:, c, b * SEQ:(b + 1) * SEQ],
                                   c == 0, c == DC - 1)
            last.then_inc(a_full, 1)

        def values(b):
            bk = claim(("v", b))
            for j in range(2):
                for c in range(DC):
                    t = slice((2 * b + j) * P, (2 * b + j + 1) * P)
                    last = product(bk[:, j * D:(j + 1) * D], XH[:, c, t], XL[:, c, t],
                                   static(WSH, O_QKV, c, 3 * D, 2 * D, D),
                                   static(WSL, O_QKV, c, 3 * D, 2 * D, D), c == 0, c == DC - 1)
            last.then_inc(a_full, 1)

        def scores(n):
            b, h = divmod(n, H)
            k, lo = h // 2, 64 * (h % 2)
            if h == 0:
                pe.wait_ge(qk_in[b % 3], 192 * (b // 3 + 1) + (32 if b % 3 == 2 else 0))
            if n == LEAD:
                pe.wait_ge(sact_ok, TILES)
            if n >= 2:
                pe.wait_ge(max_ok, n - 1 if n < LEAD else n if n < LEAD + 3 else n - 2)
            for j in range(2):
                last = pe.matmul(s_bank(n)[:, j * SEQ:(j + 1) * SEQ],
                                 lhsT=QS[b % 3][lo:lo + 3 * HD, k, j * P:(j + 1) * P],
                                 rhs=KS[b % 3][lo:lo + 3 * HD, k, :], start=True, stop=True)
            last.then_inc(s_full, 1)

        def scores_t(n):
            b, h = divmod(n, H)
            k, lo = h // 2, 64 * (h % 2)
            if h == 0:
                pe.wait_ge(m_in[b % 3], 32 * (b // 3 + 1))
            if n == 0:
                pe.wait_ge(sact_ok, TILES)
            if n >= 2:
                pe.wait_ge(exp_ok, n - 1)
            for j in range(2):
                last = pe.matmul(PB[T_B[n % 2]][:, j * SEQ:(j + 1) * SEQ],
                                 lhsT=KS[b % 3][lo:lo + 3 * HD + 1, k, j * P:(j + 1) * P],
                                 rhs=QS[b % 3][lo:lo + 3 * HD + 1, k, :], start=True, stop=True)
            last.then_inc(st_full, 1)

        def weigh(g):
            b = g // 4
            pe.wait_ge(exp_ok, 4 * g + 4)
            if g % 4 == 0:
                pe.wait_ge(v_ok, b + 1)
            if g >= 1:
                pe.wait_ge(ot_ok, g)
            for j in range(2):
                for m in range(4):
                    last = pe.matmul(PB[OT_B[0]][32 * m:32 * m + 32, 0:SEQ],
                                     lhsT=V[:, b % 2, j, (4 * g + m) % H, :],
                                     rhs=EX[g % 2][:, m, j * SEQ:(j + 1) * SEQ], start=j == 0, stop=j == 1)
            last.then_inc(pv_ok, 1)

        def natural(g):
            pe.wait_ge(ot_ok, g + 1)
            bk = claim(("nt", g))
            for j in range(2):
                last = pe.transpose(bk[:, j * P:(j + 1) * P], in_=OTs[:, g % 2, j * P:(j + 1) * P],
                                    identity=ident[:, :])
            last.then_inc(a_full, 1)

        def neg_max_t(b):
            pe.wait_ge(max_ok, H * (b + 1))
            bk = claim(("mT", b))
            for j in range(2):
                last = pe.transpose(bk[0:H, j * P:(j + 1) * P], in_=mx[:, b % 2, j, :],
                                    identity=ident[:, :])
            last.then_inc(a_full, 1)

        def out_t(b):
            pe.wait_ge(norm_ok, 4 * b + 4)
            bk = claim(("onT", b))
            for c in range(DC):
                for j in range(2):
                    last = pe.transpose(bk[:, (2 * c + j) * P:(2 * c + j + 1) * P],
                                        in_=On[:, b % 2, j, c * P:(c + 1) * P], identity=ident[:, :])
            last.then_inc(a_full, 1)

        def out_proj(b):
            pe.wait_ge(ont_ok, b + 1)
            bk = claim(("o", b))
            for j in range(2):
                for c in range(DC):
                    last = product(bk[:, j * D:(j + 1) * D], OnTH[:, c, j * P:(j + 1) * P],
                                   OnTL[:, c, j * P:(j + 1) * P], static(WSH, O_WO, c, D, 0, D),
                                   static(WSL, O_WO, c, D, 0, D), c == 0, c == DC - 1)
            last.then_inc(a_full, 1)

        def router(g):
            pe.wait_ge(a_free, 2 * g + 2)
            tt = slice(g * GT * P, (g + 1) * GT * P)
            for c in range(DC):
                last = product(PB[RT_B[g]][0:E, :], static(WSH, O_GATE, c, E, 0, E),
                               static(WSL, O_GATE, c, E, 0, E), XH[:, c, tt], XL[:, c, tt],
                               c == 0, c == DC - 1)
            last.then_inc(lt_full, 1)

        def logits(g):
            pe.wait_ge(lt_ok, g + 1)
            for t in range(GT * g, GT * g + GT):
                last = pe.transpose(PB[T_B[t // 8]][:, (t % 8) * E:(t % 8 + 1) * E],
                                    in_=LT[:, t * P:(t + 1) * P], identity=ident[0:E, 0:E])
            if g % 2:
                last.then_inc(lg_full, 1)

        def rank_base():
            pe.wait_ge(sum_ok, 1)
            bk = claim(("rk", 0))
            pe.matmul(bk[:, 0:E], lhsT=before[:, :], rhs=masksum[:, :], start=True, stop=True)
            pe.matmul(bk[:, E:2 * E], lhsT=ones[:, :], rhs=masksum[:, :], start=True, stop=True)\
              .then_inc(a_full, 1)

        pe.wait_ge(const_ok, IDENT_OK)
        for i in range(4):
            xt_tiles(i)
        pe.wait_ge(wsl_ok, 1)
        router(0)
        xt_tiles(4)
        xt_tiles(5)
        router(1)
        logits(0)
        xt_tiles(6)
        xt_tiles(7)
        router(2)
        logits(1)
        router(3)
        project("q", 0)
        logits(2)
        logits(3)
        project("k", 0)
        values(0)

        pe.wait_ge(wsl2_ok, 1)
        pe.wait_ge(lg_ok, 2)

        def shared_up(t, half):
            if t >= 2:
                pe.wait_ge(sact_ok, t - 1)
            bk = PB[(T_B, OT_B)[t % 2][half]]
            for c in range(DC):
                tt = slice(t * P, (t + 1) * P)
                last = product(bk[:, 0:FS], XH[:, c, tt], XL[:, c, tt],
                               static(WSH, O_SGU, c, 2 * FS, half * FS, FS),
                               static(WSL, O_SGU, c, 2 * FS, half * FS, FS), c == 0, c == DC - 1)
            last.then_inc(sgu_full, 1)

        def shared_down(t):
            pe.wait_ge(sact_ok, t + 1)
            bk = claim(("sT", t))
            for c in range(SC):
                last = pe.transpose(bk[0:SH, c * P:(c + 1) * P], in_=aS[:, t % 2, c * SH:(c + 1) * SH],
                                    identity=ident[:, :])
            last.then_inc(a_full, 1)

        def shared_out(t):
            pe.wait_ge(sat_ok, t + 1)
            bk = claim(("sY", t))
            for c in range(SC):
                last = product(bk[:, 0:D], aSTH[:, t % 2, c * P:(c + 1) * P],
                               aSTL[:, t % 2, c * P:(c + 1) * P],
                               static(WSH, O_SD, c, D, 0, D)[0:SH], static(WSL, O_SD, c, D, 0, D)[0:SH],
                               c == 0, c == SC - 1)
            last.then_inc(a_full, 1)

        shared_up(0, 0)
        shared_up(0, 1)
        for t in range(TILES):
            now = lead_heads(t)
            if t + 1 < TILES:
                shared_up(t + 1, 0)
            for n in now[0:1]:
                scores(n)
            if t + 1 < TILES:
                shared_up(t + 1, 1)
            for n in now[1:2]:
                scores(n)
            shared_down(t)
            if t in BESIDE:
                kind, b = BESIDE[t]
                if kind == "mT":
                    neg_max_t(b)
                elif kind == "rk":
                    rank_base()
                else:
                    project(kind, b)
            if t:
                shared_out(t - 1)
        shared_out(TILES - 1)

        AT_B, Y_B = A_B[1], OT_B

        def wait(s, v):
            if not (isinstance(v, int) and v <= 0):
                pe.wait_ge(s, v)

        def rows_t(i, c):
            wait(r_in[c % 4], 16 * (BODY // 4 * i + c // 4) + 16)
            wait(xt_ok, BODY * i + c)
            for k in range(DC):
                for j in range(2):
                    last = pe.transpose(x_bank(i, c)[:, (2 * k + j) * P:(2 * k + j + 1) * P],
                                        in_=xin[:, c % 4, j, k * P:(k + 1) * P], identity=ident[:, :])
            last.then_inc(xt_full, 1)

        def up(i, c, j):
            s = c % 2
            wait(xt_ok, BODY * i + c + 1)
            wait(gu_split, BODY * i + c + 1)
            wait(mul_ok, 2 * BODY * i + 2 * (c - 2) + j + 1)
            for k in range(DC):
                last = product(PB[2 * s + j][:, 0:GN], xTH[s][:, k, j * P:(j + 1) * P],
                               xTL[s][:, k, j * P:(j + 1) * P], GH[s][:, k * GN:(k + 1) * GN],
                               GL[s][:, k * GN:(k + 1) * GN], k == 0, k == DC - 1)
            last.then_inc(gu_full, 1)

        def act_t(i, c):
            wait(mul_ok, 2 * BODY * i + 2 * c + 2)
            wait(at_ok, BODY * i + c)
            for k in range(2):
                for j in range(2):
                    last = pe.transpose(PB[AT_B][0:FH, (2 * k + j) * P:(2 * k + j + 1) * P],
                                        in_=act[:, c % 2, j, k * FH:(k + 1) * FH], identity=ident[:, :])
            last.then_inc(at_full, 1)

        def down(i, c):
            s = c % 2
            wait(at_ok, BODY * i + c + 1)
            wait(wd_split, BODY * i + c + 1)
            wait(y_ok, 2 * BODY * i + 2 * (c - 2) + 2)
            for j in range(2):
                for k in range(2):
                    last = product(PB[Y_B[s]][:, j * D:(j + 1) * D], aTH[s][:, k, j * P:(j + 1) * P],
                                   aTL[s][:, k, j * P:(j + 1) * P], DH[s][:, k * D:(k + 1) * D],
                                   DL[s][:, k * D:(k + 1) * D], k == 0, k == 1)
            last.then_inc(dn_full, 1)

        def step(i, c, first=False, last=False):
            if not first:
                act_t(i, c - 1)
            up(i, c, 0)
            if not last:
                rows_t(i, c + 1)
            up(i, c, 1)
            if not first:
                down(i, c - 1)

        for n in range(SLOT_END):
            if n < HEADS:
                scores_t(n)
            if n + LEAD < HEADS:
                scores(n + LEAD)
            if n % 4 == 1 and 5 <= n < HEADS + 5:
                weigh(n // 4 - 1)
            if nat(n):
                natural(nat(n)[1])
            if n == X0_SLOT:
                pe.wait_ge(max_ok, HEADS)
                rows_t(0, 0)
            elif n == UP0_SLOT:
                up(0, 0, 0)
            elif n == UP0_SLOT + 1:
                pe.wait_ge(exp_ok, HEADS)
                rows_t(0, 1)
            elif n == UP0_SLOT + 2:
                up(0, 0, 1)
            elif n == UP0_SLOT + 3:
                up(0, 1, 0)
            elif n == UP0_SLOT + 5:
                up(0, 1, 1)
            u = extra(n)
            if u:
                kind, b = u
                if kind in "qk":
                    project(kind, b)
                elif kind == "v":
                    values(b)
                elif kind == "mT":
                    neg_max_t(b)
                elif kind == "onT":
                    out_t(b)
                else:
                    out_proj(b)

        pe.wait_ge(norm_ok, HEADS // 4)
        pe.wait_ge(ot_ok, HEADS // 4)
        pe.wait_ge(a_free, len(uses))
        act_t(0, 0)
        rows_t(0, 2)
        down(0, 0)
        for c in range(2, BODY):
            step(0, c)
        with pe.Fori(1, E // BODY - 1, 1) as i:
            for c in range(BODY):
                step(i, c)
        for c in range(BODY):
            step(E // BODY - 1, c, last=c == BODY - 1)
        act_t(E // BODY - 1, BODY - 1)
        down(E // BODY - 1, BODY - 1)

        over = pe.value_load(nov_i[0:1, 0:1], min_val=0, max_val=OVT)
        with pe.If(over > 0):
            with pe.Fori(0, OVT, 1) as j:
                with pe.If(over > j):
                    pe.wait_ge(ov_in, 48 * j + 48)
                    for k in range(DC):
                        last = pe.transpose(PB[0][:, k * P:(k + 1) * P], in_=ov_x[:, k * P:(k + 1) * P],
                                            identity=ident[:, :])
                    last.then_inc(ov_xT_full, 1)
                    pe.wait_ge(ov_xT_ok, j + 1)
                    for k in range(DC):
                        last = pe.matmul(PB[1][:, 0:GN], lhsT=ov_xT[:, k, :], rhs=raw[:, k * GN:(k + 1) * GN],
                                         start=k == 0, stop=k == DC - 1)
                    last.then_inc(ov_gu, 1)
                    pe.wait_ge(ov_mul, j + 1)
                    for k in range(2):
                        last = pe.transpose(PB[2][0:FH, k * P:(k + 1) * P], in_=ov_a[:, 1, k * FH:(k + 1) * FH],
                                            identity=ident[:, :])
                    last.then_inc(ov_at, 1)
                    pe.wait_ge(ov_at_ok, j + 1)
                    for k in range(2):
                        last = pe.matmul(PB[3][:, 0:D], lhsT=ov_aT[:, k, :],
                                         rhs=raw[0:FH, GO + k * D:GO + (k + 1) * D], start=k == 0, stop=k == 1)
                    last.then_inc(ov_dn, 1)
            pe.wait_ge(ov_w, OVT + 1)

    @block.scalar
    def _(sc):
        def high(u, dst, src):
            sc.wait_ge(a_full, USE[u] + 1)
            return nc.scalar.activation(dst, src, ACT.Copy)

        def square_root(g):
            sc.wait_ge(var_ok, g + 1)
            nc.scalar.activation(rstd[:, 4 * g:4 * g + 4, 1], rstd[:, 4 * g:4 * g + 4, 0], ACT.Sqrt)\
              .then_inc(sqrt_ok, 1)

        def xt_high(i):
            u = ("xt", i)
            high(u, XH[:, :, 2 * i * P:(2 * i + 2) * P],
                 bank_of(u)[:, :].rearrange("p (c n) -> p c n", c=DC)).then_inc(a_hi, 1)

        def logits_t(g):
            sc.wait_ge(lt_full, g + 1)
            nc.scalar.activation(LT[:, g * GT * P:(g + 1) * GT * P], PB[RT_B[g]][0:E, :], ACT.Copy)\
              .then_inc(lt_ok, 1)

        def logits(g):
            sc.wait_ge(lg_full, g + 1)
            if g == 0:
                sc.wait_ge(wsl2_ok, 1)
                sc.wait_ge(wsl_ok, 1)
            nc.scalar.activation(L[:, 8 * g:8 * g + 8, :],
                                 PB[T_B[g]][:, :].rearrange("p (t e) -> p t e", t=8), ACT.Copy)\
              .then_inc(lg_ok, 1)

        square_root(0)
        sc.wait_ge(wq_in, 32)
        nc.scalar.activation(WSH[:, O_GATE:O_WO], raw[:, O_GATE:O_WO], ACT.Copy).then_inc(wsh_ok, 1)
        square_root(1)
        xt_high(0)
        xt_high(1)
        sc.wait_ge(w_in0, 48)
        nc.scalar.activation(WSH[:, O_WO:O_SD], raw[:, O_WO:O_SD], ACT.Copy)
        nc.scalar.activation(WSH[0:SH, O_SD:NST], raw[0:SH, O_SD:NST], ACT.Copy).then_inc(wsh_ok, 1)
        square_root(2)
        xt_high(2)
        xt_high(3)
        square_root(3)
        logits_t(0)
        xt_high(4)
        xt_high(5)
        logits_t(1)
        xt_high(6)
        xt_high(7)
        logits(0)
        logits_t(2)
        logits_t(3)

        def stage(which, b):
            u = (which, b)
            s = 0 if which == "q" else 2
            if b >= 1:
                sc.wait_ge(qk_w, 64 * b)
            sc.wait_ge(a_full, USE[u] + 1)
            for k in range(2):
                last = nc.scalar.activation(stg[s][:, k, :], bank_of(u)[:, k * SEQ:(k + 1) * SEQ],
                                            ACT.Identity, bias=bq[:, s + k:s + k + 1])
            last.then_inc(a_hi, 1)

        sc.wait_ge(b_in, 48)
        stage("q", 0)
        logits(1)
        stage("k", 0)
        sc.wait_ge(dlt_ok, 1)
        nc.scalar.activation(run[:, :, :], run[:, :, :], ACT.Exp)
        nc.scalar.activation(XE[:, :, C_W:C_W + K], XE[:, :, C_W:C_W + K], ACT.Exp).then_inc(ex_ok, 1)

        def shared_act(t):
            sc.wait_ge(sgu_full, 2 * t + 1)
            if t >= 2:
                sc.wait_ge(sact_ok, t - 1)
            nc.scalar.activation(sgS[:, t % 2, :], PB[(T_B, OT_B)[t % 2][0]][:, 0:FS], ACT.Silu)\
              .then_inc(ssilu_ok, 1)

        def shared_actT(t):
            u = ("sT", t)
            if t >= 2:
                sc.wait_ge(a_full, USE[("sY", t - 2)] + 1)
            high(u, aSTH[:, t % 2, :], bank_of(u)[0:SH, 0:SC * P]).then_inc(sat_hi, 1)

        shared_act(0)
        for t in range(TILES):
            if t + 1 < TILES:
                shared_act(t + 1)
            shared_actT(t)
            if t in BESIDE and BESIDE[t][0] in "qk":
                stage(*BESIDE[t])

        def prob(n):
            sc.wait_ge(st_full, n + 1)
            g = n // 4
            if n == 0:
                sc.wait_ge(a_full, USE[("sY", TILES - 1)] + 1)
            if n % 4 == 0 and g >= 2:
                sc.wait_ge(pv_ok, g - 1)
            nc.scalar.activation(EX[g % 2][:, n % 4, :], PB[T_B[n % 2]][:, :], ACT.Exp, scale=SCALE)\
              .then_inc(exp_ok, 1)

        def take_out(g):
            sc.wait_ge(pv_ok, g + 1)
            if g >= 2:
                sc.wait_ge(a_full, USE[("nt", g - 2)] + 1)
            if g == 0:
                sc.wait_ge(fill_in, 16 * E)
                sc.wait_ge(route_ok, 1)
            nc.scalar.activation(OTs[:, g % 2, :], PB[OT_B[0]][:, 0:SEQ], ACT.Copy)\
              .then_inc(ot_ok, 1)

        def wait(s, v):
            if not (isinstance(v, int) and v <= 0):
                sc.wait_ge(s, v)

        def gate_high(i, c):
            wait(w_in[c % 4], 32 * (BODY // 4 * i + c // 4) + 32)
            wait(gu_full, 2 * BODY * i + 2 * (c - 2) + 2)
            o = (c % 4) * WN
            nc.scalar.activation(GH[c % 2][:, :], raw[:, o:o + GO], ACT.Copy).then_inc(guH_ok, 1)

        def silu(i, c, j):
            wait(gu_full, 2 * BODY * i + 2 * c + j + 1)
            nc.scalar.activation(sg[:, c % 2, j, :], PB[2 * (c % 2) + j][:, 0:F], ACT.Silu)\
              .then_inc(silu_ok, 1)

        def act_high(i, c):
            wait(at_full, BODY * i + c + 1)
            wait(dn_full, BODY * i + c - 1)
            nc.scalar.activation(aTH[c % 2][:, :, :],
                                 PB[A_B[1]][0:FH, :].rearrange("p (k n) -> p k n", k=2), ACT.Copy)\
              .then_inc(atH_ok, 1)

        def rows_high(i, c):
            wait(xt_full, BODY * i + c + 1)
            wait(gu_full, 2 * BODY * i + 2 * (c - 2) + 2)
            nc.scalar.activation(xTH[c % 2][:, :, :],
                                 x_bank(i, c)[:, :].rearrange("p (k n) -> p k n", k=DC), ACT.Copy)\
              .then_inc(xtH_ok, 1)

        def down_high(i, c):
            wait(w_in[c % 4], 32 * (BODY // 4 * i + c // 4) + 32)
            wait(dn_full, BODY * i + c - 1)
            o = (c % 4) * WN
            nc.scalar.activation(DH[c % 2][:, :], raw[0:FH, o + GO:o + WN], ACT.Copy).then_inc(dh_ok, 1)

        def weighted(i, c):
            for j in range(2):
                if j == 0:
                    wait(dn_full, BODY * i + c + 1)
                    wait(wcol_ok, BODY * i + c + 1)
                    wait(y_free, BODY * i + c - 2)
                nc.scalar.activation(y[:, c % 4, j, :], PB[OT_B[c % 2]][:, j * D:(j + 1) * D],
                                     ACT.Copy, scale=wcol[:, c % 4, j:j + 1]).then_inc(y_ok, 1)

        def step(i, c, first=False, last=False, tail=False):
            if not first:
                act_high(i, c - 1)
            silu(i, c, 0)
            if not last:
                rows_high(i, c + 1)
            silu(i, c, 1)
            if not tail or c < BODY - 2:
                gate_high(i, c + 2)
            down_high(i, c)
            if not first:
                weighted(i, c - 1)

        for n in range(SLOT_END):
            if n < HEADS:
                prob(n)
            if n % 4 == 1 and 5 <= n < HEADS + 5:
                take_out(n // 4 - 1)
            if n == G0_SLOT:
                sc.wait_ge(a_full, USE[("v", B - 1)] + 1)
                gate_high(0, 0)
            elif n == G0_SLOT + 4:
                gate_high(0, 1)
            elif n == X0_SLOT + 1:
                rows_high(0, 0)
            elif n == UP0_SLOT + 1:
                silu(0, 0, 0)
            elif n == UP0_SLOT + 2:
                rows_high(0, 1)
            elif n == UP0_SLOT + 3:
                silu(0, 0, 1)
            elif n == UP0_SLOT + 4:
                silu(0, 1, 0)
            elif n == UP0_SLOT + 6:
                silu(0, 1, 1)
                gate_high(0, 2)
                down_high(0, 0)
            for u in slot_uses(n - 1):
                if u[0] in "qk":
                    stage(*u)
                elif u[0] == "onT":
                    if u[1] == 0:
                        sc.wait_ge(fill_free, 1)
                    else:
                        sc.wait_ge(a_full, USE[("o", u[1] - 1)] + 1)
                    high(u, OnTH[:, :, :], bank_of(u)[:, :].rearrange("p (c n) -> p c n", c=DC))\
                        .then_inc(a_hi, 1)

        act_high(0, 0)
        rows_high(0, 2)
        gate_high(0, 3)
        down_high(0, 1)
        weighted(0, 0)
        for c in range(2, BODY):
            step(0, c)
        with sc.Fori(1, E // BODY - 1, 1) as i:
            for c in range(BODY):
                step(i, c)
        for c in range(BODY):
            step(E // BODY - 1, c, last=c == BODY - 1, tail=True)
        act_high(E // BODY - 1, BODY - 1)
        weighted(E // BODY - 1, BODY - 1)

        over = sc.value_load(nov_i[0:1, 0:1], min_val=0, max_val=OVT)
        with sc.If(over > 0):
            with sc.Fori(0, OVT, 1) as j:
                with sc.If(over > j):
                    sc.wait_ge(ov_gu, j + 1)
                    nc.scalar.activation(ov_a[:, 0, :], PB[1][:, 0:F], ACT.Silu).then_inc(ov_silu, 1)
            sc.wait_ge(ov_w, OVT + 1)

    @block.vector
    def _(ve):
        n_ = [0]

        def link(ins):
            n_[0] += 1
            ins.then_inc(chain, 1)
            ve.wait_ge(chain, n_[0])

        def low(dst, src, hi):
            return nc.vector.tensor_tensor(dst, src, raw32(hi), ALU.subtract)

        def stats(g):
            ve.wait_ge(x_in[g], 16)
            for t in range(4 * g, 4 * g + 4):
                last = nc.vector.bn_stats(st6[:, t, :], base[:, t, :])
            link(last)
            for t in range(4 * g, 4 * g + 4):
                last = nc.vector.bn_aggr(mv[:, t, :], st6[:, t, :])
            link(last)
            nc.vector.tensor_scalar_add(rstd[:, 4 * g:4 * g + 4, 0], mv[:, 4 * g:4 * g + 4, 1], LN_EPS)\
              .then_inc(var_ok, 1)

        def normalise(g):
            ve.wait_ge(sqrt_ok, g + 1)
            link(nc.vector.reciprocal(rstd[:, 4 * g:4 * g + 4, 2], rstd[:, 4 * g:4 * g + 4, 1]))
            for t in range(4 * g, 4 * g + 4):
                nc.vector.tensor_scalar(XE[:, t, 0:D], base[:, t, :], mv[:, t, 0:1], rstd[:, t, 2:3],
                                        ALU.subtract, ALU.mult).then_inc(xn_ok, 1)

        def low_of_a(u, dst, src, hi, hi_sem, hi_val):
            ve.wait_ge(hi_sem, hi_val)
            return low(dst, src, hi).then_inc(a_free, 1)

        hi_n = [0]

        def xt_low(i):
            u = ("xt", i)
            hi_n[0] += 1
            s = slice(2 * i * P, (2 * i + 2) * P)
            low_of_a(u, XL[:, :, s], bank_of(u)[:, :].rearrange("p (c n) -> p c n", c=DC), XH[:, :, s],
                     a_hi, hi_n[0])

        def stage_low(which, b):
            u = (which, b)
            s = 0 if which == "q" else 2
            hi_n[0] += 1
            ve.wait_ge(a_hi, hi_n[0])
            for k in range(2):
                last = nc.vector.scalar_tensor_tensor(out=stg[s + 1][:, k, :],
                                                      in0=bank_of(u)[:, k * SEQ:(k + 1) * SEQ],
                                                      scalar=bq[:, s + k:s + k + 1],
                                                      in1=raw32(stg[s][:, k, :]), op0=ALU.add,
                                                      op1=ALU.subtract)
            last.then_inc(stg_q if which == "q" else stg_k, 1)
            ve.wait_ge(stg_q if which == "q" else stg_k, b + 1)
            ve.sem_inc(a_free, 1)

        def values(b):
            u = ("v", b)
            ve.wait_ge(a_full, USE[u] + 1)
            if b == 0:
                ve.wait_ge(const_ok, CONSTS)
            if b >= 2:
                ve.wait_ge(pv_ok, H // 4 * (b - 1))
            nc.vector.tensor_tensor(V[:, b % 2, :, :, 0:HD],
                                    bank_of(u)[:, :].rearrange("p (t h d) -> p t h d", t=2, h=H),
                                    bv[:, :].rearrange("p (a h d) -> p a h d", a=1, h=H)
                                    .broadcast_to([P, 2, H, HD]), ALU.add).then_inc(v_ok, 1)
            ve.wait_ge(v_ok, b + 1)
            ve.sem_inc(a_free, 1)

        stats(0)
        normalise(0)
        stats(1)
        ve.wait_ge(wsh_ok, 1)
        low(WSL[:, O_GATE:O_WO], raw[:, O_GATE:O_WO], WSH[:, O_GATE:O_WO]).then_inc(wsl_ok, 1)
        normalise(1)
        stats(2)
        xt_low(0)
        xt_low(1)
        normalise(2)
        stats(3)
        xt_low(2)
        xt_low(3)
        normalise(3)
        xt_low(4)
        xt_low(5)
        xt_low(6)
        xt_low(7)

        w6 = XE[:, :, C_W:C_W + K]

        def largest(g):
            ve.wait_ge(lg_ok, g + 1)
            for t in range(8 * g, 8 * g + 8):
                last = nc.vector.max(top8[:, t, :], L[:, t, :])
            link(last)
            for t in range(8 * g, 8 * g + 8):
                last = nc.vector.max_index(idx8[:, t, :], top8[:, t, :], L[:, t, :])
            link(last)

        def differences():
            nc.vector.tensor_tensor(run[:, :, :], L[:, :, :], top8[:, :, 0:1].broadcast_to([P, TILES, E]),
                                    ALU.subtract)
            nc.vector.tensor_tensor(w6, top8[:, :, 0:K], top8[:, :, 0:1].broadcast_to([P, TILES, K]),
                                    ALU.subtract).then_inc(dlt_ok, 1)

        def one_hot(g):
            link(nc.vector.tensor_tensor(
                oh[:, 4 * g * K:4 * (g + 1) * K, :].rearrange("p (t k) e -> p t k e", k=K),
                iota_e[:, :].rearrange("p (a b e) -> p a b e", a=1, b=1).broadcast_to([P, 4, K, E]),
                XE[:, 4 * g:4 * g + 4, C_IDX:C_IDX + K].rearrange("p t (k a) -> p t k a", a=1)
                .broadcast_to([P, 4, K, E]), ALU.is_equal))

        def mask_sum():
            ve.wait_ge(mask_ok, 2)
            with nc.allow_low_precision("counts up to 16 are exact"):
                nc.vector.tensor_reduce(masksum[:, :], mask[:, :, :].rearrange("p t e -> p e t"), AX.X,
                                        ALU.add).then_inc(sum_ok, 1)

        def softmax():
            ve.wait_ge(ex_ok, 1)
            link(nc.vector.tensor_reduce(top8[:, :, 0], run[:, :, :], AX.X, ALU.add))
            link(nc.vector.reciprocal(top8[:, :, 1], top8[:, :, 0]))
            link(nc.vector.tensor_tensor(w6, w6, top8[:, :, 1:2].broadcast_to([P, TILES, K]), ALU.mult))
            link(nc.vector.tensor_reduce(top8[:, :, 2], w6, AX.X, ALU.add))
            link(nc.vector.tensor_scalar_add(top8[:, :, 3], top8[:, :, 2], TOPK_EPS))
            link(nc.vector.reciprocal(top8[:, :, 4], top8[:, :, 3]))
            link(nc.vector.tensor_tensor(w6, w6, top8[:, :, 4:5].broadcast_to([P, TILES, K]), ALU.mult))

        tiles_i = L[:, 0, :].bitcast(i32)

        def ranks():
            u = ("rk", 0)
            ve.wait_ge(a_full, USE[u] + 1)
            nc.vector.tensor_copy(run[:, 0, :], bank_of(u)[:, 0:E])
            link(nc.vector.tensor_scalar(tiles_i, bank_of(u)[:, E:2 * E], float(SLOTS - P + 1), 0.0,
                                         ALU.subtract, ALU.max))
            ve.sem_inc(rank_read, 1)
            ve.sem_inc(a_free, 1)

        OVC = (E - 1).bit_length() % 2

        def overflow():
            link(nc.vector.tensor_scalar(tiles_i, tiles_i, 7, None, ALU.logical_shift_right))
            link(nc.vector.tensor_copy(ovc[:, 0, :], tiles_i))
            link(nc.vector.tensor_copy(L[:, 1, :], ovc[:, 0, :]))
            cur, sh = 0, 1
            while sh < E:
                nc.vector.tensor_copy(ovc[:, 1 - cur, 0:sh], ovc[:, cur, 0:sh])
                link(nc.vector.tensor_tensor(ovc[:, 1 - cur, sh:E], ovc[:, cur, sh:E],
                                             ovc[:, cur, 0:E - sh], ALU.add))
                cur, sh = 1 - cur, 2 * sh
            assert cur == OVC
            nc.vector.tensor_copy(nov_i[:, 0:1], ovc[:, OVC, E - 1:E])
            link(nc.vector.tensor_tensor(L[:, 2, :], ovc[:, OVC, :], L[:, 1, :], ALU.subtract))
            link(nc.vector.tensor_scalar(L[:, 3, :], L[:, 2, :], float(P), float(REG - SLOTS), ALU.mult,
                                         ALU.add))
            link(nc.vector.scalar_tensor_tensor(out=L[:, 4, :], in0=iota_e[:, :], scalar=-float(SLOTS),
                                                in1=L[:, 3, :], op0=ALU.mult, op1=ALU.add))

        def correct(g):
            corr = L[:, 5:5 + 8, :]
            ve.wait_ge(tile_ranks_ok, 1)
            if g == 1:
                ve.wait_ge(run_ok, 1)
            r = run[:, 8 * g:8 * g + 8, :]
            link(nc.vector.scalar_tensor_tensor(out=corr, in0=r, scalar=float(SLOTS),
                                                in1=L[:, 4:5, :].broadcast_to([P, 8, E]),
                                                op0=ALU.is_ge, op1=ALU.mult))
            nc.vector.tensor_tensor(r, r, corr, ALU.add).then_inc(run_ok, 1)

        def slots(g):
            ve.wait_ge(prod_ok, g + 1)
            nc.vector.tensor_reduce(L[:, 13, 0:2 * K], prod[:, g % 2, :, :], AX.X, ALU.add)\
              .then_inc(prod_free, 1)
            ve.wait_ge(prod_free, g + 1)
            link(nc.vector.scalar_tensor_tensor(
                out=posi[:, 2 * g * K:2 * (g + 1) * K].rearrange("p (t k) -> p t k", k=K),
                in0=XE[:, 2 * g:2 * g + 2, C_IDX:C_IDX + K], scalar=float(SLOTS),
                in1=L[:, 13, 0:2 * K].rearrange("p (t k) -> p t k", k=K), op0=ALU.mult, op1=ALU.add))
            if g == TILES // 2 - 1:
                ve.sem_inc(route_ok, 1)

        def routing(t):
            if t < 4:
                one_hot(t)
                if t % 2:
                    ve.sem_inc(oh_ok, 1)
            elif t == 4:
                softmax()
            elif t == 6:
                mask_sum()
            elif t == 7:
                overflow()
            elif t in (8, 9):
                correct(t - 8)
            elif 10 <= t < 14:
                slots(2 * (t - 10))
                slots(2 * (t - 10) + 1)

        largest(0)
        stage_low("q", 0)
        largest(1)
        nc.vector.tensor_copy(XE[:, :, C_IDX:C_IDX + K], idx8[:, :, 0:K])
        differences()
        stage_low("k", 0)
        values(0)

        def shared_mul(t):
            ve.wait_ge(ssilu_ok, t + 1)
            ve.wait_ge(sgu_full, 2 * t + 2)
            if t >= 2:
                ve.wait_ge(a_full, USE[("sT", t - 2)] + 1)
            nc.vector.tensor_tensor(aS[:, t % 2, 0:FS], sgS[:, t % 2, :], PB[(T_B, OT_B)[t % 2][1]][:, 0:FS],
                                    ALU.mult).then_inc(sact_ok, 1)

        def shared_low(t):
            u = ("sT", t)
            ve.wait_ge(sat_hi, t + 1)
            low(aSTL[:, t % 2, :], bank_of(u)[0:SH, 0:SC * P], aSTH[:, t % 2, :]).then_inc(sat_ok, 1)
            ve.wait_ge(sat_ok, t + 1)
            ve.sem_inc(a_free, 1)

        def shared_add(t):
            u = ("sY", t)
            ve.wait_ge(a_full, USE[u] + 1)
            ve.wait_ge(xbo_ok, t + 1)
            nc.vector.tensor_tensor(base[:, t, :], bank_of(u)[:, 0:D], base[:, t, :], ALU.add)\
              .then_inc(a_free, 1)

        def maximum(n):
            b, h = divmod(n, H)
            ve.wait_ge(s_full, n + 1)
            if h == 0 and b >= 2:
                ve.wait_ge(m_ok, b - 1)
            nc.vector.tensor_reduce(mx[:, b % 2, :, h], s_bank(n)[:, :]
                                    .rearrange("p (j n) -> p j n", j=2), AX.X, ALU.max, negate=True)\
              .then_inc(max_ok, 1)

        def neg_max(b):
            u = ("mT", b)
            ve.wait_ge(a_full, USE[u] + 1)
            if b >= 1:
                ve.wait_ge(m_w, 16 * b)
            nc.vector.tensor_copy(mTs[:, :], bank_of(u)[0:H, 0:SEQ]).then_inc(m_ok, 1)
            ve.wait_ge(m_ok, b + 1)
            ve.sem_inc(a_free, 1)

        shared_mul(0)
        for t in range(TILES):
            now = lead_heads(t)
            for n in now[0:1]:
                maximum(n)
            if t + 1 < TILES:
                shared_mul(t + 1)
            for n in now[1:2]:
                maximum(n)
            shared_low(t)
            if t in BESIDE:
                kind, b = BESIDE[t]
                if kind == "mT":
                    neg_max(b)
                elif kind == "rk":
                    ranks()
                else:
                    stage_low(kind, b)
            if t:
                shared_add(t - 1)
            routing(t)
        shared_add(TILES - 1)

        def norm(g):
            b = g // 4
            ve.wait_ge(a_full, USE[("nt", g)] + 1)
            src = bank_of(("nt", g))[:, 0:SEQ].rearrange("p (j h d) -> p j h d", j=2, h=4)
            link(nc.vector.reciprocal(rden[:, g % 2, :, :], src[:, :, :, HD]))
            if g % 4 == 0 and b >= 2:
                ve.wait_ge(a_full, USE[("onT", b - 2)] + 1)
            nc.vector.tensor_tensor(
                On[:, b % 2, :, (g % 4) * 64:(g % 4 + 1) * 64].rearrange("p j (h d) -> p j h d", h=4),
                src[:, :, :, 0:HD],
                rden[:, g % 2, :, :].rearrange("p j (h a) -> p j h a", a=1).broadcast_to([P, 2, 4, HD]),
                ALU.mult).then_inc(norm_ok, 1)
            ve.wait_ge(norm_ok, g + 1)
            ve.sem_inc(a_free, 1)

        def wait(s, v):
            if not (isinstance(v, int) and v <= 0):
                ve.wait_ge(s, v)

        def gate_low(i, c):
            wait(guH_ok, BODY * i + c + 1)
            o = (c % 4) * WN
            low(GL[c % 2][:, :], raw[:, o:o + GO], GH[c % 2][:, :]).then_inc(gu_split, 1)

        def mul(i, c, j):
            wait(silu_ok, 2 * BODY * i + 2 * c + j + 1)
            wait(at_full, BODY * i + c - 1)
            nc.vector.tensor_tensor(act[:, c % 2, j, :], sg[:, c % 2, j, :],
                                    PB[2 * (c % 2) + j][:, F:2 * F], ALU.mult).then_inc(mul_ok, 1)

        def act_low(i, c):
            wait(atH_ok, BODY * i + c + 1)
            low(aTL[c % 2][:, :, :], PB[A_B[1]][0:FH, :].rearrange("p (k n) -> p k n", k=2),
                aTH[c % 2][:, :, :]).then_inc(at_ok, 1)

        def rows_low(i, c):
            wait(xtH_ok, BODY * i + c + 1)
            low(xTL[c % 2][:, :, :], x_bank(i, c)[:, :].rearrange("p (k n) -> p k n", k=DC),
                xTH[c % 2][:, :, :]).then_inc(xt_ok, 1)

        def down_low(i, c):
            wait(dh_ok, BODY * i + c + 1)
            o = (c % 4) * WN
            low(DL[c % 2][:, :], raw[0:FH, o + GO:o + WN], DH[c % 2][:, :]).then_inc(wd_split, 1)

        def weights_of(i, c):
            s = c % 4
            wait(r_in[s], 16 * (BODY // 4 * i + c // 4) + 16)
            wait(y_free, BODY * i + c - 2)
            nc.vector.tensor_copy(ids[:, s, :], xin[:, s, :, C_TOK].bitcast(i32))
            nc.vector.tensor_scalar_add(ecur[:, s:s + 1], ecur[:, s:s + 1], 4.0).then_inc(w_step, 1)
            wait(w_step, 2 * BODY * i + 2 * c + 1)
            nc.vector.scalar_tensor_tensor(out=wtmp[:, :, :], in0=xin[:, s, :, C_IDX:C_IDX + K],
                                           scalar=ecur[:, s:s + 1], in1=xin[:, s, :, C_W:C_W + K],
                                           op0=ALU.is_equal, op1=ALU.mult).then_inc(w_step, 1)
            wait(w_step, 2 * BODY * i + 2 * c + 2)
            nc.vector.tensor_reduce(wcol[:, s, :], wtmp[:, :, :], AX.X, ALU.add).then_inc(wcol_ok, 1)

        def step(i, c, first=False, last=False, tail=False):
            if not first:
                act_low(i, c - 1)
            mul(i, c, 0)
            if not last:
                rows_low(i, c + 1)
            mul(i, c, 1)
            if not tail or c < BODY - 2:
                gate_low(i, c + 2)
            down_low(i, c)
            if not last:
                weights_of(i, c + 1)

        for n in range(SLOT_END):
            if n + LEAD < HEADS:
                maximum(n + LEAD)
            if n == G0_SLOT + 1:
                gate_low(0, 0)
            elif n == G0_SLOT + 5:
                gate_low(0, 1)
            elif n == X0_SLOT + 1:
                rows_low(0, 0)
                weights_of(0, 0)
            elif n == UP0_SLOT + 1:
                mul(0, 0, 0)
            elif n == UP0_SLOT + 3:
                mul(0, 0, 1)
            elif n == UP0_SLOT + 4:
                mul(0, 1, 0)
            elif n == UP0_SLOT + 6:
                mul(0, 1, 1)
            for u in slot_uses(n - 1):
                kind, b = u
                if kind == "nt":
                    norm(b)
                elif kind in "qk":
                    stage_low(kind, b)
                elif kind == "v":
                    values(b)
                elif kind == "mT":
                    neg_max(b)
                elif kind == "onT":
                    hi_n[0] += 1
                    ve.wait_ge(a_hi, hi_n[0])
                    low(OnTL[:, :, :], bank_of(u)[:, :].rearrange("p (c n) -> p c n", c=DC), OnTH[:, :, :])\
                        .then_inc(ont_ok, 1)
                    ve.wait_ge(ont_ok, b + 1)
                    ve.sem_inc(a_free, 1)
                elif kind == "o":
                    ve.wait_ge(a_full, USE[u] + 1)
                    bs = base[:, 2 * b:2 * b + 2, :]
                    nc.vector.tensor_tensor(bs, bank_of(u)[:, :].rearrange("p (j n) -> p j n", j=2), bs,
                                            ALU.add).then_inc(base_ok, 1)
                    ve.wait_ge(base_ok, b + 1)
                    ve.sem_inc(a_free, 1)
            if n == UP0_SLOT + 2:
                rows_low(0, 1)

        gate_low(0, 2)
        down_low(0, 0)
        weights_of(0, 1)
        act_low(0, 0)
        rows_low(0, 2)
        gate_low(0, 3)
        down_low(0, 1)
        weights_of(0, 2)
        for c in range(2, BODY):
            step(0, c)
        with ve.Fori(1, E // BODY - 1, 1) as i:
            for c in range(BODY):
                step(i, c)
        for c in range(BODY):
            step(E // BODY - 1, c, last=c == BODY - 1, tail=True)
        act_low(E // BODY - 1, BODY - 1)

        over = ve.value_load(nov_i[0:1, 0:1], min_val=0, max_val=OVT)
        with ve.If(over > 0):
            ve.wait_ge(y_free, E + 1)
            link(nc.vector.memset(ov_cmp[:, 0, 0:1], 0.0))
            for j in range(OVT):
                last = nc.vector.tensor_scalar(ov_cmp[:, j, :], ovc[:, OVC, :], float(j), None, ALU.is_le)
            link(last)
            link(nc.vector.tensor_reduce(ov_e[:, :], ov_cmp[:, :, :], AX.X, ALU.add))
            link(nc.vector.tensor_scalar_min(ov_e[:, :], ov_e[:, :], float(E - 1)))
            nc.vector.tensor_copy(ov_ei[:, :], ov_e[:, :]).then_inc(ov_e_ok, 1)
            ve.wait_ge(ov_e_ok, 1)
            with ve.Fori(0, OVT, 1) as j:
                with ve.If(over > j):
                    ve.wait_ge(ov_xT_full, j + 1)
                    nc.vector.tensor_copy(ov_xT[:, :, :], PB[0][:, 0:DC * P].rearrange("p (k n) -> p k n", k=DC))\
                      .then_inc(ov_xT_ok, 1)
                    nc.vector.tensor_copy(ov_c[:, 0:1], ov_e[:, bass.ds(j, 1)]).then_inc(ov_s, 1)
                    ve.wait_ge(ov_s, 3 * j + 1)
                    nc.vector.scalar_tensor_tensor(out=wtmp[:, 0, :], in0=ov_x[:, C_IDX:C_IDX + K],
                                                   scalar=ov_c[:, 0:1], in1=ov_x[:, C_W:C_W + K],
                                                   op0=ALU.is_equal, op1=ALU.mult).then_inc(ov_s, 1)
                    ve.wait_ge(ov_s, 3 * j + 2)
                    nc.vector.tensor_reduce(ov_c[:, 1:2], wtmp[:, 0, :], AX.X, ALU.add).then_inc(ov_s, 1)
                    nc.vector.tensor_copy(ov_id[:, 0:1], ov_x[:, C_TOK:C_TOK + 1].bitcast(i32))
                    ve.wait_ge(ov_silu, j + 1)
                    nc.vector.tensor_tensor(ov_a[:, 1, :], ov_a[:, 0, :], PB[1][:, F:2 * F], ALU.mult)\
                      .then_inc(ov_mul, 1)
                    ve.wait_ge(ov_at, j + 1)
                    nc.vector.tensor_copy(ov_aT[:, :, :], PB[2][0:FH, 0:2 * P].rearrange("p (k n) -> p k n", k=2))\
                      .then_inc(ov_at_ok, 1)
                    ve.wait_ge(ov_dn, j + 1)
                    ve.wait_ge(ov_s, 3 * j + 3)
                    nc.vector.tensor_scalar(ov_y[:, :], PB[3][:, 0:D], ov_c[:, 1:2], None, ALU.mult)\
                      .then_inc(ov_y_ok, 1)
            ve.wait_ge(ov_w, OVT + 1)

    block_cm.__exit__(None, None, None)


def kernel(**inputs):
    import numpy as np
    import concourse.bacc as bacc
    from concourse.bass_utils import run_bass_kernel_spmd

    def rows(w, p=128):
        return np.ascontiguousarray(w.reshape(-1, p, w.shape[1]).transpose(1, 0, 2))

    a = {k[3:]: np.asarray(v) for k, v in inputs.items()}
    x = a["attn_x"].reshape(-1, a["attn_x"].shape[-1])
    D = x.shape[1]
    b = a["attn_b_qkv"]
    gu, dn = a["ffn_w_gate_up"], a["ffn_w_down"]
    E, F = gu.shape[0], dn.shape[2]
    ws = a["ffn_ws_down"].T
    chunks = -(-len(ws) // 128)
    ws = np.pad(ws, ((0, -len(ws) % chunks), (0, 0)))
    arrays = {
        "x": np.ascontiguousarray(x),
        "gate": rows(a["ffn_gate_w"].T),
        "wqkv": rows(a["attn_w_qkv"].T),
        "bqk": np.ascontiguousarray(b[:2 * D].reshape(4, 128).T),
        "bvo": np.stack([b[2 * D:], a["attn_b_o"]]),
        "wo": rows(a["attn_w_o"].T),
        "wsgu": rows(a["ffn_ws_gate_up"].T),
        "wsd": rows(ws, len(ws) // chunks),
        "wgu": np.ascontiguousarray(gu.reshape(E, 2 * F, 2, 128).transpose(0, 3, 2, 1)).reshape(E, 128, 4 * F),
        "wd": np.ascontiguousarray(dn.reshape(E, D, 2, F // 2).transpose(0, 3, 2, 1)).reshape(E, F // 2, 2 * D),
    }
    nc = bacc.Bacc("TRN2", target_bir_lowering=False, num_devices=1)
    ts = [nc.dram_tensor(k, v.shape, mybir.dt.from_np(v.dtype), kind="ExternalInput").ap()
          for k, v in arrays.items()]
    out = nc.dram_tensor("out", (x.shape[0] + 256, D), mybir.dt.float32, kind="ExternalOutput").ap()
    block_kernel(nc, *ts, out)
    r = run_bass_kernel_spmd(nc, [arrays], core_ids=[0])
    return r.results[0]["out"][:x.shape[0]].reshape(a["attn_x"].shape)
```
